# Optimizing a Trainium2 kernel written in Bass

```python
import numpy as np
import jax
import jax.numpy as jnp

def _softmax(x, axis=-1):
    return jax.nn.softmax(x, axis=axis)

def _gelu(x):
    return jax.nn.gelu(x, approximate=True)

def _silu(x):
    return jax.nn.silu(x)

def _sigmoid(x):
    return jax.nn.sigmoid(x)

def _layernorm(x, axis=-1, eps=1e-05):
    m = jnp.mean(x, axis=axis, keepdims=True)
    v = jnp.var(x, axis=axis, keepdims=True)
    return (x - m) / jnp.sqrt(v + eps)

def _scatter_add(tgt, idx, src, axis=0):
    return tgt.at[idx].add(src)

def _segment_sum(src, seg, n):
    return jax.ops.segment_sum(src, seg, n)
kernel_name = 'mk_prb_d4_jaxref_r4_7b2543'

def setup_inputs(seed: int=0):
    np.random.seed(seed)
    _w = jnp.asarray

    def _L0_attn_setup():
        import jax, jax.numpy as jnp
        import numpy as np
        DIM = 512
        key = jax.random.key(seed)
        ks = jax.random.split(key, 9)
        scale = 1.0 / np.sqrt(DIM)
        x = jax.random.normal(ks[0], (4, 1024, DIM), dtype=jnp.float32)

        def lin(kw, kb):
            W = jax.random.uniform(kw, (DIM, DIM), jnp.float32, -scale, scale)
            b = jax.random.uniform(kb, (DIM,), jnp.float32, -scale, scale)
            return (W, b)
        Wq, bq = lin(ks[1], ks[2])
        Wk, bk = lin(ks[3], ks[4])
        Wv, bv = lin(ks[5], ks[6])
        Wg, bg = lin(ks[7], ks[8])
        return {'x': x, 'Wq': Wq, 'bq': bq, 'Wk': Wk, 'bk': bk, 'Wv': Wv, 'bv': bv, 'Wg': Wg, 'bg': bg}
    _L0_attn_in = _L0_attn_setup()

    def _L0_ffn_setup():
        import jax, jax.numpy as jnp
        import numpy as np
        HIDDEN = 512
        INTER = 1376
        LUT_SIZE = 16

        def _ghost_linear(x, idx, lut):
            w = lut[idx]
            return jnp.einsum('bsh,oh->bso', x, w)
        key = jax.random.key(seed)
        k_x, k_lut, k_g, k_u, k_d = jax.random.split(key, 5)
        x = jax.random.normal(k_x, (2, 1024, HIDDEN), dtype=jnp.float32)
        lut = jax.random.normal(k_lut, (LUT_SIZE,), dtype=jnp.float32) * 0.02
        gate_idx = jax.random.randint(k_g, (INTER, HIDDEN), 0, LUT_SIZE, dtype=jnp.int32)
        up_idx = jax.random.randint(k_u, (INTER, HIDDEN), 0, LUT_SIZE, dtype=jnp.int32)
        down_idx = jax.random.randint(k_d, (HIDDEN, INTER), 0, LUT_SIZE, dtype=jnp.int32)
        return {'x': x, 'lut': lut, 'gate_idx': gate_idx, 'up_idx': up_idx, 'down_idx': down_idx}
    _L0_ffn_in = _L0_ffn_setup()

    def _L1_attn_setup():
        import jax, jax.numpy as jnp
        import numpy as np
        EMBED = 512
        D_COMPR = 128
        D_ROPE = 128
        N_HEADS = 8
        HEAD_DIM = D_COMPR // N_HEADS
        B, S = (4, 512)

        def _lin(x, w, b):
            return jnp.einsum('bsi,oi->bso', x, w) + b

        def _rope_emb(seq_len):
            inv_freq = 1.0 / 10000.0 ** (jnp.arange(0, D_ROPE, 2, dtype=jnp.float32) / D_ROPE)
            t = jnp.arange(seq_len, dtype=jnp.float32)
            freqs = jnp.einsum('i,j->ij', t, inv_freq)
            return jnp.concatenate([freqs, freqs], axis=-1)

        def _apply_rope(x, emb):
            cos, sin = (jnp.cos(emb), jnp.sin(emb))
            x1, x2 = jnp.split(x, 2, axis=-1)
            rot = jnp.concatenate([-x2, x1], axis=-1)
            return x * cos + rot * sin
        key = jax.random.key(seed)
        ks = jax.random.split(key, 20)
        sc = 0.02
        inp = {'x': jax.random.normal(ks[0], (B, S, EMBED), dtype=jnp.float32)}

        def w(k, o, i):
            return jax.random.normal(k, (o, i), dtype=jnp.float32) * sc
        inp['CQ_w'] = w(ks[1], D_COMPR, EMBED)
        inp['CQ_b'] = jnp.zeros((D_COMPR,), jnp.float32)
        inp['CQC_w'] = w(ks[2], D_COMPR - D_ROPE, D_COMPR)
        inp['CQC_b'] = jnp.zeros((D_COMPR - D_ROPE,), jnp.float32)
        inp['CQR_w'] = w(ks[3], D_ROPE, EMBED)
        inp['CQR_b'] = jnp.zeros((D_ROPE,), jnp.float32)
        inp['CKV_w'] = w(ks[4], D_COMPR, EMBED)
        inp['CKV_b'] = jnp.zeros((D_COMPR,), jnp.float32)
        inp['CKR_w'] = w(ks[5], D_ROPE, EMBED)
        inp['CKR_b'] = jnp.zeros((D_ROPE,), jnp.float32)
        inp['CKC_w'] = w(ks[6], D_COMPR - D_ROPE, D_COMPR)
        inp['CKC_b'] = jnp.zeros((D_COMPR - D_ROPE,), jnp.float32)
        inp['CV_w'] = w(ks[7], D_COMPR, D_COMPR)
        inp['CV_b'] = jnp.zeros((D_COMPR,), jnp.float32)
        inp['OUT_w'] = w(ks[8], EMBED, D_COMPR)
        inp['OUT_b'] = jnp.zeros((EMBED,), jnp.float32)
        return inp
    _L1_attn_in = _L1_attn_setup()

    def _L1_ffn_setup():
        import jax, jax.numpy as jnp
        import numpy as np
        DIM = 512
        HID = 1408
        ZERO_POINT = 128.0

        def _qlinear(x, wq, scale):
            W = (wq.astype(jnp.float32) - ZERO_POINT) * scale[:, None]
            return jnp.einsum('bsd,hd->bsh', x, W)
        key = jax.random.key(seed)
        ks = jax.random.split(key, 7)
        B, S = (4, 512)
        sg = jax.random.uniform(ks[1], (HID,)) * (0.02 / np.sqrt(DIM)) + 0.0001
        su = jax.random.uniform(ks[3], (HID,)) * (0.02 / np.sqrt(DIM)) + 0.0001
        sd = jax.random.uniform(ks[5], (DIM,)) * (0.02 / np.sqrt(HID)) + 0.0001
        return {'x': jax.random.normal(ks[0], (B, S, DIM), dtype=jnp.float32), 'wq_gate': jax.random.randint(ks[2], (HID, DIM), 0, 64, dtype=jnp.int32), 's_gate': sg, 'wq_up': jax.random.randint(ks[4], (HID, DIM), 0, 64, dtype=jnp.int32), 's_up': su, 'wq_down': jax.random.randint(ks[6], (DIM, HID), 0, 64, dtype=jnp.int32), 's_down': sd}
    _L1_ffn_in = _L1_ffn_setup()

    def _L2_attn_setup():
        import jax, jax.numpy as jnp
        import numpy as np
        L, N, E, H = (512, 2, 512, 16)
        DH = E // H
        SCALE = DH ** (-0.5)
        key = jax.random.key(seed)
        k1, k2, k3 = jax.random.split(key, 3)
        x = jax.random.normal(k1, (L, N, E), dtype=jnp.float32)
        weight_qkv = jax.random.normal(k2, (3 * E, E), dtype=jnp.float32) * 0.02
        weight_out = jax.random.normal(k3, (E, E), dtype=jnp.float32) * 0.02
        return {'x': x, 'weight_qkv': weight_qkv, 'weight_out': weight_out}
    _L2_attn_in = _L2_attn_setup()

    def _L2_ffn_setup():
        import jax, jax.numpy as jnp
        import numpy as np
        B, T, D = (2, 256, 512)
        E, K, H = (64, 4, 128)
        S, HS = (2, H * K)
        CAP = 128
        key = jax.random.key(seed)
        ks = jax.random.split(key, 9)
        scale = 0.02
        return {'x': jax.random.normal(ks[0], (B, T, D), jnp.float32), 'Wr': jax.random.normal(ks[1], (D, E), jnp.float32) * scale, 'router_bias': jnp.zeros((E,), jnp.float32), 'Wg': jax.random.normal(ks[2], (E, D, H), jnp.float32) * scale, 'Wu': jax.random.normal(ks[3], (E, D, H), jnp.float32) * scale, 'Wd': jax.random.normal(ks[4], (E, H, D), jnp.float32) * scale, 'Sg': jax.random.normal(ks[5], (S, D, HS), jnp.float32) * scale, 'Su': jax.random.normal(ks[6], (S, D, HS), jnp.float32) * scale, 'Sd': jax.random.normal(ks[7], (S, HS, D), jnp.float32) * scale}
    _L2_ffn_in = _L2_ffn_setup()

    def _L3_attn_setup():
        import jax, jax.numpy as jnp
        import numpy as np
        HEAD_NUM = 16
        ROPE_BASE = 10000.0

        def _rotate_half(x):
            x_even = x[..., ::2]
            x_odd = x[..., 1::2]
            return jnp.stack((-x_odd, x_even), axis=-1).reshape(x.shape)

        def _rope_cos_sin(seq_len, head_dim):
            half = head_dim // 2
            inv_freq = 1.0 / ROPE_BASE ** (jnp.arange(half, dtype=jnp.float32) / half)
            t = jnp.arange(seq_len, dtype=jnp.float32)
            freqs = t[:, None] * inv_freq[None, :]
            cos = jnp.repeat(jnp.cos(freqs), 2, axis=-1)
            sin = jnp.repeat(jnp.sin(freqs), 2, axis=-1)
            return (cos, sin)
        key = jax.random.key(seed)
        ks = jax.random.split(key, 9)
        B, S, H = (2, 512, 512)
        std = 1.0 / np.sqrt(H)
        return {'x': jax.random.normal(ks[0], (B, S, H), jnp.float32), 'Wq': jax.random.normal(ks[1], (H, H), jnp.float32) * std, 'bq': jax.random.normal(ks[2], (H,), jnp.float32) * std, 'Wk': jax.random.normal(ks[3], (H, H), jnp.float32) * std, 'bk': jax.random.normal(ks[4], (H,), jnp.float32) * std, 'Wv': jax.random.normal(ks[5], (H, H), jnp.float32) * std, 'bv': jax.random.normal(ks[6], (H,), jnp.float32) * std, 'Wo': jax.random.normal(ks[7], (H, H), jnp.float32) * std, 'bo': jax.random.normal(ks[8], (H,), jnp.float32) * std}
    _L3_attn_in = _L3_attn_setup()

    def _L3_ffn_setup():
        import jax, jax.numpy as jnp
        import numpy as np
        import math
        N_EMBD = 512
        N_HEAD = 16
        HEAD_DIM = N_EMBD // N_HEAD
        B, T = (2, 512)
        key = jax.random.key(seed)
        k1, k2, k3 = jax.random.split(key, 3)
        x = jax.random.normal(k1, (B, T, N_EMBD), dtype=jnp.float32)
        W_gate = jax.random.normal(k2, (N_HEAD, N_EMBD), dtype=jnp.float32) * 0.02
        W_qkv = jax.random.normal(k3, (3 * N_EMBD, N_EMBD), dtype=jnp.float32) * 0.02
        return {'x': x, 'W_gate': W_gate, 'W_qkv': W_qkv}
    _L3_ffn_in = _L3_ffn_setup()
    _d = {'L0_attn_x': _L0_attn_in['x'], 'L0_attn_Wq': _L0_attn_in['Wq'], 'L0_attn_bq': _L0_attn_in['bq'], 'L0_attn_Wk': _L0_attn_in['Wk'], 'L0_attn_bk': _L0_attn_in['bk'], 'L0_attn_Wv': _L0_attn_in['Wv'], 'L0_attn_bv': _L0_attn_in['bv'], 'L0_attn_Wg': _L0_attn_in['Wg'], 'L0_attn_bg': _L0_attn_in['bg'], 'L0_ffn_lut': _L0_ffn_in['lut'], 'L0_ffn_gate_idx': _L0_ffn_in['gate_idx'], 'L0_ffn_up_idx': _L0_ffn_in['up_idx'], 'L0_ffn_down_idx': _L0_ffn_in['down_idx'], 'L1_attn_CQ_w': _L1_attn_in['CQ_w'], 'L1_attn_CQ_b': _L1_attn_in['CQ_b'], 'L1_attn_CQC_w': _L1_attn_in['CQC_w'], 'L1_attn_CQC_b': _L1_attn_in['CQC_b'], 'L1_attn_CQR_w': _L1_attn_in['CQR_w'], 'L1_attn_CQR_b': _L1_attn_in['CQR_b'], 'L1_attn_CKV_w': _L1_attn_in['CKV_w'], 'L1_attn_CKV_b': _L1_attn_in['CKV_b'], 'L1_attn_CKR_w': _L1_attn_in['CKR_w'], 'L1_attn_CKR_b': _L1_attn_in['CKR_b'], 'L1_attn_CKC_w': _L1_attn_in['CKC_w'], 'L1_attn_CKC_b': _L1_attn_in['CKC_b'], 'L1_attn_CV_w': _L1_attn_in['CV_w'], 'L1_attn_CV_b': _L1_attn_in['CV_b'], 'L1_attn_OUT_w': _L1_attn_in['OUT_w'], 'L1_attn_OUT_b': _L1_attn_in['OUT_b'], 'L1_ffn_wq_gate': _L1_ffn_in['wq_gate'], 'L1_ffn_s_gate': _L1_ffn_in['s_gate'], 'L1_ffn_wq_up': _L1_ffn_in['wq_up'], 'L1_ffn_s_up': _L1_ffn_in['s_up'], 'L1_ffn_wq_down': _L1_ffn_in['wq_down'], 'L1_ffn_s_down': _L1_ffn_in['s_down'], 'L2_attn_weight_qkv': _L2_attn_in['weight_qkv'], 'L2_attn_weight_out': _L2_attn_in['weight_out'], 'L2_ffn_Wr': _L2_ffn_in['Wr'], 'L2_ffn_router_bias': _L2_ffn_in['router_bias'], 'L2_ffn_Wg': _L2_ffn_in['Wg'], 'L2_ffn_Wu': _L2_ffn_in['Wu'], 'L2_ffn_Wd': _L2_ffn_in['Wd'], 'L2_ffn_Sg': _L2_ffn_in['Sg'], 'L2_ffn_Su': _L2_ffn_in['Su'], 'L2_ffn_Sd': _L2_ffn_in['Sd'], 'L3_attn_Wq': _L3_attn_in['Wq'], 'L3_attn_bq': _L3_attn_in['bq'], 'L3_attn_Wk': _L3_attn_in['Wk'], 'L3_attn_bk': _L3_attn_in['bk'], 'L3_attn_Wv': _L3_attn_in['Wv'], 'L3_attn_bv': _L3_attn_in['bv'], 'L3_attn_Wo': _L3_attn_in['Wo'], 'L3_attn_bo': _L3_attn_in['bo'], 'L3_ffn_W_gate': _L3_ffn_in['W_gate'], 'L3_ffn_W_qkv': _L3_ffn_in['W_qkv']}
    _x0 = _d['L0_attn_x']
    _d['L0_attn_x'] = jax.random.normal(jax.random.fold_in(jax.random.key(seed), 1), (1, 2048, 512), dtype=_x0.dtype)
    del _x0
    return _d

def reference(L0_attn_x, L0_attn_Wq, L0_attn_bq, L0_attn_Wk, L0_attn_bk, L0_attn_Wv, L0_attn_bv, L0_attn_Wg, L0_attn_bg, L0_ffn_lut, L0_ffn_gate_idx, L0_ffn_up_idx, L0_ffn_down_idx, L1_attn_CQ_w, L1_attn_CQ_b, L1_attn_CQC_w, L1_attn_CQC_b, L1_attn_CQR_w, L1_attn_CQR_b, L1_attn_CKV_w, L1_attn_CKV_b, L1_attn_CKR_w, L1_attn_CKR_b, L1_attn_CKC_w, L1_attn_CKC_b, L1_attn_CV_w, L1_attn_CV_b, L1_attn_OUT_w, L1_attn_OUT_b, L1_ffn_wq_gate, L1_ffn_s_gate, L1_ffn_wq_up, L1_ffn_s_up, L1_ffn_wq_down, L1_ffn_s_down, L2_attn_weight_qkv, L2_attn_weight_out, L2_ffn_Wr, L2_ffn_router_bias, L2_ffn_Wg, L2_ffn_Wu, L2_ffn_Wd, L2_ffn_Sg, L2_ffn_Su, L2_ffn_Sd, L3_attn_Wq, L3_attn_bq, L3_attn_Wk, L3_attn_bk, L3_attn_Wv, L3_attn_bv, L3_attn_Wo, L3_attn_bo, L3_ffn_W_gate, L3_ffn_W_qkv):

    def _L0_attn_ref(x, Wq, bq, Wk, bk, Wv, bv, Wg, bg):
        import jax, jax.numpy as jnp
        import numpy as np
        DIM = 512
        q = jnp.einsum('bsd,ed->bse', x, Wq) + bq
        k = jnp.einsum('bsd,ed->bse', x, Wk) + bk
        v = jnp.einsum('bsd,ed->bse', x, Wv) + bv
        g = jax.nn.sigmoid(jnp.einsum('bsd,ed->bse', x, Wg) + bg)
        kv_state = jnp.cumsum(k * v, axis=1)
        return q * kv_state * g

    def _L0_ffn_ref(x, lut, gate_idx, up_idx, down_idx):
        import jax, jax.numpy as jnp
        import numpy as np
        HIDDEN = 512
        INTER = 1376
        LUT_SIZE = 16

        def _ghost_linear(x, idx, lut):
            w = lut[idx]
            return jnp.einsum('bsh,oh->bso', x, w)
        gate = _ghost_linear(x, gate_idx, lut)
        up = _ghost_linear(x, up_idx, lut)
        h = jax.nn.silu(gate) * up
        return _ghost_linear(h, down_idx, lut)

    def _L1_attn_ref(x, CQ_w, CQ_b, CQC_w, CQC_b, CQR_w, CQR_b, CKV_w, CKV_b, CKR_w, CKR_b, CKC_w, CKC_b, CV_w, CV_b, OUT_w, OUT_b):
        import jax, jax.numpy as jnp
        import numpy as np
        EMBED = 512
        D_COMPR = 128
        D_ROPE = 128
        N_HEADS = 8
        HEAD_DIM = D_COMPR // N_HEADS
        B, S = (4, 512)

        def _lin(x, w, b):
            return jnp.einsum('bsi,oi->bso', x, w) + b

        def _rope_emb(seq_len):
            inv_freq = 1.0 / 10000.0 ** (jnp.arange(0, D_ROPE, 2, dtype=jnp.float32) / D_ROPE)
            t = jnp.arange(seq_len, dtype=jnp.float32)
            freqs = jnp.einsum('i,j->ij', t, inv_freq)
            return jnp.concatenate([freqs, freqs], axis=-1)

        def _apply_rope(x, emb):
            cos, sin = (jnp.cos(emb), jnp.sin(emb))
            x1, x2 = jnp.split(x, 2, axis=-1)
            rot = jnp.concatenate([-x2, x1], axis=-1)
            return x * cos + rot * sin
        b, s, _ = x.shape
        gelu = lambda t: jax.nn.gelu(t, approximate=False)
        cq = gelu(_lin(x, CQ_w, CQ_b))
        cqc = _lin(cq, CQC_w, CQC_b)
        cqr = _lin(x, CQR_w, CQR_b)
        ckv = gelu(_lin(x, CKV_w, CKV_b))
        ckr = _lin(x, CKR_w, CKR_b)
        ckc = _lin(ckv, CKC_w, CKC_b)
        emb = _rope_emb(s)
        cqr = _apply_rope(cqr, emb)
        ckr = _apply_rope(ckr, emb)
        Q = gelu(jnp.concatenate([cqc, cqr], axis=-1))
        K = gelu(jnp.concatenate([ckc, ckr], axis=-1))
        V = _lin(ckv, CV_w, CV_b)
        Q = Q.reshape(b, s, N_HEADS, HEAD_DIM).transpose(0, 2, 1, 3)
        K = K.reshape(b, s, N_HEADS, HEAD_DIM).transpose(0, 2, 1, 3)
        V = V.reshape(b, s, N_HEADS, HEAD_DIM).transpose(0, 2, 1, 3)
        scale = 1.0 / np.sqrt(HEAD_DIM).astype(np.float32)
        scores = jnp.einsum('bhqd,bhkd->bhqk', Q, K) * scale
        causal = jnp.triu(jnp.ones((s, s), dtype=bool), k=1)
        scores = jnp.where(causal[None, None], -jnp.inf, scores)
        attn = jax.nn.softmax(scores, axis=-1)
        out = jnp.einsum('bhqk,bhkd->bhqd', attn, V)
        out = out.transpose(0, 2, 1, 3).reshape(b, s, D_COMPR)
        return _lin(out, OUT_w, OUT_b)

    def _L1_ffn_ref(x, wq_gate, s_gate, wq_up, s_up, wq_down, s_down):
        import jax, jax.numpy as jnp
        import numpy as np
        DIM = 512
        HID = 1408
        ZERO_POINT = 128.0

        def _qlinear(x, wq, scale):
            W = (wq.astype(jnp.float32) - ZERO_POINT) * scale[:, None]
            return jnp.einsum('bsd,hd->bsh', x, W)
        gate = _qlinear(x, wq_gate, s_gate)
        gate = jax.nn.silu(gate)
        up = _qlinear(x, wq_up, s_up)
        return _qlinear(gate * up, wq_down, s_down)

    def _L2_attn_ref(x, weight_qkv, weight_out):
        import jax, jax.numpy as jnp
        import numpy as np
        L, N, E, H = (512, 2, 512, 16)
        DH = E // H
        SCALE = DH ** (-0.5)
        l, n, e = x.shape
        h, dh = (H, DH)
        qkv = jnp.einsum('lne,fe->lnf', x, weight_qkv)
        q, k, v = jnp.split(qkv, 3, axis=-1)
        q = q.reshape(l, n, h, dh) * jnp.asarray(SCALE, x.dtype)
        k = k.reshape(l, n, h, dh)
        v = v.reshape(l, n, h, dh)
        attn = jnp.einsum('lnhd,mnhd->nhlm', q, k)
        causal = jnp.tril(jnp.ones((l, l), dtype=bool))
        attn = jnp.where(causal, attn, jnp.asarray(-jnp.inf, attn.dtype))
        attn = jax.nn.softmax(attn, axis=-1)
        out = jnp.einsum('nhlm,mnhd->lnhd', attn, v).reshape(l, n, e)
        return jnp.einsum('lne,fe->lnf', out, weight_out)

    def _L2_ffn_ref(x, Wr, router_bias, Wg, Wu, Wd, Sg, Su, Sd):
        import jax, jax.numpy as jnp
        import numpy as np
        B, T, D = (2, 256, 512)
        E, K, H = (64, 4, 128)
        S, HS = (2, H * K)
        CAP = 128
        Bx, Tx, Dx = x.shape
        N = Bx * Tx
        flat = x.reshape(N, Dx)
        logits = flat @ Wr + router_bias
        scores = jax.nn.softmax(logits, axis=-1)
        topk_scores, topk_idx = jax.lax.top_k(scores, K)
        topk_scores = topk_scores / topk_scores.sum(-1, keepdims=True)
        eid = topk_idx.reshape(-1)
        w = topk_scores.reshape(-1)
        tok = jnp.repeat(jnp.arange(N), K)
        oh = jax.nn.one_hot(eid, E, dtype=jnp.int32)
        pos = (jnp.cumsum(oh, axis=0) * oh).sum(-1) - 1
        valid = pos < CAP
        xb = jnp.zeros((E, CAP, Dx), x.dtype).at[eid, pos].set(flat[tok], mode='drop')
        h = jax.nn.silu(jnp.einsum('ecd,edh->ech', xb, Wg)) * jnp.einsum('ecd,edh->ech', xb, Wu)
        yb = jnp.einsum('ech,ehd->ecd', h, Wd)
        y = yb[eid, jnp.minimum(pos, CAP - 1)] * (w * valid)[:, None]
        out = jnp.zeros((N, Dx), x.dtype).at[tok].add(y)
        hs = jax.nn.silu(jnp.einsum('nd,sdh->nsh', flat, Sg)) * jnp.einsum('nd,sdh->nsh', flat, Su)
        out = out + jnp.einsum('nsh,shd->nd', hs, Sd)
        return out.reshape(Bx, Tx, Dx)

    def _L3_attn_ref(x, Wq, bq, Wk, bk, Wv, bv, Wo, bo):
        import jax, jax.numpy as jnp
        import numpy as np
        HEAD_NUM = 16
        ROPE_BASE = 10000.0

        def _rotate_half(x):
            x_even = x[..., ::2]
            x_odd = x[..., 1::2]
            return jnp.stack((-x_odd, x_even), axis=-1).reshape(x.shape)

        def _rope_cos_sin(seq_len, head_dim):
            half = head_dim // 2
            inv_freq = 1.0 / ROPE_BASE ** (jnp.arange(half, dtype=jnp.float32) / half)
            t = jnp.arange(seq_len, dtype=jnp.float32)
            freqs = t[:, None] * inv_freq[None, :]
            cos = jnp.repeat(jnp.cos(freqs), 2, axis=-1)
            sin = jnp.repeat(jnp.sin(freqs), 2, axis=-1)
            return (cos, sin)
        B, S, H = x.shape
        nh = HEAD_NUM
        d = H // nh
        scale = jnp.float32(np.sqrt(d))

        def proj(W, b):
            y = x @ W.T + b
            return y.reshape(B, S, nh, d).transpose(0, 2, 1, 3)
        Q = proj(Wq, bq)
        K = proj(Wk, bk)
        V = proj(Wv, bv)
        cos, sin = _rope_cos_sin(S, d)
        Q = Q * cos + _rotate_half(Q) * sin
        K = K * cos + _rotate_half(K) * sin
        scores = jnp.einsum('bhqd,bhkd->bhqk', Q, K) / scale
        causal = jnp.tril(jnp.ones((S, S), dtype=bool))
        scores = jnp.where(causal, scores, jnp.float32(-jnp.inf))
        attn = jax.nn.softmax(scores, axis=-1)
        out = jnp.einsum('bhqk,bhkd->bhqd', attn, V)
        out = out.transpose(0, 2, 1, 3).reshape(B, S, H)
        return out @ Wo.T + bo

    def _L3_ffn_ref(x, W_gate, W_qkv):
        import jax, jax.numpy as jnp
        import numpy as np
        import math
        N_EMBD = 512
        N_HEAD = 16
        HEAD_DIM = N_EMBD // N_HEAD
        B, T = (2, 512)
        Bb, Tt, C = x.shape
        H, hd = (N_HEAD, HEAD_DIM)
        gating = jax.nn.softmax(x @ W_gate.T, axis=-1)
        idx = jnp.argmax(gating, axis=-1)
        indicator = jax.nn.one_hot(idx, H, dtype=gating.dtype)
        top1_val = jnp.max(gating, axis=-1, keepdims=True)
        gating_top1 = indicator * top1_val
        qkv = x @ W_qkv.T
        q, k, v = jnp.split(qkv, 3, axis=-1)
        k = k.reshape(Bb, Tt, H, hd)
        v = v.reshape(Bb, Tt, H, hd)
        k_shared = jnp.einsum('bth,bthd->btd', indicator, k)
        v_shared = jnp.einsum('bth,bthd->btd', gating_top1, v)
        q = q.reshape(Bb, Tt, H, hd).transpose(0, 2, 1, 3)
        att = jnp.einsum('bhqd,bkd->bhqk', q, k_shared) * (1.0 / math.sqrt(hd))
        causal = jnp.tril(jnp.ones((Tt, Tt), dtype=bool))
        att = jnp.where(causal[None, None, :, :], att, -jnp.inf)
        att = jax.nn.softmax(att, axis=-1)
        y = jnp.einsum('bhqk,bkd->bhqd', att, v_shared)
        y = y.transpose(0, 2, 1, 3).reshape(Bb, Tt, C)
        return y
    x = L0_attn_x
    xn = _layernorm(x, axis=-1)
    x = x + _L0_attn_ref(xn, L0_attn_Wq, L0_attn_bq, L0_attn_Wk, L0_attn_bk, L0_attn_Wv, L0_attn_bv, L0_attn_Wg, L0_attn_bg) + _L0_ffn_ref(xn, L0_ffn_lut, L0_ffn_gate_idx, L0_ffn_up_idx, L0_ffn_down_idx)
    xn = _layernorm(x, axis=-1)
    x = x + _L1_attn_ref(xn, L1_attn_CQ_w, L1_attn_CQ_b, L1_attn_CQC_w, L1_attn_CQC_b, L1_attn_CQR_w, L1_attn_CQR_b, L1_attn_CKV_w, L1_attn_CKV_b, L1_attn_CKR_w, L1_attn_CKR_b, L1_attn_CKC_w, L1_attn_CKC_b, L1_attn_CV_w, L1_attn_CV_b, L1_attn_OUT_w, L1_attn_OUT_b) + _L1_ffn_ref(xn, L1_ffn_wq_gate, L1_ffn_s_gate, L1_ffn_wq_up, L1_ffn_s_up, L1_ffn_wq_down, L1_ffn_s_down)
    xn = _layernorm(x, axis=-1)
    x = x + _L2_attn_ref(xn, L2_attn_weight_qkv, L2_attn_weight_out) + _L2_ffn_ref(xn, L2_ffn_Wr, L2_ffn_router_bias, L2_ffn_Wg, L2_ffn_Wu, L2_ffn_Wd, L2_ffn_Sg, L2_ffn_Su, L2_ffn_Sd)
    xn = _layernorm(x, axis=-1)
    x = x + _L3_attn_ref(xn, L3_attn_Wq, L3_attn_bq, L3_attn_Wk, L3_attn_bk, L3_attn_Wv, L3_attn_bv, L3_attn_Wo, L3_attn_bo) + _L3_ffn_ref(xn, L3_ffn_W_gate, L3_ffn_W_qkv)
    return x

_drawn_inputs = setup_inputs


def setup_inputs(seed=0):
    import zlib

    import numpy as np

    out = dict(_drawn_inputs(seed))
    spreads = {'L1_attn_CQ_b': (0.0, 0.1),
     'L1_attn_CQR_b': (0.0, 0.8),
     'L1_attn_CKV_b': (0.0, 0.8),
     'L1_attn_CKR_b': (0.0, 0.8),
     'L1_attn_CV_b': (0.0, 0.8),
     'L1_attn_OUT_b': (0.0, 0.462),
     'L2_ffn_router_bias': (0.0, 0.8)}
    factors = {'L0_attn_bg': 5.603,
     'L0_ffn_lut': 2.879,
     'L1_attn_CQR_w': 8.0,
     'L1_attn_CKV_w': 8.0,
     'L1_attn_CKR_w': 8.0,
     'L1_attn_CV_w': 8.0,
     'L1_attn_OUT_w': 8.0,
     'L1_ffn_s_gate': 8.0,
     'L1_ffn_s_up': 8.0,
     'L1_ffn_s_down': 8.0,
     'L2_ffn_Wr': 8.0,
     'L2_ffn_Wg': 8.0,
     'L2_ffn_Wu': 8.0,
     'L2_ffn_Wd': 8.0,
     'L2_ffn_Sg': 5.154,
     'L2_ffn_Su': 5.03,
     'L2_ffn_Sd': 5.04,
     'L3_attn_Wq': 4.283,
     'L3_attn_bq': 8.0,
     'L3_attn_Wk': 4.111,
     'L3_attn_bk': 8.0,
     'L3_attn_Wv': 2.898,
     'L3_attn_bv': 7.806,
     'L3_attn_Wo': 2.8,
     'L3_attn_bo': 49.668,
     'L3_ffn_W_gate': 8.0,
     'L3_ffn_W_qkv': 8.0,
     'L2_attn_weight_qkv': 4.11,
     'L2_attn_weight_out': 3.91}
    for name, (base, spread) in spreads.items():
        noise = np.random.default_rng([zlib.crc32(name.encode()), seed]).standard_normal(out[name].shape)
        drawn = base * np.exp(spread * noise) if base else spread * noise
        out[name] = jnp.asarray(drawn.astype(out[name].dtype))
    for name, factor in factors.items():
        out[name] = (out[name] * factor).astype(out[name].dtype)
    return out
```

```python
import numpy as np
import concourse.bass as bass
from concourse import mybir
from contextlib import ExitStack

F32, BF16, I32, U32 = mybir.dt.float32, mybir.dt.bfloat16, mybir.dt.int32, mybir.dt.uint32
ALU = mybir.AluOpType
ACT = mybir.ActivationFunctionType
X_AXIS = mybir.AxisListType.X

P = 128
T = 2048
D = 512
C = D // P
TB = 512
NB = T // TB
TT = T // P
TPB = TB // P
H0 = 1376
H1 = 1408
J0 = -(-H0 // P)
J1 = H1 // P
LUT = 16
PIECE = 704
EXPERTS, TOPK, CAP = 64, 4, 128
HX = 128
JS = 8
SLOTS = EXPERTS * CAP
EPS = 1e-5
NEG = -3.0e38
BANKS = 8


class Tally:

    def __init__(self, nc, ctx, name, base=0):
        self.sem = ctx.enter_context(nc.semaphore(name))
        self.base = base


class Chain:

    def __init__(self, tally):
        self.tally, self.engine, self.n = tally, None, 0

    def start(self, engine, passed=0):
        self.engine, self.at, self.n = engine, self.tally.base + passed, 0

    def link(self, ins):
        ins.then_inc(self.tally.sem, 1)
        self.n += 1
        self.engine.wait_ge(self.tally.sem, self.at + self.n)

    def mark(self, ins):
        ins.then_inc(self.tally.sem, 1)
        self.n += 1


class Groups:

    def __init__(self, core, kinds, blocks=NB):
        self.kinds, self.core, self.blocks = kinds, core, blocks
        self.total = {e: kinds.count(e) for e in "av"}
        self.filled0 = core.filled.base
        self.base = {"a": core.emptied_a.base, "v": core.emptied_v.base}

    def bank(self, g):
        return (g + 2) % BANKS

    def wait_free(self, pe, b, g):
        if g >= BANKS:
            self.wait_emptied(pe, b, g - BANKS)

    def wait_emptied(self, eng, b, g):
        e = self.kinds[g]
        tally = self.core.emptied_a if e == "a" else self.core.emptied_v
        eng.wait_ge(tally.sem, self.base[e] + b * self.total[e] + self.kinds[:g + 1].count(e))

    def wait_filled(self, eng, b, g):
        eng.wait_ge(self.core.filled.sem, self.filled0 + b * len(self.kinds) + g + 1)

    def wait_block(self, eng, b):
        eng.wait_ge(self.core.emptied_v.sem, self.base["v"] + b * self.total["v"])

    def close(self):
        self.core.filled.base += self.blocks * len(self.kinds)
        self.core.emptied_a.base += self.blocks * self.total["a"]
        self.core.emptied_v.base += self.blocks * self.total["v"]


class Core:

    def __init__(self, nc, ctx, io):
        self.nc, self.io = nc, io

        def sb(name, shape, dt=F32):
            return ctx.enter_context(nc.sbuf_tensor(name, shape, dt))

        self.x = sb("x", [P, C, T])
        self.ident = sb("ident", [P, P])
        self.ident_b = sb("ident_b", [P, P], BF16)
        self.mask_b = sb("mask_b", [P, P], BF16)
        self.mean_w = sb("mean_w", [P, P])
        self.ones = sb("ones", [P, TB])
        self.eps = sb("eps", [P, 1])
        self.ps = ctx.enter_context(nc.psum_tensor("ps", [P, BANKS, 512], F32))

        def tally(name, base=0):
            return Tally(nc, ctx, name, base)

        self.loaded = tally("loaded")
        self.stored = tally("stored", 1)
        self.const = tally("const")
        self.filled = tally("filled")
        self.emptied_a = tally("emptied_a", 1)
        self.emptied_v = tally("emptied_v", 1)
        self.v_chain, self.a_chain = tally("v_chain"), tally("a_chain")
        self.ln_mean, self.ln_centred, self.ln_squared = tally("ln_mean"), tally("ln_centred"), tally("ln_squared")
        self.ln_var, self.ln_std, self.ln_rstd, self.xn_ready = (
            tally("ln_var"), tally("ln_std"), tally("ln_rstd"), tally("xn_ready"))
        self.split_a, self.split_v = tally("split_a"), tally("split_v")


class Norm:

    def __init__(self, core, ctx, layer):
        self.core, self.layer = core, layer
        nc = core.nc

        def sb(name, shape):
            return ctx.enter_context(nc.sbuf_tensor(f"{name}{layer}", shape, F32))

        self.xc = sb("xc", [P, C, TB])
        self.sq = sb("sq", [P, C, TB])
        self.std = sb("std", [P, TB])
        self.rstd = sb("rstd", [P, TB])
        self.xn = sb("xn", [P, C, TB])

    def count(self, b):
        return NB * (self.layer - self.core.start) + b + 1

    def tensor(self, pe, b):
        k = self.core
        for c in range(C):
            m = pe.matmul(k.ps[:, 0, :], k.mean_w[:, :], k.x[:, c, bass.ds(b * TB, TB)],
                          start=c == 0, stop=c == C - 1)
        m.then_inc(k.ln_mean.sem, 1)
        pe.wait_ge(k.ln_squared.sem, self.count(b))
        for c in range(C):
            m = pe.matmul(k.ps[:, 1, :], k.mean_w[:, :], self.sq[:, c, :], start=c == 0, stop=c == C - 1)
        m.then_inc(k.ln_var.sem, 1)
        pe.wait_ge(k.xn_ready.sem, self.count(b))

    def scalar(self, act, b):
        k = self.core
        act.wait_ge(k.ln_centred.sem, self.count(b))
        act.activation(self.sq[:, :, :], self.xc[:, :, :], ACT.Square).then_inc(k.ln_squared.sem, 1)
        act.wait_ge(k.ln_var.sem, self.count(b))
        act.activation(self.std[:, :], k.ps[:, 1, :], ACT.Sqrt, bias=k.eps[:, 0:1]).then_inc(k.ln_std.sem, 1)

    def vector(self, dve, b):
        k = self.core
        dve.wait_ge(k.ln_mean.sem, self.count(b))
        dve.tensor_tensor(self.xc[:, :, :], k.x[:, :, bass.ds(b * TB, TB)],
                          k.ps[:, 0, :].unsqueeze(1).to_broadcast([P, C, TB]), ALU.subtract)\
           .then_inc(k.ln_centred.sem, 1)
        dve.wait_ge(k.ln_std.sem, self.count(b))
        dve.reciprocal(self.rstd[:, :], self.std[:, :]).then_inc(k.ln_rstd.sem, 1)
        dve.wait_ge(k.ln_rstd.sem, self.count(b))
        dve.wait_ge(k.ln_centred.sem, self.count(b))
        dve.tensor_tensor(self.xn[:, :, :], self.xc[:, :, :],
                          self.rstd[:, :].unsqueeze(1).to_broadcast([P, C, TB]), ALU.mult)\
           .then_inc(k.xn_ready.sem, 1)


def project(pe, out, weights, moving, chunks=C):
    for c in range(chunks):
        m = pe.matmul(out, weights(c), moving(c), start=c == 0, stop=c == chunks - 1)
    return m


def setup(core):
    nc, k = core.nc, core
    with nc.Block() as block:
        @block.sync
        def _(sp):
            for b in range(NB):
                sp.dma_start(k.x[:, :, b * TB:(b + 1) * TB],
                             k.io["xT"].rearrange("(c p) t -> p c t", p=P)[:, :, b * TB:(b + 1) * TB])\
                  .then_inc(k.loaded.sem, 16)
            sp.wait_ge(k.loaded.sem, 16 * NB)

        @block.vector
        def _(dve):
            dve.memset(k.mean_w[:, :], 1.0 / D).then_inc(k.emptied_v.sem, 1)
            dve.memset(k.ones[:, :], 1.0).then_inc(k.emptied_a.sem, 1)
            dve.memset(k.eps[:, :], EPS).then_inc(k.stored.sem, 1)
            dve.wait_ge(k.const.sem, 4)
            dve.tensor_copy(k.ident_b[:, :], k.ident[:, :]).then_inc(k.const.sem, 1)

        @block.gpsimd
        def _(pool):
            pool.memset(k.ident[:, :], 0.0).then_inc(k.const.sem, 1)
            pool.memset(k.mask_b[:, :], 0.0).then_inc(k.const.sem, 1)
            pool.wait_ge(k.const.sem, 2)
            pool.affine_select(out=k.ident[:, :], in_=k.ident[:, :], compare_op=ALU.not_equal, fill=1.0,
                               base=0, pattern=[[-1, P]], channel_multiplier=1).then_inc(k.const.sem, 1)
            pool.affine_select(out=k.mask_b[:, :], in_=k.mask_b[:, :], compare_op=ALU.is_ge, fill=NEG,
                               base=0, pattern=[[-1, P]], channel_multiplier=1).then_inc(k.const.sem, 1)
    k.loaded.base += 16 * NB


def load(eng, core, pairs):
    for dst, src in pairs:
        eng.dma_start(dst, src).then_inc(core.loaded.sem, 16)
    core.loaded.base += 16 * len(pairs)


def layer0(core):
    nc, k, io = core.nc, core, core.io
    with ExitStack() as ctx:
        def sb(name, shape, dt=F32):
            return ctx.enter_context(nc.sbuf_tensor(name, shape, dt))

        wa = sb("wa", [P, 4, C, D])
        ba = sb("ba", [P, 4, C])
        wf = sb("wf", [P, 24 * PIECE])
        w_gate = wf[:, 0:C * H1].rearrange("p (c n) -> p c n", c=C)
        w_up = wf[:, C * H1:2 * C * H1].rearrange("p (c n) -> p c n", c=C)
        w_down = wf[:, 2 * C * H1:2 * C * H1 + J0 * D].rearrange("p (j n) -> p j n", j=J0)
        loads = [(wa[:, :, :, :], io["L0_w"]), (ba[:, :, :], io["L0_b"])]

        look_up(core, wf, loads)

        norm = Norm(core, ctx, 0)
        carry = sb("carry", [P, C])
        v_sb, g_sb = sb("v_sb", [P, 2, TB]), sb("g_sb", [P, 2, TB])
        kv, kvs, qg = sb("kv", [P, TB]), sb("kvs", [P, TB]), sb("qg", [P, TB])
        h = sb("h", [P, J0, TB])
        sg = sb("sg", [P, 2, TB])

        grp = Groups(core, "avav" * C + "av" * J0 + "v" * C)
        ffn, down = 4 * C, 4 * C + 2 * J0
        per_block = 4 * C
        chain = Chain(k.v_chain)

        with nc.Block() as block:
            @block.tensor
            def _(pe):
                with pe.Fori(0, NB) as b:
                    grp.wait_block(pe, b)
                    norm.tensor(pe, b)
                    for g in range(4 * C):
                        grp.wait_free(pe, b, g)
                        oc, which = g // 4, g % 4
                        project(pe, k.ps[:, grp.bank(g), :], lambda c: wa[:, which, c, oc * P:(oc + 1) * P],
                                lambda c: norm.xn[:, c, :]).then_inc(k.filled.sem, 1)
                    for j in range(J0):
                        rows = min(P, H0 - j * P)
                        for u, w in enumerate((w_gate, w_up)):
                            g = ffn + 2 * j + u
                            grp.wait_free(pe, b, g)
                            project(pe, k.ps[0:rows, grp.bank(g), :], lambda c: w[:, c, j * P:j * P + rows],
                                    lambda c: norm.xn[:, c, :]).then_inc(k.filled.sem, 1)
                    grp.wait_emptied(pe, b, down - 1)
                    for oc in range(C):
                        grp.wait_free(pe, b, down + oc)
                        for j in range(J0):
                            rows = min(P, H0 - j * P)
                            m = pe.matmul(k.ps[:, grp.bank(down + oc), :], w_down[0:rows, j, oc * P:(oc + 1) * P],
                                          h[0:rows, j, :], start=j == 0, stop=j == J0 - 1)
                        m.then_inc(k.filled.sem, 1)

            @block.scalar
            def _(act):
                with act.Fori(0, NB) as b:
                    norm.scalar(act, b)
                    for oc in range(C):
                        if oc >= 2:
                            grp.wait_emptied(act, b, 4 * (oc - 2) + 3)
                        else:
                            grp.wait_block(act, b)
                        grp.wait_filled(act, b, 4 * oc)
                        act.activation(v_sb[:, oc % 2, :], k.ps[:, grp.bank(4 * oc), :], ACT.Identity,
                                       bias=ba[:, 0, oc:oc + 1]).then_inc(k.emptied_a.sem, 1)
                        grp.wait_filled(act, b, 4 * oc + 2)
                        act.activation(g_sb[:, oc % 2, :], k.ps[:, grp.bank(4 * oc + 2), :], ACT.Sigmoid,
                                       bias=ba[:, 2, oc:oc + 1]).then_inc(k.emptied_a.sem, 1)
                    for j in range(J0):
                        rows = min(P, H0 - j * P)
                        g = ffn + 2 * j
                        if j >= 2:
                            grp.wait_emptied(act, b, g - 3)
                        grp.wait_filled(act, b, g)
                        act.activation(sg[0:rows, j % 2, :], k.ps[0:rows, grp.bank(g), :], ACT.Silu)\
                           .then_inc(k.emptied_a.sem, 1)

            @block.vector
            def _(dve):
                chain.start(dve)
                chain.link(dve.memset(carry[:, :], 0.0))
                with dve.Fori(0, NB) as b:
                    norm.vector(dve, b)
                    chain.start(dve, 1 + b * per_block)
                    for oc in range(C):
                        grp.wait_filled(dve, b, 4 * oc + 1)
                        grp.wait_emptied(dve, b, 4 * oc)
                        dve.scalar_tensor_tensor(kv[:, :], k.ps[:, grp.bank(4 * oc + 1), :], ba[:, 1, oc:oc + 1],
                                                 v_sb[:, oc % 2, :], ALU.add, ALU.mult).then_inc(k.emptied_v.sem, 1)
                        grp.wait_emptied(dve, b, 4 * oc + 1)
                        chain.link(dve.tensor_tensor_scan(kvs[:, :], k.ones[:, :], kv[:, :], carry[:, oc:oc + 1],
                                                          ALU.mult, ALU.add))
                        chain.mark(dve.tensor_copy(carry[:, oc:oc + 1], kvs[:, TB - 1:TB]))
                        grp.wait_filled(dve, b, 4 * oc + 3)
                        grp.wait_emptied(dve, b, 4 * oc + 2)
                        dve.scalar_tensor_tensor(qg[:, :], k.ps[:, grp.bank(4 * oc + 3), :], ba[:, 3, oc:oc + 1],
                                                 g_sb[:, oc % 2, :], ALU.add, ALU.mult).then_inc(k.emptied_v.sem, 1)
                        grp.wait_emptied(dve, b, 4 * oc + 3)
                        chain.link(dve.tensor_tensor(qg[:, :], qg[:, :], kvs[:, :], ALU.mult))
                        xs = k.x[:, oc, bass.ds(b * TB, TB)]
                        chain.link(dve.tensor_tensor(xs, xs, qg[:, :], ALU.add))
                    for j in range(J0):
                        rows = min(P, H0 - j * P)
                        g = ffn + 2 * j
                        grp.wait_emptied(dve, b, g)
                        grp.wait_filled(dve, b, g + 1)
                        dve.tensor_tensor(h[0:rows, j, :], k.ps[0:rows, grp.bank(g + 1), :], sg[0:rows, j % 2, :],
                                          ALU.mult).then_inc(k.emptied_v.sem, 1)
                    for oc in range(C):
                        grp.wait_filled(dve, b, down + oc)
                        xs = k.x[:, oc, bass.ds(b * TB, TB)]
                        dve.tensor_tensor(xs, xs, k.ps[:, grp.bank(down + oc), :], ALU.add)\
                           .then_inc(k.emptied_v.sem, 1)
                    assert chain.n == per_block
        grp.close()
        k.v_chain.base += 1 + NB * per_block


def look_up(core, wf, loads):
    nc, k, io = core.nc, core, core.io
    pieces = 24
    with ExitStack() as ctx:
        def sb(name, shape, dt=F32):
            return ctx.enter_context(nc.sbuf_tensor(name, shape, dt))

        table, step = sb("table", [P, LUT]), sb("step", [P, LUT // 2])
        idx = sb("idx", [P, 2, PIECE], I32)
        bit0 = sb("bit0", [P, 2, PIECE], I32)
        bits = sb("bits", [P, 2, 3, PIECE], I32)
        cand = sb("cand", [P, 8, PIECE])

        hop = sb("hop", [P, 1])
        idx_in = [Tally(nc, ctx, f"idx_in{p}") for p in range(2)]
        idx_used, bit0_ready, cand_ready, picked, kept = (
            Tally(nc, ctx, n) for n in ("idx_used", "bit0_ready", "cand_ready", "picked", "kept"))
        with nc.Block() as block:
            @block.sync
            def _(sp):
                sp.dma_start(table[:, :], io["L0_ffn_lut"].partition_broadcast(P)).then_inc(k.loaded.sem, 16)
                for p in range(2):
                    sp.dma_start(idx[:, p, :], io["L0_idx"][:, p, :]).then_inc(idx_in[p].sem, 16)
                with sp.Fori(0, pieces // 2 - 1) as i:
                    for p in range(2):
                        sp.wait_ge(idx_used.sem, 2 * i + p + 1)
                        sp.dma_start(idx[:, p, :], io["L0_idx"][:, bass.ds(2 * i + p + 2, 1), :]
                                     .rearrange("p a n -> p (a n)")).then_inc(idx_in[p].sem, 16)
                for dst, src in loads:
                    sp.dma_start(dst, src).then_inc(k.loaded.sem, 16)
                sp.wait_ge(k.loaded.sem, k.loaded.base + 16 + 16 * len(loads))

            @block.vector
            def _(dve):
                dve.wait_ge(k.loaded.sem, k.loaded.base + 16)
                pairs = table[:, :].rearrange("p (n two) -> p n two", two=2)
                dve.tensor_tensor(step[:, :], pairs[:, :, 1], pairs[:, :, 0], ALU.subtract).then_inc(k.v_chain.sem, 1)
                with dve.Fori(0, pieces // 2) as i:
                    for p in range(2):
                        n = 2 * i + p
                        dve.wait_ge(idx_in[p].sem, 16 * (i + 1))
                        dve.tensor_scalar(bit0[:, p, :], idx[:, p, :], 1, None, ALU.bitwise_and)\
                           .then_inc(bit0_ready.sem, 1)
                        for q in range(3):
                            m = dve.tensor_scalar(bits[:, p, q, :], idx[:, p, :], 2 << q, None, ALU.bitwise_and)
                        m.then_inc(idx_used.sem, 1)
                        dve.wait_ge(idx_used.sem, n + 1)
                        dve.wait_ge(cand_ready.sem, n + 1)
                        dve.memset(hop[:, :], 0.0).then_inc(picked.sem, 1)
                        for q, n_out in enumerate((4, 2, 1)):
                            stride = 2 << q
                            out = cand[:, 0::stride, :]
                            dve.wait_ge(picked.sem, 4 * n + 1 + q)
                            dve.memset(hop[:, :], 0.0)
                            dve.copy_predicated(out, bits[:, p, q, :].unsqueeze(1).to_broadcast([P, n_out, PIECE]),
                                                cand[:, stride // 2::stride, :]).then_inc(picked.sem, 1)

            @block.scalar
            def _(act):
                act.wait_ge(k.v_chain.sem, k.v_chain.base + 1)
                with act.Fori(0, pieces // 2) as i:
                    for p in range(2):
                        n = 2 * i + p
                        act.wait_ge(bit0_ready.sem, n + 1)
                        for q in range(8):
                            m = act.activation(cand[:, q, :], bit0[:, p, :], ACT.Identity,
                                               bias=table[:, 2 * q:2 * q + 1], scale=step[:, q:q + 1])
                        m.then_inc(cand_ready.sem, 1)
                        act.wait_ge(picked.sem, 4 * n + 4)
                        act.activation(wf[:, bass.ds(n * PIECE, PIECE)], cand[:, 0, :], ACT.Copy)\
                           .then_inc(kept.sem, 1)
                        act.wait_ge(kept.sem, n + 1)
        k.loaded.base += 16 + 16 * len(loads)
        k.v_chain.base += 1


class Split:

    def __init__(self, core, ctx, name, items):
        self.core, self.items = core, items
        nc = core.nc
        self.parts = ctx.enter_context(nc.sbuf_tensor("parts" + name, [P, 2, 3, TB], BF16))
        self.rest = ctx.enter_context(nc.sbuf_tensor("rest" + name, [P, 2, TB], F32))
        self.stored = [Tally(nc, ctx, f"parts_stored{name}{n}") for n in range(2)]
        self.a0, self.v0 = core.split_a.base, core.split_v.base
        self.per_buffer = [(items + 1) // 2, items // 2]

    def step(self, b, i):
        return b * (2 * self.items) + 2 * i

    def prime(self, dve):
        for n in range(2):
            dve.memset(self.rest[:, n, 0:1], 0.0).then_inc(self.stored[n].sem, 1)

    def wait_free(self, act, b, i):
        act.wait_ge(self.stored[i % 2].sem, 16 * (b * self.per_buffer[i % 2] + i // 2) + 1)

    def scalar_1(self, act, b, i, src, scale, rows=P):
        self.wait_free(act, b, i)
        act.activation(self.parts[0:rows, i % 2, 0, :], src, ACT.Copy, scale=scale)\
           .then_inc(self.core.split_a.sem, 1)

    def vector_1(self, dve, b, i, src, scale, rows=P):
        dve.wait_ge(self.core.split_a.sem, self.a0 + self.step(b, i) + 1)
        dve.scalar_tensor_tensor(self.rest[0:rows, i % 2, :], src, scale, self.parts[0:rows, i % 2, 0, :],
                                 ALU.mult, ALU.subtract).then_inc(self.core.split_v.sem, 1)

    def scalar_2(self, act, b, i, rows=P):
        act.wait_ge(self.core.split_v.sem, self.v0 + self.step(b, i) + 1)
        act.activation(self.parts[0:rows, i % 2, 1, :], self.rest[0:rows, i % 2, :], ACT.Copy)\
           .then_inc(self.core.split_a.sem, 1)

    def vector_2(self, dve, b, i, rows=P):
        dve.wait_ge(self.core.split_a.sem, self.a0 + self.step(b, i) + 2)
        dve.tensor_tensor(self.parts[0:rows, i % 2, 2, :], self.rest[0:rows, i % 2, :],
                          self.parts[0:rows, i % 2, 1, :], ALU.subtract).then_inc(self.core.split_v.sem, 1)

    def store(self, sp, b, i, dst, rows=P, after=0):
        if after is not None:
            sp.wait_ge(self.core.split_v.sem, self.v0 + self.step(b, i + after) + 2)
        sp.dma_start(dst[:, :, bass.ds(b * TB, TB)].rearrange("a r t -> r a t"),
                     self.parts[0:rows, i % 2, :, :]).then_inc(self.stored[i % 2].sem, 16)

    def wait_done(self, act, b, i):
        act.wait_ge(self.core.split_v.sem, self.v0 + self.step(b, i) + 1)

    def wait_stores(self, sp):
        for n in range(2):
            sp.wait_ge(self.stored[n].sem, 16 * NB * self.per_buffer[n] + 1)

    def close(self):
        self.core.split_a.base += 2 * NB * self.items
        self.core.split_v.base += 2 * NB * self.items


def banks_of(i):
    return -(-(i + 1) // 4)


def score_bank(i):
    return {1: i % 4, 2: 2 * (i % 2)}.get(banks_of(i), 0)


def overlapping(i):
    def mine(e):
        return set(range(score_bank(e), score_bank(e) + banks_of(e)))
    return max([e for e in range(i) if mine(e) & mine(i)], default=-1)


def attention(core, name, heads, dh, q_parts, k_parts, v_all, out, shared=False):
    nc, k = core.nc, core
    passes = 2 if dh == 32 else 1
    assert 8 * dh == P * passes
    chunks = [(i, c) for i in range(TT) for c in range(banks_of(i))]
    by_a = [c < (banks_of(i) + 1) // 2 for i, c in chunks]
    NC, NA = len(chunks), sum(by_a)
    NV = NC - NA
    RING = 4
    assert NC % RING == 0 and not by_a[-1] and not by_a[-2]

    with ExitStack() as ctx:
        def sb(nm, shape, dt=F32):
            return ctx.enter_context(nc.sbuf_tensor(nm + name, shape, dt))

        def tally(nm, base=0):
            return Tally(nc, ctx, nm + name, base)

        qs, ks = sb("qs", [P, 2, passes, T], BF16), sb("ks", [P, 2, passes, T], BF16)
        vh = None if shared else sb("vh", [P, 2, TT, dh])
        prob, turned_sb = sb("prob", [P, 2, T]), sb("turned_sb", [P, RING, 512])
        top, total, inv = sb("top", [P, 2, TT]), sb("total", [P, 2, TT]), sb("inv", [P, 2, TT])
        o_sb = sb("o_sb", [dh, 2, T])
        free_note = sb("free_note", [1, 8])

        qk_in = [tally(f"qk_in{n}") for n in range(2)]
        v_in = None if shared else tally("v_in")
        scored, top_ready, exp_done = tally("scored", 2 * TT), tally("top_ready"), tally("exp_done", 1)
        inv_done, scaled, turned = tally("inv_done"), tally("scaled"), tally("turned")
        copied_a, copied_v = tally("copied_a"), tally("copied_v", 2)
        used = tally("used", NC + RING)
        o_copied = tally("o_copied", 2)
        o_stored = [tally(f"o_stored{n}", 1) for n in range(2)]

        def wait_copied(eng, h, t):
            tl, per, mine = (copied_a, NA, True) if by_a[t] else (copied_v, NV, False)
            eng.wait_ge(tl.sem, tl.base + (h if t >= 0 else h - 1) * per
                        + sum(f == mine for f in by_a[:t % NC + 1]))

        def chunk_range(i):
            return range(chunks.index((i, 0)), chunks.index((i, 0)) + banks_of(i))

        def scores(i):
            return k.ps[:, score_bank(i):score_bank(i) + banks_of(i), :].rearrange("p a n -> p (a n)")\
                [:, 0:(i + 1) * P]

        def tiles_of(t):
            i, c = chunks[t]
            return range(4 * c, min(4 * c + 4, i + 1))

        def copy_chunk(eng, h, t):
            width = P * len(tiles_of(t))
            eng.wait_ge(used.sem, NC * h + t + 1 + NC)
            eng.wait_ge(turned.sem, NC * h + t + 1)
            src, dst = k.ps[:, 4 + t % 2, 0:width], turned_sb[:, t % RING, 0:width]
            if by_a[t]:
                eng.activation(dst, src, ACT.Copy).then_inc(copied_a.sem, 1)
            else:
                eng.tensor_copy(dst, src).then_inc(copied_v.sem, 1)

        with nc.Block() as block:
            @block.gpsimd
            def _(pool):
                for n, tl in enumerate((scored, exp_done, copied_v, used, o_copied, *o_stored)):
                    pool.memset(free_note[:, n:n + 1], 0.0).then_inc(tl.sem, tl.base)
                if shared:
                    return
                with pool.Fori(0, heads // 2) as it:
                    for p in range(2):
                        h = 2 * it + p
                        pool.wait_ge(used.sem, NC * h + RING)
                        pool.tensor_copy(vh[:, p, :, :], v_all[:, :, bass.ds(h * dh, dh)]).then_inc(v_in.sem, 1)

            @block.sync
            def _(sp):
                with sp.Fori(0, heads // 2) as it:
                    for p in range(2):
                        h = 2 * it + p
                        sp.wait_ge(scored.sem, TT * h + TT)
                        for parts, dst, same, order in ((q_parts, qs, False, (0, 0, 1, 1, 0, 1, 2, 2)),
                                                        (k_parts, ks, shared, (0, 1, 0, 1, 2, 2, 0, 1))):
                            for n, which in enumerate(order):
                                at, ps_ = n * dh % P, n * dh // P
                                rows = slice(0, dh) if same else bass.ds(h * dh, dh)
                                sp.dma_start(dst[at:at + dh, p, ps_, :], parts[which, rows, :])\
                                  .then_inc(qk_in[p].sem, 16)

            @block.tensor
            def _(pe):
                def score(h, p, i):
                    pe.wait_ge(exp_done.sem, TT * h + 1 + overlapping(i) + 1)
                    if i == 0:
                        pe.wait_ge(qk_in[p].sem, 16 * 16 * (it + 1))
                    for c in range(banks_of(i)):
                        width = min(512, (i + 1) * P - 512 * c)
                        bank, last = score_bank(i) + c, c == banks_of(i) - 1
                        if last:
                            pe.matmul(k.ps[:, bank, width - P:width], k.ident_b[:, :], k.mask_b[:, :],
                                      start=True, stop=False, skip_group_check=True)
                        for s in range(passes):
                            m = pe.matmul(k.ps[:, bank, 0:width], qs[:, p, s, i * P:(i + 1) * P],
                                          ks[:, p, s, 512 * c:512 * c + width], start=s == 0 and not last,
                                          stop=s == passes - 1, skip_group_check=True)
                    m.then_inc(scored.sem, 1)

                def turn(h, t):
                    i, c = chunks[t]
                    if c == 0:
                        pe.wait_ge(scaled.sem, TT * h + i + 1)
                    wait_copied(pe, h, t - 2)
                    for n, kt in enumerate(tiles_of(t)):
                        m = pe.transpose(k.ps[:, 4 + t % 2, n * P:(n + 1) * P],
                                         prob[:, i % 2, kt * P:(kt + 1) * P], k.ident[:, :])
                    m.then_inc(turned.sem, 1)

                def weigh(h, p, t):
                    i, c = chunks[t]
                    if t == 0 and not shared:
                        pe.wait_ge(v_in.sem, h + 1)
                    if i % 4 == 0 and c == 0:
                        pe.wait_ge(o_copied.sem, 4 * h + i // 4 + 1)
                    wait_copied(pe, h, t)
                    for n, kt in enumerate(tiles_of(t)):
                        m = pe.matmul(k.ps[0:dh, 6 + i // 4 % 2, i % 4 * P:(i % 4 + 1) * P],
                                      v_all[:, kt, :] if shared else vh[:, p, kt, :],
                                      turned_sb[:, t % RING, n * P:(n + 1) * P],
                                      start=kt == 0, stop=kt == i)
                    m.then_inc(used.sem, 1)

                pe.wait_ge(exp_done.sem, 1)
                with pe.Fori(0, heads // 2) as it:
                    for p in range(2):
                        h = 2 * it + p
                        for i in range(TT + 1):
                            if i < TT:
                                score(h, p, i)
                            if i >= 1:
                                for t in chunk_range(i - 1):
                                    turn(h, t)
                                    if t >= 1:
                                        weigh(h, p, t - 1)
                        weigh(h, p, NC - 1)

            @block.scalar
            def _(act):
                with act.Fori(0, heads // 2) as it:
                    for p in range(2):
                        h = 2 * it + p
                        for i in range(TT + 1):
                            if i >= 1:
                                for t in chunk_range(i - 1):
                                    if by_a[t]:
                                        copy_chunk(act, h, t)
                            if i < TT:
                                act.wait_ge(top_ready.sem, TT * h + i + 1)
                                act.activation(prob[:, i % 2, 0:(i + 1) * P], scores(i), ACT.Exp,
                                               bias=top[:, p, i:i + 1], accum_out=total[:, p, i:i + 1])\
                                   .then_inc(exp_done.sem, 1)
                            if i in (5, 9, 13, TT):
                                qb = (i - 2) // 4
                                if qb == 0:
                                    act.wait_ge(o_stored[p].sem, 16 * it + 1)
                                act.wait_ge(used.sem, NC * (h + 1) + RING + chunk_range(4 * qb + 3)[-1] + 1)
                                act.activation(o_sb[:, p, qb * 512:(qb + 1) * 512],
                                               k.ps[0:dh, 6 + qb % 2, :], ACT.Copy).then_inc(o_copied.sem, 1)
                        act.wait_ge(o_copied.sem, 4 * (h + 1) + 2)
                        act.dma_start(out[bass.ds(h * dh, dh), :], o_sb[:, p, :]).then_inc(o_stored[p].sem, 16)
                for p in range(2):
                    act.wait_ge(o_stored[p].sem, 16 * (heads // 2) + 1)

            @block.vector
            def _(dve):
                with dve.Fori(0, heads // 2) as it:
                    for p in range(2):
                        h = 2 * it + p
                        for i in range(TT + 1):
                            if i < TT:
                                dve.wait_ge(scored.sem, TT * (h + 2) + i + 1)
                                dve.tensor_reduce(top[:, p, i:i + 1], scores(i), X_AXIS, ALU.max, negate=True)\
                                   .then_inc(top_ready.sem, 1)
                            if i >= 1:
                                for t in chunk_range(i - 1):
                                    if not by_a[t]:
                                        copy_chunk(dve, h, t)
                            if i < TT:
                                dve.wait_ge(exp_done.sem, TT * h + i + 2)
                                dve.reciprocal(inv[:, p, i:i + 1], total[:, p, i:i + 1]).then_inc(inv_done.sem, 1)
                                dve.wait_ge(inv_done.sem, TT * h + i + 1)
                                row = prob[:, i % 2, 0:(i + 1) * P]
                                dve.tensor_scalar(row, row, inv[:, p, i:i + 1], None, ALU.mult)\
                                   .then_inc(scaled.sem, 1)


def layer1(core):
    nc, k, io = core.nc, core, core.io
    with ExitStack() as ctx:
        def sb(name, shape, dt=F32):
            return ctx.enter_context(nc.sbuf_tensor(name, shape, dt))

        v_all = sb("v1_all", [P, TT, P])
        with ExitStack() as inner:
            layer1_blocks(core, inner, v_all)
        attention(core, "1", 8, 16, io["q1_parts"], io["k1_parts"], v_all, io["o1"])
        w_out, b_out = sb("w_out1", [P, 1, D]), sb("b_out1", [P, C])
        project_out(core, ctx, "1", io["o1"], None, w_out, b_out,
                    [(w_out[:, 0, :], io["L1_out_w"]), (b_out[:, :], io["L1_out_b"])])


def project_out(core, ctx, name, heads_out, added, weights, bias, loads, result=None):
    nc, k = core.nc, core
    chunks = weights.shape[1]
    o_in = ctx.enter_context(nc.sbuf_tensor("o_in" + name, [P, 2, chunks, TB], F32))
    a_in = ctx.enter_context(nc.sbuf_tensor("a_in" + name, [P, 2, C, TB], F32)) if added is not None else None
    arrived = [Tally(nc, ctx, f"o_arrived{name}{n}") for n in range(2)]
    per = 2 if added is not None else 1
    grp = Groups(core, "v" * C)
    chain = Chain(k.v_chain)
    per_chain = C if added is not None else 0
    with nc.Block() as block:
        @block.sync
        def _(sp):
            load(sp, core, loads)

            def fetch(b, p):
                sp.dma_start(o_in[:, p, :, :], heads_out.rearrange("(c p) t -> p c t", p=P)
                             [:, :, bass.ds(b * TB, TB)]).then_inc(arrived[p].sem, 16)
                if added is not None:
                    sp.dma_start(a_in[:, p, :, :], added.rearrange("(c p) t -> p c t", p=P)
                                 [:, :, bass.ds(b * TB, TB)]).then_inc(arrived[p].sem, 16)

            for b in range(NB):
                if b >= 2:
                    grp.wait_block(sp, b - 1)
                fetch(b, b % 2)
            if result is not None:
                for b in range(NB):
                    grp.wait_block(sp, b + 1)
                    sp.dma_start(result.rearrange("(c p) t -> p c t", p=P)[:, :, b * TB:(b + 1) * TB],
                                 k.x[:, :, b * TB:(b + 1) * TB]).then_inc(k.stored.sem, 16)
                sp.wait_ge(k.stored.sem, k.stored.base + 16 * NB)

        @block.tensor
        def _(pe):
            pe.wait_ge(k.loaded.sem, k.loaded.base)
            for b in range(NB):
                grp.wait_block(pe, b)
                pe.wait_ge(arrived[b % 2].sem, 16 * per * (b // 2 + 1))
                for oc in range(C):
                    project(pe, k.ps[:, grp.bank(oc), :], lambda c: weights[:, c, oc * P:(oc + 1) * P],
                            lambda c: o_in[:, b % 2, c, :], chunks).then_inc(k.filled.sem, 1)

        @block.vector
        def _(dve):
            dve.wait_ge(k.loaded.sem, k.loaded.base)
            for b in range(NB):
                chain.start(dve, b * per_chain)
                for oc in range(C):
                    xs = k.x[:, oc, b * TB:(b + 1) * TB]
                    if added is not None:
                        dve.wait_ge(arrived[b % 2].sem, 16 * per * (b // 2 + 1))
                        chain.link(dve.tensor_tensor(xs, xs, a_in[:, b % 2, oc, :], ALU.add))
                    grp.wait_filled(dve, b, oc)
                    dve.scalar_tensor_tensor(xs, k.ps[:, grp.bank(oc), :], bias[:, oc:oc + 1], xs,
                                             ALU.add, ALU.add).then_inc(k.emptied_v.sem, 1)
    grp.close()
    k.v_chain.base += NB * per_chain


def widen(core, ctx, name, dst, src, pieces, loads):
    nc, k = core.nc, core
    with ExitStack() as inner:
        raw = inner.enter_context(nc.sbuf_tensor("raw" + name, [P, 2, 2 * PIECE], I32))
        raw_in = [Tally(nc, ctx, f"raw_in{name}{n}") for n in range(2)]
        widened = Tally(nc, ctx, "widened" + name, 2)
        with nc.Block() as block:
            @block.gpsimd
            def _(pool):
                pool.memset(raw[0:1, 0, 0:1], 0).then_inc(widened.sem, 2)

            @block.sync
            def _(sp):
                for dst_, src_ in loads:
                    sp.dma_start(dst_, src_).then_inc(k.loaded.sem, 16)
                with sp.Fori(0, pieces // 2) as i:
                    for p in range(2):
                        n = 2 * i + p
                        sp.wait_ge(widened.sem, n + 1)
                        sp.dma_start(raw[:, p, :], src[:, bass.ds(n, 1), :].rearrange("p a n -> p (a n)"))\
                          .then_inc(raw_in[p].sem, 16)
                sp.wait_ge(k.loaded.sem, k.loaded.base + 16 * len(loads))

            @block.vector
            def _(dve):
                dve.wait_ge(widened.sem, 2)
                with dve.Fori(0, pieces // 2) as i:
                    for p in range(2):
                        n = 2 * i + p
                        dve.wait_ge(raw_in[p].sem, 16 * (i + 1))
                        dve.tensor_scalar(dst[:, bass.ds(n * 2 * PIECE, 2 * PIECE)], raw[:, p, :], -128.0, None,
                                          ALU.add).then_inc(widened.sem, 1)
        k.loaded.base += 16 * len(loads)


def layer1_blocks(core, ctx, v_all):
    nc, k, io = core.nc, core, core.io

    def sb(name, shape, dt=F32):
        return ctx.enter_context(nc.sbuf_tensor(name, shape, dt))

    wp = sb("wp1", [P, 3, C, P])
    bp = sb("bp1", [P, 3])
    wv, bv = sb("wv1", [P, P]), sb("bv1", [P, P])
    rot = sb("rot1", [P, P])
    wf = sb("wf1", [P, (2 * C + C) * H1])
    w_gate = wf[:, 0:C * H1].rearrange("p (c n) -> p c n", c=C)
    w_up = wf[:, C * H1:2 * C * H1].rearrange("p (c n) -> p c n", c=C)
    w_down = wf[:, 2 * C * H1:].rearrange("p (j n) -> p j n", j=J1)
    s_hid, s_down = sb("s_hid", [P, 2, J1]), sb("s_down", [P, C])
    widen(core, ctx, "1", wf, io["L1_wq"], 12,
          [(wp[:, :, :, :], io["L1_w"]), (bp[:, :], io["L1_b"]), (wv[:, :], io["L1_cv_w"]),
           (bv[:, :], io["L1_cv_b"].partition_broadcast(P)), (rot[:, :], io["L1_rot"]),
           (s_hid[:, :, :], io["L1_s_hid"]), (s_down[:, :], io["L1_s_down"])])

    norm = Norm(core, ctx, 1)
    split = Split(core, ctx, "1", 2)
    plain = sb("plain1", [P, 2, TB])
    turned_, mixed = sb("turned1", [P, 2, TB]), sb("mixed1", [P, 2, TB])
    act_qk = sb("act_qk1", [P, 2, TB])
    ckv = sb("ckv", [P, TB])
    wave = sb("wave1", [P, 2, TB])
    h, sg = sb("h1", [P, J1, TB]), sb("sg1", [P, 2, TB])
    wave_in = Tally(nc, ctx, "wave_in1")
    qk_act = Tally(nc, ctx, "qk_act1")

    grp = Groups(core, "aaa" + "vv" + "v" + "av" * J1 + "v" * C)
    Q, K_, KV, RQ, RK, V, FFN = 0, 1, 2, 3, 4, 5, 6
    DOWN = FFN + 2 * J1
    chain = Chain(k.v_chain)
    per_block = 4

    with nc.Block() as block:
        @block.sync
        def _(sp):
            with sp.Fori(0, NB) as b:
                split.store(sp, b, 0, io["q1_parts"], after=1)
                split.store(sp, b, 1, io["k1_parts"], after=None)
            split.wait_stores(sp)

        @block.tensor
        def _(pe):
            with pe.Fori(0, NB) as b:
                grp.wait_block(pe, b)
                norm.tensor(pe, b)
                for g, w in ((Q, 0), (K_, 2), (KV, 1)):
                    project(pe, k.ps[:, grp.bank(g), :], lambda c: wp[:, w, c, :], lambda c: norm.xn[:, c, :])\
                        .then_inc(k.filled.sem, 1)
                for n, g in enumerate((RQ, RK)):
                    grp.wait_emptied(pe, b, (Q, K_)[n])
                    pe.matmul(k.ps[:, grp.bank(g), :], rot[:, :], plain[:, n, :], start=True, stop=True)\
                      .then_inc(k.filled.sem, 1)
                grp.wait_emptied(pe, b, KV)
                for t in range(TPB):
                    m = pe.matmul(k.ps[:, grp.bank(V), t * P:(t + 1) * P], ckv[:, t * P:(t + 1) * P], wv[:, :],
                                  start=True, stop=True)
                m.then_inc(k.filled.sem, 1)
                for j in range(J1):
                    for u, w in enumerate((w_gate, w_up)):
                        g = FFN + 2 * j + u
                        grp.wait_free(pe, b, g)
                        project(pe, k.ps[:, grp.bank(g), :], lambda c: w[:, c, j * P:(j + 1) * P],
                                lambda c: norm.xn[:, c, :]).then_inc(k.filled.sem, 1)
                grp.wait_emptied(pe, b, DOWN - 1)
                for oc in range(C):
                    grp.wait_free(pe, b, DOWN + oc)
                    project(pe, k.ps[:, grp.bank(DOWN + oc), :], lambda j: w_down[:, j, oc * P:(oc + 1) * P],
                            lambda j: h[:, j, :], J1).then_inc(k.filled.sem, 1)

        @block.scalar
        def _(act):
            with act.Fori(0, NB) as b:
                grp.wait_block(act, b)
                act.dma_start(wave[:, :, :], io["L1_wave"][:, :, bass.ds(b * TB, TB)]).then_inc(wave_in.sem, 16)
                norm.scalar(act, b)
                for n, g in enumerate((Q, K_)):
                    grp.wait_filled(act, b, g)
                    act.activation(plain[:, n, :], k.ps[:, grp.bank(g), :], ACT.Identity,
                                   bias=bp[:, 2 * n:2 * n + 1]).then_inc(k.emptied_a.sem, 1)
                grp.wait_filled(act, b, KV)
                act.activation(ckv[:, :], k.ps[:, grp.bank(KV), :], ACT.Gelu, bias=bp[:, 1:2])\
                   .then_inc(k.emptied_a.sem, 1)
                for n in range(2):
                    act.wait_ge(k.v_chain.sem, chain.tally.base + b * per_block + 2 * n + 2)
                    act.activation(act_qk[:, n, :], mixed[:, n, :], ACT.Gelu).then_inc(qk_act.sem, 1)
                    act.wait_ge(qk_act.sem, 2 * b + n + 1)
                    split.scalar_1(act, b, n, act_qk[:, n, :], (0.25, 1.0)[n])
                    split.scalar_2(act, b, n)
                for j in range(J1):
                    g = FFN + 2 * j
                    if j >= 2:
                        grp.wait_emptied(act, b, g - 3)
                    grp.wait_filled(act, b, g)
                    act.activation(sg[:, j % 2, :], k.ps[:, grp.bank(g), :], ACT.Silu, scale=s_hid[:, 0, j:j + 1])\
                       .then_inc(k.emptied_a.sem, 1)

        @block.vector
        def _(dve):
            split.prime(dve)
            with dve.Fori(0, NB) as b:
                norm.vector(dve, b)
                chain.start(dve, b * per_block)
                dve.wait_ge(wave_in.sem, 16 * (b + 1))
                for n, (g, r) in enumerate(((Q, RQ), (K_, RK))):
                    grp.wait_emptied(dve, b, g)
                    chain.mark(dve.tensor_tensor(mixed[:, n, :], plain[:, n, :], wave[:, 0, :], ALU.mult))
                    grp.wait_filled(dve, b, r)
                    dve.tensor_tensor(turned_[:, n, :], k.ps[:, grp.bank(r), :], wave[:, 1, :], ALU.mult)\
                       .then_inc(k.emptied_v.sem, 1)
                    grp.wait_emptied(dve, b, r)
                    dve.wait_ge(k.v_chain.sem, chain.at + chain.n)
                    chain.link(dve.tensor_tensor(mixed[:, n, :], mixed[:, n, :], turned_[:, n, :], ALU.add))
                for n in range(2):
                    dve.wait_ge(qk_act.sem, 2 * b + n + 1)
                    split.vector_1(dve, b, n, act_qk[:, n, :], (0.25, 1.0)[n])
                    split.vector_2(dve, b, n)
                grp.wait_filled(dve, b, V)
                dve.tensor_tensor(v_all[:, bass.ds(b * TPB, TPB), :],
                                  k.ps[:, grp.bank(V), :].rearrange("p (t n) -> p t n", t=TPB),
                                  bv[:, :].unsqueeze(1).to_broadcast([P, TPB, P]), ALU.add)\
                   .then_inc(k.emptied_v.sem, 1)
                assert chain.n == per_block
                for j in range(J1):
                    g = FFN + 2 * j
                    grp.wait_emptied(dve, b, g)
                    grp.wait_filled(dve, b, g + 1)
                    dve.scalar_tensor_tensor(h[:, j, :], k.ps[:, grp.bank(g + 1), :], s_hid[:, 1, j:j + 1],
                                             sg[:, j % 2, :], ALU.mult, ALU.mult).then_inc(k.emptied_v.sem, 1)
                for oc in range(C):
                    grp.wait_filled(dve, b, DOWN + oc)
                    xs = k.x[:, oc, bass.ds(b * TB, TB)]
                    dve.scalar_tensor_tensor(xs, k.ps[:, grp.bank(DOWN + oc), :], s_down[:, oc:oc + 1], xs,
                                             ALU.mult, ALU.add).then_inc(k.emptied_v.sem, 1)
    grp.close()
    split.close()
    k.v_chain.base += NB * per_block


def layer2(core):
    nc, k, io = core.nc, core, core.io
    with ExitStack() as ctx:
        def sb(name, shape, dt=F32):
            return ctx.enter_context(nc.sbuf_tensor(name, shape, dt))

        rows = sb("rows", [P, TT, D])
        logits = sb("logits", [P, TT, EXPERTS])
        slot_in, slot_out = sb("slot_in", [P, TOPK, TT], I32), sb("slot_out", [P, TOPK, TT], I32)
        share = sb("share", [P, TOPK, TT])
        with ExitStack() as inner:
            layer2_blocks(core, inner, rows, logits)
        with ExitStack() as inner:
            route(core, inner, logits, slot_in, slot_out, share)
        with ExitStack() as inner:
            experts(core, inner, rows, slot_in, slot_out, share)


def layer2_blocks(core, ctx, rows, logits):
    nc, k, io = core.nc, core, core.io

    def sb(name, shape, dt=F32):
        return ctx.enter_context(nc.sbuf_tensor(name, shape, dt))

    HS = JS * P
    wr, br = sb("wr", [P, C, EXPERTS]), sb("br", [P, EXPERTS])
    wv, wo = sb("wv2", [P, C, D]), sb("wo2", [P, C, D])
    s_gate, s_up, s_down = sb("s_gate", [P, C, HS]), sb("s_up", [P, C, HS]), sb("s_down2", [P, JS, D])
    norm = Norm(core, ctx, 2)
    value = sb("value2", [P, C, TB])
    h, sg = sb("h2", [P, JS, TB]), sb("sg2", [P, 2, TB])

    grp = Groups(core, "v" + "a" * TPB + "a" * C + "av" * JS + "v" * C)
    R, ROWS, V = 0, 1, 1 + TPB
    FFN = V + C
    OUT = FFN + 2 * JS
    with nc.Block() as block:
        @block.sync
        def _(sp):
            load(sp, core, [(wr[:, :, :], io["L2_wr"]), (br[:, :], io["L2_br"].partition_broadcast(P)),
                            (wv[:, :, :], io["L2_wv"]), (s_gate[:, :, :], io["L2_sg"]), (s_up[:, :, :], io["L2_su"]),
                            (wo[:, :, :], io["L2_wo"]), (s_down[:, :, :], io["L2_sd"])])

        @block.tensor
        def _(pe):
            pe.wait_ge(k.loaded.sem, k.loaded.base)
            with pe.Fori(0, NB) as b:
                grp.wait_block(pe, b)
                norm.tensor(pe, b)
                for t in range(TPB):
                    m = project(pe, k.ps[:, grp.bank(R), t * EXPERTS:(t + 1) * EXPERTS],
                                lambda c: norm.xn[:, c, t * P:(t + 1) * P], lambda c: wr[:, c, :])
                m.then_inc(k.filled.sem, 1)
                for t in range(TPB):
                    for c in range(C):
                        m = pe.transpose(k.ps[:, grp.bank(ROWS + t), c * P:(c + 1) * P],
                                         norm.xn[:, c, t * P:(t + 1) * P], k.ident[:, :])
                    m.then_inc(k.filled.sem, 1)
                for oc in range(C):
                    grp.wait_free(pe, b, V + oc)
                    project(pe, k.ps[:, grp.bank(V + oc), :], lambda c: wv[:, c, oc * P:(oc + 1) * P],
                            lambda c: norm.xn[:, c, :]).then_inc(k.filled.sem, 1)
                for j in range(JS):
                    for u, w in enumerate((s_gate, s_up)):
                        g = FFN + 2 * j + u
                        grp.wait_free(pe, b, g)
                        project(pe, k.ps[:, grp.bank(g), :], lambda c: w[:, c, j * P:(j + 1) * P],
                                lambda c: norm.xn[:, c, :]).then_inc(k.filled.sem, 1)
                grp.wait_emptied(pe, b, OUT - 1)
                for oc in range(C):
                    grp.wait_free(pe, b, OUT + oc)
                    for j in range(C + JS):
                        w, y = (wo, value) if j < C else (s_down, h)
                        c = j if j < C else j - C
                        m = pe.matmul(k.ps[:, grp.bank(OUT + oc), :], w[:, c, oc * P:(oc + 1) * P], y[:, c, :],
                                      start=j == 0, stop=j == C + JS - 1)
                    m.then_inc(k.filled.sem, 1)

        @block.scalar
        def _(act):
            with act.Fori(0, NB) as b:
                norm.scalar(act, b)
                for t in range(TPB):
                    grp.wait_filled(act, b, ROWS + t)
                    act.activation(rows[:, bass.ds(b * TPB + t, 1), :], k.ps[:, grp.bank(ROWS + t), :].unsqueeze(1), ACT.Copy)\
                       .then_inc(k.emptied_a.sem, 1)
                for oc in range(C):
                    grp.wait_filled(act, b, V + oc)
                    act.activation(value[:, oc, :], k.ps[:, grp.bank(V + oc), :], ACT.Copy)\
                       .then_inc(k.emptied_a.sem, 1)
                for j in range(JS):
                    g = FFN + 2 * j
                    if j >= 2:
                        grp.wait_emptied(act, b, g - 3)
                    grp.wait_filled(act, b, g)
                    act.activation(sg[:, j % 2, :], k.ps[:, grp.bank(g), :], ACT.Silu).then_inc(k.emptied_a.sem, 1)

        @block.vector
        def _(dve):
            dve.wait_ge(k.loaded.sem, k.loaded.base)
            with dve.Fori(0, NB) as b:
                norm.vector(dve, b)
                grp.wait_filled(dve, b, R)
                dve.tensor_tensor(logits[:, bass.ds(b * TPB, TPB), :],
                                  k.ps[:, grp.bank(R), 0:TPB * EXPERTS].rearrange("p (t e) -> p t e", t=TPB),
                                  br[:, :].unsqueeze(1).to_broadcast([P, TPB, EXPERTS]), ALU.add)\
                   .then_inc(k.emptied_v.sem, 1)
                for j in range(JS):
                    g = FFN + 2 * j
                    grp.wait_emptied(dve, b, g)
                    grp.wait_filled(dve, b, g + 1)
                    dve.tensor_tensor(h[:, j, :], k.ps[:, grp.bank(g + 1), :], sg[:, j % 2, :], ALU.mult)\
                       .then_inc(k.emptied_v.sem, 1)
                for oc in range(C):
                    grp.wait_filled(dve, b, OUT + oc)
                    xs = k.x[:, oc, bass.ds(b * TB, TB)]
                    dve.tensor_tensor(xs, xs, k.ps[:, grp.bank(OUT + oc), :], ALU.add).then_inc(k.emptied_v.sem, 1)
    grp.close()


def route(core, ctx, logits, slot_in, slot_out, share):
    nc, k, io = core.nc, core, core.io

    def sb(name, shape, dt=F32):
        return ctx.enter_context(nc.sbuf_tensor(name, shape, dt))

    E, PAD = EXPERTS, 8
    TAKEN, NONE = -7.0, -5.0
    row = sb("row", [P, 4, TT])
    expd = sb("expd", [P, TT, E])
    score = sb("score", [P, TT, E + PAD])
    left = sb("left", [P, TT, E + PAD])
    best, taken = sb("best", [P, TT, 8]), sb("taken", [P, TT, 8])
    picked = sb("picked_e", [P, TT, E])
    before = sb("before", [P, TT, E])
    place = sb("place", [P, TT, E])
    which, one, got = sb("which", [P, 1, E]), sb("one", [P, TT, E]), sb("got", [P, 4, TT])
    which_i = sb("which_i", [P, E], I32)
    earlier, ones = sb("earlier", [P, P]), sb("ones_p", [P, P])
    best_e = sb("best_e", [P, TT, 8], U32)
    best_f = sb("best_f", [P, TT, 8])
    made, expd_done, placed = Tally(nc, ctx, "route_made"), Tally(nc, ctx, "route_exp"), Tally(nc, ctx, "route_pe")
    shifted = Tally(nc, ctx, "route_shifted")
    chosen = Tally(nc, ctx, "route_chosen")
    chain = Chain(k.v_chain)

    with nc.Block() as block:
        @block.gpsimd
        def _(pool):
            pool.memset(earlier[:, :], 1.0).then_inc(made.sem, 1)
            pool.memset(ones[:, :], 1.0).then_inc(made.sem, 1)
            pool.iota(which_i[:, :], pattern=[[1, E]], base=0, channel_multiplier=0).then_inc(made.sem, 1)
            pool.wait_ge(made.sem, 3)
            pool.affine_select(out=earlier[:, :], in_=earlier[:, :], compare_op=ALU.is_gt, fill=0.0,
                               base=0, pattern=[[1, P]], channel_multiplier=-1).then_inc(made.sem, 1)

        @block.scalar
        def _(act):
            act.wait_ge(shifted.sem, 1)
            act.activation(expd[:, :, :], logits[:, :, :], ACT.Exp).then_inc(expd_done.sem, 1)

        @block.tensor
        def _(pe):
            pe.wait_ge(made.sem, 4)
            pe.wait_ge(chosen.sem, 1)
            for n in range(2):
                half = slice(n * TT // 2, (n + 1) * TT // 2)
                out = k.ps[:, n, :].rearrange("p (t e) -> p t e", e=E)
                pe.matmul(out, earlier[:, :], picked[:, half, :], start=True, stop=False)
                pe.matmul(out, ones[:, :], before[:, half, :], start=False, stop=True).then_inc(placed.sem, 1)

        @block.vector
        def _(dve):
            chain.start(dve)

            def wide(v, n=E):
                return v.unsqueeze(2).to_broadcast([P, TT, n])

            chain.mark(dve.memset(score[:, :, E:], NONE))
            chain.mark(dve.memset(taken[:, :, :], NONE))
            chain.link(dve.tensor_reduce(row[:, 0, :], logits[:, :, :], X_AXIS, ALU.max))
            dve.tensor_tensor(logits[:, :, :], logits[:, :, :], wide(row[:, 0, :]), ALU.subtract)\
               .then_inc(shifted.sem, 1)
            dve.wait_ge(expd_done.sem, 1)
            chain.link(dve.tensor_reduce(row[:, 1, :], expd[:, :, :], X_AXIS, ALU.add))
            chain.link(dve.reciprocal(row[:, 2, :], row[:, 1, :]))
            chain.link(dve.tensor_tensor(score[:, :, 0:E], expd[:, :, :], wide(row[:, 2, :]), ALU.mult))
            for t in range(TT):
                chain.mark(dve.max(best[:, t, :], score[:, t, 0:E]))
            dve.wait_ge(k.v_chain.sem, chain.at + chain.n)
            chain.link(dve.tensor_copy(taken[:, :, 0:TOPK], best[:, :, 0:TOPK]))
            for t in range(TT):
                chain.mark(dve.match_replace(left[:, t, :], taken[:, t, :], score[:, t, :], TAKEN))
                chain.mark(dve.max_index(best_e[:, t, :], best[:, t, :], score[:, t, 0:E]))
            dve.wait_ge(k.v_chain.sem, chain.at + chain.n)
            chain.link(dve.tensor_scalar(picked[:, :, :], left[:, :, 0:E], NONE - 1.0, None, ALU.is_lt))
            chain.link(dve.memset(before[:, 0, :], 0.0))
            for t in range(1, TT):
                chain.link(dve.tensor_tensor(before[:, t, :], before[:, t - 1, :], picked[:, t - 1, :], ALU.add))
            chain.link(dve.memset(got[:, :, :], 0.0))
            dve.tensor_copy(best_f[:, :, :], best_e[:, :, :]).then_inc(chosen.sem, 1)
            chain.link(dve.tensor_reduce(row[:, 3, :], best[:, :, 0:TOPK], X_AXIS, ALU.add))
            chain.link(dve.reciprocal(row[:, 3, :], row[:, 3, :]))
            dve.wait_ge(made.sem, 3)
            chain.link(dve.tensor_copy(which[:, 0, :], which_i[:, :]))
            dve.wait_ge(placed.sem, 2)
            for n in range(2):
                chain.mark(dve.tensor_copy(place[:, n * TT // 2:(n + 1) * TT // 2, :],
                                           k.ps[:, n, :].rearrange("p (t e) -> p t e", e=E)))
            dve.wait_ge(k.v_chain.sem, chain.at + chain.n)
            dve.wait_ge(chosen.sem, 1)
            for c in range(TOPK):
                e = best_f[:, :, c]
                chain.link(dve.tensor_tensor(one[:, :, :], wide(e), which[:, :, :].to_broadcast([P, TT, E]),
                                             ALU.is_equal))
                chain.link(dve.tensor_tensor(one[:, :, :], one[:, :, :], place[:, :, :], ALU.mult))
                chain.link(dve.tensor_reduce(got[:, 0, :], one[:, :, :], X_AXIS, ALU.add))
                chain.mark(dve.tensor_scalar(got[:, 1, :], got[:, 0, :], float(CAP), None, ALU.is_lt))
                chain.mark(dve.tensor_scalar(got[:, 2, :], got[:, 0, :], float(CAP - 1), None, ALU.min))
                chain.link(dve.tensor_scalar(got[:, 3, :], e, float(CAP), None, ALU.mult))
                chain.link(dve.tensor_tensor(got[:, 2, :], got[:, 2, :], got[:, 3, :], ALU.add))
                chain.mark(dve.tensor_copy(slot_out[:, c, :], got[:, 2, :]))
                chain.link(dve.tensor_scalar(got[:, 3, :], got[:, 1, :], -float(2 * SLOTS), float(2 * SLOTS),
                                             ALU.mult, ALU.add))
                chain.link(dve.tensor_tensor(got[:, 3, :], got[:, 3, :], got[:, 2, :], ALU.add))
                chain.mark(dve.tensor_copy(slot_in[:, c, :], got[:, 3, :]))
                chain.link(dve.tensor_tensor(share[:, c, :], best[:, :, c], row[:, 3, :], ALU.mult))
                chain.link(dve.tensor_tensor(share[:, c, :], share[:, c, :], got[:, 1, :], ALU.mult))
    k.v_chain.base += chain.n


def experts(core, ctx, rows, slot_in, slot_out, share):
    nc, k, io = core.nc, core, core.io

    def sb(name, shape, dt=F32):
        return ctx.enter_context(nc.sbuf_tensor(name, shape, dt))

    sent = Tally(nc, ctx, "sent")
    w = sb("w_exp", [P, 2, 3 * D])
    xe, xeT = sb("xe", [P, 2, D]), sb("xeT", [P, 2, C, P])
    ge, he, ye = sb("ge", [P, 2, P]), sb("he", [P, 2, P]), sb("ye", [P, 2, D])
    w_in = [Tally(nc, ctx, f"w_in{n}") for n in range(2)]
    y_out = [Tally(nc, ctx, f"y_out{n}", 1) for n in range(2)]
    xT_filled, xT_copied = Tally(nc, ctx, "xT_filled"), Tally(nc, ctx, "xT_copied")
    gu_filled, g_done, h_done = Tally(nc, ctx, "gu_filled"), Tally(nc, ctx, "g_done"), Tally(nc, ctx, "h_done")
    y_filled, y_copied = Tally(nc, ctx, "y_filled", 2), Tally(nc, ctx, "y_copied", 2)
    note = sb("note2", [1, 8])

    with nc.Block() as block:
        @block.gpsimd
        def _(pool):
            for n, tl in enumerate((*y_out, y_filled, y_copied)):
                pool.memset(note[:, n:n + 1], 0.0).then_inc(tl.sem, tl.base)
            for t in range(TT):
                for c in range(TOPK):
                    pool.indirect_dma_start(
                        out=io["slots_x"], out_offset=bass.IndirectOffsetOnAxis(ap=slot_in[:, c, t:t + 1], axis=0),
                        in_=rows[:, t, :], in_offset=None, bounds_check=SLOTS - 1, oob_is_err=False)\
                        .then_inc(sent.sem, 16)

        @block.sync
        def _(sp):
            sp.wait_ge(y_filled.sem, 2)
            with sp.Fori(0, EXPERTS // 2) as it:
                for p in range(2):
                    e = 2 * it + p
                    sp.wait_ge(y_filled.sem, e + 1)
                    sp.dma_start(w[:, p, :], io["L2_we"][bass.ds(e, 1), :, :].rearrange("a p n -> (a p) n"))\
                      .then_inc(w_in[p].sem, 16)
                    sp.wait_ge(sent.sem, 16 * TT * TOPK)
                    sp.dma_start(xe[:, p, :], io["slots_x"][bass.ds(e * CAP, CAP), :]).then_inc(w_in[p].sem, 16)

        @block.tensor
        def _(pe):
            with pe.Fori(0, EXPERTS // 2) as it:
                for p in range(2):
                    e = 2 * it + p
                    pe.wait_ge(w_in[p].sem, 32 * (it + 1))
                    pe.wait_ge(y_copied.sem, e + 1)
                    for c in range(C):
                        m = pe.transpose(k.ps[:, p, c * P:(c + 1) * P], xe[:, p, c * P:(c + 1) * P], k.ident[:, :])
                    m.then_inc(xT_filled.sem, 1)
                    pe.wait_ge(xT_copied.sem, e + 1)
                    for u in range(2):
                        m = project(pe, k.ps[:, 2 + 2 * u + p, 0:P],
                                    lambda c: w[:, p, u * D + c * P:u * D + (c + 1) * P], lambda c: xeT[:, p, c, :])
                        m.then_inc(gu_filled.sem, 1)
                    pe.wait_ge(h_done.sem, e + 1)
                    pe.matmul(k.ps[:, 6 + p, :], he[:, p, :], w[:, p, 2 * D:3 * D], start=True, stop=True)\
                      .then_inc(y_filled.sem, 1)

        @block.scalar
        def _(act):
            with act.Fori(0, EXPERTS // 2) as it:
                for p in range(2):
                    e = 2 * it + p
                    act.wait_ge(gu_filled.sem, 2 * e + 1)
                    act.activation(ge[:, p, :], k.ps[:, 2 + p, 0:P], ACT.Silu).then_inc(g_done.sem, 1)
                    act.wait_ge(y_filled.sem, e + 3)
                    act.wait_ge(y_out[p].sem, 16 * it + 1)
                    act.activation(ye[:, p, :], k.ps[:, 6 + p, :], ACT.Copy).then_inc(y_copied.sem, 1)
                    act.wait_ge(y_copied.sem, e + 3)
                    act.dma_start(io["slots_y"][bass.ds(e * CAP, CAP), :], ye[:, p, :]).then_inc(y_out[p].sem, 16)
            for p in range(2):
                act.wait_ge(y_out[p].sem, 16 * (EXPERTS // 2) + 1)

        @block.vector
        def _(dve):
            with dve.Fori(0, EXPERTS // 2) as it:
                for p in range(2):
                    e = 2 * it + p
                    dve.wait_ge(xT_filled.sem, e + 1)
                    dve.tensor_copy(xeT[:, p, :, :], k.ps[:, p, :].rearrange("p (c n) -> p c n", c=C))\
                       .then_inc(xT_copied.sem, 1)
                    dve.wait_ge(gu_filled.sem, 2 * e + 2)
                    dve.wait_ge(g_done.sem, e + 1)
                    dve.tensor_tensor(he[:, p, :], k.ps[:, 4 + p, 0:P], ge[:, p, :], ALU.mult).then_inc(h_done.sem, 1)

    res, acc = sb("res", [P, 2, TOPK, D]), sb("acc2", [P, 2, D])
    fetched = [Tally(nc, ctx, f"fetched{n}") for n in range(2)]
    summed, acc_turned, added = Tally(nc, ctx, "summed"), Tally(nc, ctx, "acc_turned"), Tally(nc, ctx, "added")
    with nc.Block() as block:
        def add_back(dve, t):
            dve.wait_ge(acc_turned.sem, t + 1)
            xs = k.x[:, :, t * P:(t + 1) * P]
            dve.tensor_tensor(xs, xs, k.ps[:, t % 2, :].rearrange("p (c n) -> p c n", c=C), ALU.add)\
               .then_inc(added.sem, 1)

        @block.gpsimd
        def _(pool):
            for t in range(TT):
                if t >= 2:
                    pool.wait_ge(summed.sem, 4 * (t - 1))
                for c in range(TOPK):
                    pool.indirect_dma_start(
                        out=res[:, t % 2, c, :], out_offset=None, in_=io["slots_y"],
                        in_offset=bass.IndirectOffsetOnAxis(ap=slot_out[:, c, t:t + 1], axis=0),
                        bounds_check=SLOTS - 1, oob_is_err=False).then_inc(fetched[t % 2].sem, 16)

        @block.vector
        def _(dve):
            for t in range(TT):
                dve.wait_ge(fetched[t % 2].sem, 16 * TOPK * (t // 2 + 1))
                if t >= 2:
                    dve.wait_ge(acc_turned.sem, t - 1)
                a = acc[:, t % 2, :]
                dve.tensor_scalar(a, res[:, t % 2, 0, :], share[:, 0, t:t + 1], None, ALU.mult).then_inc(summed.sem, 1)
                for c in range(1, TOPK):
                    dve.wait_ge(summed.sem, 4 * t + c)
                    dve.scalar_tensor_tensor(a, res[:, t % 2, c, :], share[:, c, t:t + 1], a, ALU.mult, ALU.add)\
                       .then_inc(summed.sem, 1)
                if t >= 1:
                    add_back(dve, t - 1)
            add_back(dve, TT - 1)

        @block.tensor
        def _(pe):
            for t in range(TT):
                pe.wait_ge(summed.sem, 4 * (t + 1))
                if t >= 2:
                    pe.wait_ge(added.sem, t - 1)
                for c in range(C):
                    m = pe.transpose(k.ps[:, t % 2, c * P:(c + 1) * P], acc[:, t % 2, c * P:(c + 1) * P],
                                     k.ident[:, :])
                m.then_inc(acc_turned.sem, 1)


def clear_slots(core):
    nc, k = core.nc, core
    with ExitStack() as ctx:
        zero = ctx.enter_context(nc.sbuf_tensor("zero", [P, D], F32))
        cleared, zeroed = Tally(nc, ctx, "cleared"), Tally(nc, ctx, "zeroed")
        with nc.Block() as block:
            @block.vector
            def _(dve):
                dve.memset(zero[:, :], 0.0).then_inc(zeroed.sem, 1)

            @block.sync
            def _(sp):
                sp.wait_ge(zeroed.sem, 1)
                for n in range(4):
                    sp.dma_start(k.io["slots_x"][n * SLOTS // 4:(n + 1) * SLOTS // 4, :]
                                 .rearrange("(p s) n -> p s n", p=P),
                                 zero[:, :].unsqueeze(1).to_broadcast([P, SLOTS // 4 // P, D]))\
                      .then_inc(cleared.sem, 16)
                sp.wait_ge(cleared.sem, 64)


def layer3(core):
    nc, k, io = core.nc, core, core.io
    with ExitStack() as ctx:
        def sb(name, shape, dt=F32):
            return ctx.enter_context(nc.sbuf_tensor(name, shape, dt))

        v_all = sb("v3_all", [P, TT, D])
        v_one = sb("v3_one", [P, TT, 32])
        with ExitStack() as inner:
            layer3_blocks(core, inner, v_all, v_one)
        attention(core, "3", 16, 32, io["q3_parts"], io["k3_parts"], v_all, io["o3"])
        attention(core, "4", 16, 32, io["q4_parts"], io["k4_parts"], v_one, io["o4"], shared=True)
        w_out, b_out = sb("w_out3", [P, C, D]), sb("b_out3", [P, C])
        project_out(core, ctx, "3", io["o3"], io["o4"], w_out, b_out,
                    [(w_out[:, :, :], io["L3_wo"]), (b_out[:, :], io["L3_bo"])], io["out"])


def layer3_blocks(core, ctx, v_all, v_one):
    nc, k, io = core.nc, core, core.io

    def sb(name, shape, dt=F32):
        return ctx.enter_context(nc.sbuf_tensor(name, shape, dt))

    HEADS, DH = 16, 32
    SCALE = float(1.0 / np.sqrt(np.float32(DH)))
    TAKEN, NONE = -7.0, -5.0
    wa, ba = sb("wa3", [P, 2, C, D]), sb("ba3", [P, 2, C])
    wv, bv = sb("wv3", [P, C, D]), sb("bv3", [P, D])
    wf, wg = sb("wf3", [P, 3, C, D]), sb("wg3", [P, C, HEADS])
    rot = sb("rot3", [P, P])
    norm = Norm(core, ctx, 3)
    split = Split(core, ctx, "3", 13)
    plain = sb("plain3", [P, 4, TB])
    turned_, mixed = sb("turned3", [P, TB]), sb("mixed3", [P, 2, TB])
    fq = sb("fq", [P, 2, TB])
    wave = sb("wave3", [P, 2, TB])
    gate, gexp = sb("gate3", [P, TPB, HEADS]), sb("gexp3", [P, TPB, HEADS])
    gsum, ginv = sb("gsum3", [P, TPB]), sb("ginv3", [P, TPB])
    prob, left = sb("gprob3", [P, TPB, HEADS + 8]), sb("gleft3", [P, TPB, HEADS + 8])
    best, taken = sb("gbest3", [P, TPB, 8]), sb("gtaken3", [P, TPB, 8])
    pick = sb("pick3", [P, 2, TPB, HEADS])
    prod = sb("prod3", [P, D])
    hop = sb("hop3", [P, 2])
    k_one, kT = sb("k_one3", [P, TPB, DH]), sb("kT3", [DH, TB])
    wave_in, mixed_ready, g_exp = Tally(nc, ctx, "wave_in3"), Tally(nc, ctx, "mixed_ready3"), Tally(nc, ctx, "g_exp3")
    k_ready = Tally(nc, ctx, "k_ready3")

    order = ["p0", "p1", "p2", "p3", "r0", "r1", "p4", "p5", "r2", "r3", "p6", "p7", "r4", "r5", "gate", "r6", "r7"]
    order += [f"{n}{t}" for t in range(TPB) for n in "kv"]
    order += [f"f{n}" for n in range(C)] + ["kT"] + [f"V{t}" for t in range(TPB)]
    at = {n: g for g, n in enumerate(order)}
    grp = Groups(core, "".join("a" if n[0] in "pf" or n == "kT" else "v" for n in order))
    chain = Chain(k.v_chain)
    per_block = 31

    with nc.Block() as block:
        def choose(dve, b):
            g = at["gate"]
            grp.wait_filled(dve, b, g)
            logits = k.ps[:, grp.bank(g), 0:TPB * HEADS].rearrange("p (t h) -> p t h", t=TPB)
            chain.link(dve.tensor_reduce(gsum[:, :], logits, X_AXIS, ALU.max))
            dve.tensor_tensor(gate[:, :, :], logits, gsum[:, :].unsqueeze(2).to_broadcast([P, TPB, HEADS]),
                              ALU.subtract).then_inc(k.emptied_v.sem, 1)
            dve.wait_ge(g_exp.sem, b + 1)
            chain.link(dve.tensor_reduce(gsum[:, :], gexp[:, :, :], X_AXIS, ALU.add))
            chain.link(dve.reciprocal(ginv[:, :], gsum[:, :]))
            chain.link(dve.tensor_tensor(prob[:, :, 0:HEADS], gexp[:, :, :],
                                         ginv[:, :].unsqueeze(2).to_broadcast([P, TPB, HEADS]), ALU.mult))
            dve.memset(hop[:, 0:1], 0.0)
            for t in range(TPB):
                chain.mark(dve.max(best[:, t, :], prob[:, t, 0:HEADS]))
            dve.wait_ge(k.v_chain.sem, chain.at + chain.n)
            chain.link(dve.tensor_copy(taken[:, :, 0:1], best[:, :, 0:1]))
            dve.memset(hop[:, 1:2], 0.0)
            for t in range(TPB):
                chain.mark(dve.match_replace(left[:, t, :], taken[:, t, :], prob[:, t, :], TAKEN))
            dve.wait_ge(k.v_chain.sem, chain.at + chain.n)
            chain.link(dve.tensor_scalar(pick[:, 0, :, :], left[:, :, 0:HEADS], NONE - 1.0, None, ALU.is_lt))
            chain.link(dve.tensor_tensor(pick[:, 1, :, :], pick[:, 0, :, :],
                                         best[:, :, 0:1].to_broadcast([P, TPB, HEADS]), ALU.mult))

        @block.sync
        def _(sp):
            load(sp, core, [(wa[:, :, :, :], io["L3_wqk"]), (ba[:, :, :], io["L3_bqk"]), (rot[:, :], io["L3_rot"]),
                            (wg[:, :, :], io["L3_wg"]), (wf[:, :, :, :], io["L3_wf"]), (wv[:, :, :], io["L3_wv"]),
                            (bv[:, :], io["L3_bv"].partition_broadcast(P))])
            with sp.Fori(0, NB) as b:
                for n in range(8):
                    dst = io["q3_parts"] if n % 2 == 0 else io["k3_parts"]
                    split.store(sp, b, n, dst[:, n // 2 * P:(n // 2 + 1) * P, :], after={0: 1, 1: None}.get(n, 0))
                for n in range(C):
                    split.store(sp, b, 8 + n, io["q4_parts"][:, n * P:(n + 1) * P, :])
                split.store(sp, b, 12, io["k4_parts"], DH)
            split.wait_stores(sp)

        @block.tensor
        def _(pe):
            pe.wait_ge(k.loaded.sem, k.loaded.base)
            with pe.Fori(0, NB) as b:
                grp.wait_block(pe, b)
                norm.tensor(pe, b)
                for g, name in enumerate(order):
                    grp.wait_free(pe, b, g)
                    out, n = k.ps[:, grp.bank(g), :], int(name[1]) if name[1].isdigit() else 0
                    tile = slice(n * P, (n + 1) * P)
                    if name[0] == "p":
                        oc = n // 2
                        m = project(pe, out, lambda c: wa[:, n % 2, c, oc * P:(oc + 1) * P],
                                    lambda c: norm.xn[:, c, :])
                    elif name[0] == "r":
                        grp.wait_emptied(pe, b, at[f"p{n}"])
                        m = pe.matmul(out, rot[:, :], plain[:, n % 4, :], start=True, stop=True)
                    elif name == "gate":
                        for t in range(TPB):
                            m = project(pe, k.ps[:, grp.bank(g), t * HEADS:(t + 1) * HEADS],
                                        lambda c: norm.xn[:, c, t * P:(t + 1) * P], lambda c: wg[:, c, :])
                    elif name == "kT":
                        pe.wait_ge(k_ready.sem, b + 1)
                        for t in range(TPB):
                            m = pe.transpose(k.ps[0:DH, grp.bank(g), t * P:(t + 1) * P], k_one[:, t, :], k.ident[:, :])
                    elif name[0] in "kv":
                        u = 1 + "kv".index(name[0])
                        m = project(pe, out, lambda c: norm.xn[:, c, tile], lambda c: wf[:, u, c, :])
                    elif name[0] == "f":
                        m = project(pe, out, lambda c: wf[:, 0, c, tile], lambda c: norm.xn[:, c, :])
                    else:
                        m = project(pe, out, lambda c: norm.xn[:, c, tile], lambda c: wv[:, c, :])
                    m.then_inc(k.filled.sem, 1)

        @block.scalar
        def _(act):
            with act.Fori(0, NB) as b:
                grp.wait_block(act, b)
                act.dma_start(wave[:, :, :], io["L3_wave"][:, :, bass.ds(b * TB, TB)]).then_inc(wave_in.sem, 16)
                norm.scalar(act, b)

                def take(n):
                    g = at[f"p{n}"]
                    if n >= 4:
                        grp.wait_emptied(act, b, at[f"r{n - 4}"])
                    grp.wait_filled(act, b, g)
                    act.activation(plain[:, n % 4, :], k.ps[:, grp.bank(g), :], ACT.Identity,
                                   bias=ba[:, n % 2, n // 2:n // 2 + 1]).then_inc(k.emptied_a.sem, 1)

                def parts(n):
                    act.wait_ge(mixed_ready.sem, 8 * b + n + 1)
                    split.scalar_1(act, b, n, mixed[:, n % 2, :], SCALE if n % 2 == 0 else 1.0)
                    split.scalar_2(act, b, n)

                for n in range(4):
                    take(n)
                for n in range(8):
                    parts(n)
                    if n % 2 == 1 and n < 4:
                        take(n + 3)
                        take(n + 4)
                    if n == 5:
                        grp.wait_emptied(act, b, at["gate"])
                        act.activation(gexp[:, :, :], gate[:, :, :], ACT.Exp).then_inc(g_exp.sem, 1)
                for n in range(C):
                    g = at[f"f{n}"]
                    grp.wait_filled(act, b, g)
                    act.activation(fq[:, n % 2, :], k.ps[:, grp.bank(g), :], ACT.Copy).then_inc(k.emptied_a.sem, 1)
                    grp.wait_emptied(act, b, g)
                    split.scalar_1(act, b, 8 + n, fq[:, n % 2, :], SCALE)
                    split.scalar_2(act, b, 8 + n)
                grp.wait_filled(act, b, at["kT"])
                act.activation(kT[:, :], k.ps[0:DH, grp.bank(at["kT"]), :], ACT.Copy).then_inc(k.emptied_a.sem, 1)
                grp.wait_emptied(act, b, at["kT"])
                split.scalar_1(act, b, 12, kT[:, :], 1.0, DH)
                split.scalar_2(act, b, 12, DH)

        @block.vector
        def _(dve):
            split.prime(dve)
            chain.start(dve)
            chain.link(dve.memset(prob[:, :, HEADS:], NONE))
            chain.link(dve.memset(taken[:, :, :], NONE))
            dve.wait_ge(k.loaded.sem, k.loaded.base)
            with dve.Fori(0, NB) as b:
                norm.vector(dve, b)
                chain.start(dve, 2 + b * per_block)
                dve.wait_ge(wave_in.sem, 16 * (b + 1))
                for n in range(8):
                    grp.wait_emptied(dve, b, at[f"p{n}"])
                    chain.mark(dve.tensor_tensor(mixed[:, n % 2, :], plain[:, n % 4, :], wave[:, 0, :], ALU.mult))
                    g = at[f"r{n}"]
                    grp.wait_filled(dve, b, g)
                    dve.tensor_tensor(turned_[:, :], k.ps[:, grp.bank(g), :], wave[:, 1, :], ALU.mult)\
                       .then_inc(k.emptied_v.sem, 1)
                    grp.wait_emptied(dve, b, g)
                    dve.wait_ge(k.v_chain.sem, chain.at + chain.n)
                    dve.tensor_tensor(mixed[:, n % 2, :], mixed[:, n % 2, :], turned_[:, :], ALU.add)\
                       .then_inc(mixed_ready.sem, 1)
                    split.vector_1(dve, b, n, mixed[:, n % 2, :], SCALE if n % 2 == 0 else 1.0)
                    split.vector_2(dve, b, n)
                    if n == 5:
                        choose(dve, b)
                for t in range(TPB):
                    for u, name in enumerate("kv"):
                        g = at[f"{name}{t}"]
                        grp.wait_filled(dve, b, g)
                        dve.tensor_tensor(prod[:, :].rearrange("p (h d) -> p h d", d=DH),
                                          k.ps[:, grp.bank(g), :].rearrange("p (h d) -> p h d", d=DH),
                                          pick[:, u, t, :].unsqueeze(2).to_broadcast([P, HEADS, DH]), ALU.mult)\
                           .then_inc(k.emptied_v.sem, 1)
                        grp.wait_emptied(dve, b, g)
                        dst = k_one[:, t:t + 1, :] if u == 0 else v_one[:, bass.ds(b * TPB + t, 1), :]
                        chain.link(dve.tensor_reduce(dst.rearrange("p a d -> p (a d)"),
                                                     prod[:, :].rearrange("p (h d) -> p d h", d=DH), X_AXIS, ALU.add))
                dve.memset(gsum[:, 0:1], 0.0).then_inc(k_ready.sem, 1)
                for n in range(C):
                    split.vector_1(dve, b, 8 + n, fq[:, n % 2, :], SCALE)
                    split.vector_2(dve, b, 8 + n)
                split.vector_1(dve, b, 12, kT[:, :], 1.0, DH)
                split.vector_2(dve, b, 12, DH)
                for t in range(TPB):
                    g = at[f"V{t}"]
                    grp.wait_filled(dve, b, g)
                    dve.tensor_tensor(v_all[:, bass.ds(b * TPB + t, 1), :].rearrange("p a d -> p (a d)"),
                                      k.ps[:, grp.bank(g), :], bv[:, :], ALU.add).then_inc(k.emptied_v.sem, 1)
                assert chain.n == per_block, chain.n
    grp.close()
    split.close()
    k.v_chain.base += 2 + NB * per_block


def program(nc, io, upto=4, start=0):
    def scratch(name, shape, dt=BF16):
        io[name] = nc.dram_tensor(name, shape, dt, kind="Internal").ap()

    scratch("q1_parts", (3, P, T))
    scratch("k1_parts", (3, P, T))
    scratch("slots_x", (SLOTS, D), F32)
    scratch("slots_y", (SLOTS, D), F32)
    for n in "34":
        scratch(f"q{n}_parts", (3, D, T))
        scratch(f"k{n}_parts", (3, D if n == "3" else 32, T))
        scratch("o" + n, (D, T), F32)
    scratch("o1", (P, T), F32)
    with ExitStack() as ctx:
        core = Core(nc, ctx, io)
        core.start = start
        setup(core)
        clear_slots(core)
        for n, layer in enumerate((layer0, layer1, layer2, layer3)):
            if start <= n < upto:
                layer(core)
        if upto < 4:
            dump(core)


def dump(core):
    nc, k = core.nc, core
    with nc.Block() as block:
        @block.sync
        def _(sp):
            sp.dma_start(k.io["out"].rearrange("(c p) t -> p c t", p=P), k.x[:, :, :]).then_inc(k.stored.sem, 16)
            sp.wait_ge(k.stored.sem, k.stored.base + 16)


def columns(v):
    return np.ascontiguousarray(v.reshape(-1, P).T)


def chunked(w):
    o, i = w.shape
    return np.ascontiguousarray(w.T.reshape(i // P, P, o).transpose(1, 0, 2))


def layout(inputs):
    a = {n: np.asarray(v) for n, v in inputs.items()}
    out = {"xT": np.ascontiguousarray(a["L0_attn_x"][0].T), "L0_ffn_lut": a["L0_ffn_lut"]}
    out["L0_w"] = np.stack([chunked(a["L0_attn_W" + n]) for n in "vkgq"], 1)
    out["L0_b"] = np.stack([columns(a["L0_attn_b" + n]) for n in "vkgq"], 1)
    idx = np.zeros((P, 24 * PIECE), np.int32)
    for n, name in enumerate(("gate", "up")):
        w = idx[:, n * C * H1:(n + 1) * C * H1].reshape(P, C, H1)
        w[:, :, :H0] = chunked(a[f"L0_ffn_{name}_idx"])
    w = idx[:, 2 * C * H1:2 * C * H1 + J0 * D].reshape(P, J0, D)
    down = np.zeros((J0 * P, D), np.int32)
    down[:H0] = a["L0_ffn_down_idx"].T
    w[:, :, :] = down.reshape(J0, P, D).transpose(1, 0, 2)
    out["L0_idx"] = idx.reshape(P, 24, PIECE)
    out["L1_w"] = np.stack([chunked(a[f"L1_attn_{n}_w"]) for n in ("CQR", "CKV", "CKR")], 1)
    out["L1_b"] = np.stack([a[f"L1_attn_{n}_b"] for n in ("CQR", "CKV", "CKR")], 1)
    out["L1_cv_w"], out["L1_cv_b"] = np.ascontiguousarray(a["L1_attn_CV_w"].T), a["L1_attn_CV_b"]
    out["L1_out_w"], out["L1_out_b"] = np.ascontiguousarray(a["L1_attn_OUT_w"].T), columns(a["L1_attn_OUT_b"])
    out["L1_wq"] = np.concatenate([chunked(a["L1_ffn_wq_" + n]).reshape(P, 4, H1) for n in ("gate", "up", "down")], 1)
    out["L1_s_hid"] = np.stack([columns(a["L1_ffn_s_gate"]), columns(a["L1_ffn_s_up"])], 1)
    out["L1_s_down"] = columns(a["L1_ffn_s_down"])
    out["L2_wr"], out["L2_br"] = chunked(a["L2_ffn_Wr"].T), a["L2_ffn_router_bias"]
    out["L2_wv"], out["L2_wo"] = chunked(a["L2_attn_weight_qkv"][2 * D:]), chunked(a["L2_attn_weight_out"])
    for n, name in (("L2_sg", "L2_ffn_Sg"), ("L2_su", "L2_ffn_Su")):
        out[n] = chunked(a[name].transpose(0, 2, 1).reshape(JS * P, D))
    out["L2_sd"] = chunked(a["L2_ffn_Sd"].reshape(JS * P, D).T)
    we = [a["L2_ffn_" + n].reshape(EXPERTS, C, P, HX).transpose(0, 2, 1, 3).reshape(EXPERTS, P, D)
          for n in ("Wg", "Wu")]
    out["L2_we"] = np.concatenate(we + [a["L2_ffn_Wd"]], 2)
    out["L3_wqk"] = np.stack([chunked(a["L3_attn_W" + n]) for n in "qk"], 1)
    out["L3_bqk"] = np.stack([columns(a["L3_attn_b" + n]) for n in "qk"], 1)
    out["L3_wv"], out["L3_bv"] = chunked(a["L3_attn_Wv"]), a["L3_attn_bv"]
    out["L3_wo"], out["L3_bo"] = chunked(a["L3_attn_Wo"]), columns(a["L3_attn_bo"])
    out["L3_wg"] = chunked(a["L3_ffn_W_gate"])
    out["L3_wf"] = np.stack([chunked(a["L3_ffn_W_qkv"][n * D:(n + 1) * D]) for n in range(3)], 1)
    freq = (1.0 / 10000.0 ** (np.arange(16, dtype=np.float32) / 16)).astype(np.float32)
    angle = np.tile(np.repeat(np.outer(np.arange(T, dtype=np.float32), freq), 2, 1), (1, 4)).T
    out["L3_wave"] = np.ascontiguousarray(np.stack([np.cos(angle), np.sin(angle)], 1).astype(np.float32))
    rot = np.zeros((P, P), np.float32)
    for f in range(0, P, 2):
        rot[f + 1, f], rot[f, f + 1] = -1.0, 1.0
    out["L3_rot"] = rot
    freq = (1.0 / 10000.0 ** (np.arange(0, P, 2, dtype=np.float32) / P)).astype(np.float32)
    angle = np.tile(np.outer(np.arange(T, dtype=np.float32), freq), (1, 2)).T
    out["L1_wave"] = np.ascontiguousarray(np.stack([np.cos(angle), np.sin(angle)], 1).astype(np.float32))
    rot = np.zeros((P, P), np.float32)
    for f in range(P // 2):
        rot[f + P // 2, f], rot[f, f + P // 2] = -1.0, 1.0
    out["L1_rot"] = rot
    return out


def kernel(**inputs):
    import concourse.bacc as bacc
    from concourse.bass_utils import run_bass_kernel_spmd

    nc = bacc.Bacc("TRN2", target_bir_lowering=False, num_devices=1)
    arrays = {f"in_{n}": v for n, v in layout(inputs).items()}
    io = {n[3:]: nc.dram_tensor(n, v.shape, mybir.dt.from_np(v.dtype), kind="ExternalInput").ap()
          for n, v in arrays.items()}
    io["out"] = nc.dram_tensor("out", (D, T), F32, kind="ExternalOutput").ap()
    program(nc, io)
    result = run_bass_kernel_spmd(nc, [arrays], core_ids=[0]).results[0]["out"]
    return np.ascontiguousarray(result.T)[None]
```

```python
import numpy as np
import concourse.bass as bass
from concourse import mybir
from contextlib import ExitStack

F32, BF16, F16 = mybir.dt.float32, mybir.dt.bfloat16, mybir.dt.float16
I32, U32 = mybir.dt.int32, mybir.dt.uint32
ALU = mybir.AluOpType
ACT = mybir.ActivationFunctionType
X_AXIS = mybir.AxisListType.X

P = 128
T = 2048
D = 512
C = D // P
TB = 512
NB = T // TB
TT = T // P
TPB = TB // P
H0 = 1376
H1 = 1408
J0 = -(-H0 // P)
J1 = H1 // P
LUT = 16
PIECE = 704
EXPERTS, TOPK, CAP = 64, 4, 128
HX = 128
JS = 8
SLOTS = EXPERTS * CAP
EPS = 1e-5
NEG = -3.0e38
BANKS = 8
SHIFT = float(10 * np.log(2))


class Tally:

    def __init__(self, nc, ctx, name, base=0):
        self.sem = ctx.enter_context(nc.semaphore(name))
        self.base = base


class Chain:

    def __init__(self, tally):
        self.tally, self.engine, self.n = tally, None, 0

    def start(self, engine, passed=0):
        self.engine, self.at, self.n = engine, self.tally.base + passed, 0

    def link(self, ins):
        ins.then_inc(self.tally.sem, 1)
        self.n += 1
        self.engine.wait_ge(self.tally.sem, self.at + self.n)

    def mark(self, ins):
        ins.then_inc(self.tally.sem, 1)
        self.n += 1


class Groups:

    def __init__(self, core, kinds, blocks=NB):
        self.kinds, self.core, self.blocks = kinds, core, blocks
        self.total = {e: kinds.count(e) for e in "av"}
        self.filled0 = core.filled.base
        self.base = {"a": core.emptied_a.base, "v": core.emptied_v.base}

    def bank(self, g):
        return (g + 2) % BANKS

    def wait_free(self, pe, b, g):
        if g >= BANKS:
            self.wait_emptied(pe, b, g - BANKS)

    def wait_emptied(self, eng, b, g):
        e = self.kinds[g]
        tally = self.core.emptied_a if e == "a" else self.core.emptied_v
        eng.wait_ge(tally.sem, self.base[e] + b * self.total[e] + self.kinds[:g + 1].count(e))

    def wait_filled(self, eng, b, g):
        eng.wait_ge(self.core.filled.sem, self.filled0 + b * len(self.kinds) + g + 1)

    def wait_block(self, eng, b):
        eng.wait_ge(self.core.emptied_v.sem, self.base["v"] + b * self.total["v"])

    def close(self):
        self.core.filled.base += self.blocks * len(self.kinds)
        self.core.emptied_a.base += self.blocks * self.total["a"]
        self.core.emptied_v.base += self.blocks * self.total["v"]


class Core:

    def __init__(self, nc, ctx, io):
        self.nc, self.io = nc, io

        def sb(name, shape, dt=F32):
            return ctx.enter_context(nc.sbuf_tensor(name, shape, dt))

        self.x = sb("x", [P, C, T])
        self.ident = sb("ident", [P, P])
        self.ident_b = sb("ident_b", [P, P], BF16)
        self.mask_b, self.maskT_b = sb("mask_b", [P, P], BF16), sb("maskT_b", [P, P], BF16)
        self.mean_w = sb("mean_w", [P, P])
        self.ones = sb("ones", [P, TB])
        self.eps = sb("eps", [P, 1])
        self.ps = ctx.enter_context(nc.psum_tensor("ps", [P, BANKS, 512], F32))

        def tally(name, base=0):
            return Tally(nc, ctx, name, base)

        self.loaded = tally("loaded")
        self.stored = tally("stored", 1)
        self.const = tally("const")
        self.filled = tally("filled")
        self.emptied_a = tally("emptied_a", 1)
        self.emptied_v = tally("emptied_v", 1)
        self.v_chain, self.a_chain = tally("v_chain"), tally("a_chain")
        self.ln_mean, self.ln_centred, self.ln_squared = tally("ln_mean"), tally("ln_centred"), tally("ln_squared")
        self.ln_var, self.ln_std, self.ln_rstd, self.xn_ready = (
            tally("ln_var"), tally("ln_std"), tally("ln_rstd"), tally("xn_ready"))
        self.split_a, self.split_v = tally("split_a"), tally("split_v")


class Norm:

    def __init__(self, core, ctx, layer):
        self.core, self.layer = core, layer
        nc = core.nc

        def sb(name, shape):
            return ctx.enter_context(nc.sbuf_tensor(f"{name}{layer}", shape, F32))

        self.xc = sb("xc", [P, C, TB])
        self.sq = sb("sq", [P, C, TB])
        self.std = sb("std", [P, TB])
        self.rstd = sb("rstd", [P, TB])
        self.xn = sb("xn", [P, C, TB])

    def count(self, b):
        return NB * (self.layer - self.core.start) + b + 1

    def tensor(self, pe, b):
        k = self.core
        for c in range(C):
            m = pe.matmul(k.ps[:, 0, :], k.mean_w[:, :], k.x[:, c, bass.ds(b * TB, TB)],
                          start=c == 0, stop=c == C - 1)
        m.then_inc(k.ln_mean.sem, 1)
        pe.wait_ge(k.ln_squared.sem, self.count(b))
        for c in range(C):
            m = pe.matmul(k.ps[:, 1, :], k.mean_w[:, :], self.sq[:, c, :], start=c == 0, stop=c == C - 1)
        m.then_inc(k.ln_var.sem, 1)
        pe.wait_ge(k.xn_ready.sem, self.count(b))

    def scalar(self, act, b):
        k = self.core
        act.wait_ge(k.ln_centred.sem, self.count(b))
        act.activation(self.sq[:, :, :], self.xc[:, :, :], ACT.Square).then_inc(k.ln_squared.sem, 1)
        act.wait_ge(k.ln_var.sem, self.count(b))
        act.activation(self.std[:, :], k.ps[:, 1, :], ACT.Sqrt, bias=k.eps[:, 0:1]).then_inc(k.ln_std.sem, 1)

    def vector(self, dve, b):
        k = self.core
        dve.wait_ge(k.ln_mean.sem, self.count(b))
        dve.tensor_tensor(self.xc[:, :, :], k.x[:, :, bass.ds(b * TB, TB)],
                          k.ps[:, 0, :].unsqueeze(1).to_broadcast([P, C, TB]), ALU.subtract)\
           .then_inc(k.ln_centred.sem, 1)
        dve.wait_ge(k.ln_std.sem, self.count(b))
        dve.reciprocal(self.rstd[:, :], self.std[:, :]).then_inc(k.ln_rstd.sem, 1)
        dve.wait_ge(k.ln_rstd.sem, self.count(b))
        dve.wait_ge(k.ln_centred.sem, self.count(b))
        dve.tensor_tensor(self.xn[:, :, :], self.xc[:, :, :],
                          self.rstd[:, :].unsqueeze(1).to_broadcast([P, C, TB]), ALU.mult)\
           .then_inc(k.xn_ready.sem, 1)


def project(pe, out, weights, moving, chunks=C):
    for c in range(chunks):
        m = pe.matmul(out, weights(c), moving(c), start=c == 0, stop=c == chunks - 1)
    return m


def setup(core):
    nc, k = core.nc, core
    with nc.Block() as block:
        @block.sync
        def _(sp):
            for b in range(NB):
                sp.dma_start(k.x[:, :, b * TB:(b + 1) * TB],
                             k.io["xT"].rearrange("(c p) t -> p c t", p=P)[:, :, b * TB:(b + 1) * TB])\
                  .then_inc(k.loaded.sem, 16)
            sp.wait_ge(k.loaded.sem, 16 * NB)

        @block.vector
        def _(dve):
            dve.memset(k.mean_w[:, :], 1.0 / D).then_inc(k.emptied_v.sem, 1)
            dve.memset(k.ones[:, :], 1.0).then_inc(k.emptied_a.sem, 1)
            dve.memset(k.eps[:, :], EPS).then_inc(k.stored.sem, 1)
            dve.wait_ge(k.const.sem, 6)
            dve.tensor_copy(k.ident_b[:, :], k.ident[:, :]).then_inc(k.const.sem, 1)

        @block.gpsimd
        def _(pool):
            pool.memset(k.ident[:, :], 0.0).then_inc(k.const.sem, 1)
            pool.memset(k.mask_b[:, :], 0.0).then_inc(k.const.sem, 1)
            pool.memset(k.maskT_b[:, :], 0.0).then_inc(k.const.sem, 1)
            pool.wait_ge(k.const.sem, 3)
            pool.affine_select(out=k.ident[:, :], in_=k.ident[:, :], compare_op=ALU.not_equal, fill=1.0,
                               base=0, pattern=[[-1, P]], channel_multiplier=1).then_inc(k.const.sem, 1)
            pool.affine_select(out=k.mask_b[:, :], in_=k.mask_b[:, :], compare_op=ALU.is_ge, fill=NEG,
                               base=0, pattern=[[-1, P]], channel_multiplier=1).then_inc(k.const.sem, 1)
            pool.affine_select(out=k.maskT_b[:, :], in_=k.maskT_b[:, :], compare_op=ALU.is_ge, fill=NEG,
                               base=0, pattern=[[1, P]], channel_multiplier=-1).then_inc(k.const.sem, 1)
    k.loaded.base += 16 * NB


def load(eng, core, pairs):
    for dst, src in pairs:
        eng.dma_start(dst, src).then_inc(core.loaded.sem, 16)
    core.loaded.base += 16 * len(pairs)


def layer0(core):
    nc, k, io = core.nc, core, core.io
    with ExitStack() as ctx:
        def sb(name, shape, dt=F32):
            return ctx.enter_context(nc.sbuf_tensor(name, shape, dt))

        wa = sb("wa", [P, 4, C, D])
        ba = sb("ba", [P, 4, C])
        wf = sb("wf", [P, 24 * PIECE])
        w_gate = wf[:, 0:C * H1].rearrange("p (c n) -> p c n", c=C)
        w_up = wf[:, C * H1:2 * C * H1].rearrange("p (c n) -> p c n", c=C)
        w_down = wf[:, 2 * C * H1:2 * C * H1 + J0 * D].rearrange("p (j n) -> p j n", j=J0)
        loads = [(wa[:, :, :, :], io["L0_w"]), (ba[:, :, :], io["L0_b"])]

        look_up(core, wf, loads)

        norm = Norm(core, ctx, 0)
        carry = sb("carry", [P, C])
        v_sb, g_sb = sb("v_sb", [P, 2, TB]), sb("g_sb", [P, 2, TB])
        kv, kvs, qg = sb("kv", [P, TB]), sb("kvs", [P, TB]), sb("qg", [P, TB])
        h = sb("h", [P, J0, TB])
        sg = sb("sg", [P, 2, TB])

        grp = Groups(core, "avav" * C + "av" * J0 + "v" * C)
        ffn, down = 4 * C, 4 * C + 2 * J0
        per_block = 4 * C
        chain = Chain(k.v_chain)

        with nc.Block() as block:
            @block.tensor
            def _(pe):
                with pe.Fori(0, NB) as b:
                    grp.wait_block(pe, b)
                    norm.tensor(pe, b)
                    for g in range(4 * C):
                        grp.wait_free(pe, b, g)
                        oc, which = g // 4, g % 4
                        project(pe, k.ps[:, grp.bank(g), :], lambda c: wa[:, which, c, oc * P:(oc + 1) * P],
                                lambda c: norm.xn[:, c, :]).then_inc(k.filled.sem, 1)
                    for j in range(J0):
                        rows = min(P, H0 - j * P)
                        for u, w in enumerate((w_gate, w_up)):
                            g = ffn + 2 * j + u
                            grp.wait_free(pe, b, g)
                            project(pe, k.ps[0:rows, grp.bank(g), :], lambda c: w[:, c, j * P:j * P + rows],
                                    lambda c: norm.xn[:, c, :]).then_inc(k.filled.sem, 1)
                    grp.wait_emptied(pe, b, down - 1)
                    for oc in range(C):
                        grp.wait_free(pe, b, down + oc)
                        for j in range(J0):
                            rows = min(P, H0 - j * P)
                            m = pe.matmul(k.ps[:, grp.bank(down + oc), :], w_down[0:rows, j, oc * P:(oc + 1) * P],
                                          h[0:rows, j, :], start=j == 0, stop=j == J0 - 1)
                        m.then_inc(k.filled.sem, 1)

            @block.scalar
            def _(act):
                with act.Fori(0, NB) as b:
                    norm.scalar(act, b)
                    for oc in range(C):
                        if oc >= 2:
                            grp.wait_emptied(act, b, 4 * (oc - 2) + 3)
                        else:
                            grp.wait_block(act, b)
                        grp.wait_filled(act, b, 4 * oc)
                        act.activation(v_sb[:, oc % 2, :], k.ps[:, grp.bank(4 * oc), :], ACT.Identity,
                                       bias=ba[:, 0, oc:oc + 1]).then_inc(k.emptied_a.sem, 1)
                        grp.wait_filled(act, b, 4 * oc + 2)
                        act.activation(g_sb[:, oc % 2, :], k.ps[:, grp.bank(4 * oc + 2), :], ACT.Sigmoid,
                                       bias=ba[:, 2, oc:oc + 1]).then_inc(k.emptied_a.sem, 1)
                    for j in range(J0):
                        rows = min(P, H0 - j * P)
                        g = ffn + 2 * j
                        if j >= 2:
                            grp.wait_emptied(act, b, g - 3)
                        grp.wait_filled(act, b, g)
                        act.activation(sg[0:rows, j % 2, :], k.ps[0:rows, grp.bank(g), :], ACT.Silu)\
                           .then_inc(k.emptied_a.sem, 1)

            @block.vector
            def _(dve):
                chain.start(dve)
                chain.link(dve.memset(carry[:, :], 0.0))
                with dve.Fori(0, NB) as b:
                    norm.vector(dve, b)
                    chain.start(dve, 1 + b * per_block)
                    for oc in range(C):
                        grp.wait_filled(dve, b, 4 * oc + 1)
                        grp.wait_emptied(dve, b, 4 * oc)
                        dve.scalar_tensor_tensor(kv[:, :], k.ps[:, grp.bank(4 * oc + 1), :], ba[:, 1, oc:oc + 1],
                                                 v_sb[:, oc % 2, :], ALU.add, ALU.mult).then_inc(k.emptied_v.sem, 1)
                        grp.wait_emptied(dve, b, 4 * oc + 1)
                        chain.link(dve.tensor_tensor_scan(kvs[:, :], k.ones[:, :], kv[:, :], carry[:, oc:oc + 1],
                                                          ALU.mult, ALU.add))
                        chain.mark(dve.tensor_copy(carry[:, oc:oc + 1], kvs[:, TB - 1:TB]))
                        grp.wait_filled(dve, b, 4 * oc + 3)
                        grp.wait_emptied(dve, b, 4 * oc + 2)
                        dve.scalar_tensor_tensor(qg[:, :], k.ps[:, grp.bank(4 * oc + 3), :], ba[:, 3, oc:oc + 1],
                                                 g_sb[:, oc % 2, :], ALU.add, ALU.mult).then_inc(k.emptied_v.sem, 1)
                        grp.wait_emptied(dve, b, 4 * oc + 3)
                        chain.link(dve.tensor_tensor(qg[:, :], qg[:, :], kvs[:, :], ALU.mult))
                        xs = k.x[:, oc, bass.ds(b * TB, TB)]
                        chain.link(dve.tensor_tensor(xs, xs, qg[:, :], ALU.add))
                    for j in range(J0):
                        rows = min(P, H0 - j * P)
                        g = ffn + 2 * j
                        grp.wait_emptied(dve, b, g)
                        grp.wait_filled(dve, b, g + 1)
                        dve.tensor_tensor(h[0:rows, j, :], k.ps[0:rows, grp.bank(g + 1), :], sg[0:rows, j % 2, :],
                                          ALU.mult).then_inc(k.emptied_v.sem, 1)
                    for oc in range(C):
                        grp.wait_filled(dve, b, down + oc)
                        xs = k.x[:, oc, bass.ds(b * TB, TB)]
                        dve.tensor_tensor(xs, xs, k.ps[:, grp.bank(down + oc), :], ALU.add)\
                           .then_inc(k.emptied_v.sem, 1)
                    assert chain.n == per_block
        grp.close()
        k.v_chain.base += 1 + NB * per_block


def look_up(core, wf, loads):
    nc, k, io = core.nc, core, core.io
    pieces = 24
    with ExitStack() as ctx:
        def sb(name, shape, dt=F32):
            return ctx.enter_context(nc.sbuf_tensor(name, shape, dt))

        table, step = sb("table", [P, LUT]), sb("step", [P, LUT // 2])
        idx = sb("idx", [P, 2, PIECE], I32)
        bit0 = sb("bit0", [P, 2, PIECE], I32)
        bits = sb("bits", [P, 2, 3, PIECE], I32)
        cand = sb("cand", [P, 8, PIECE])

        hop = sb("hop", [P, 1])
        idx_in = [Tally(nc, ctx, f"idx_in{p}") for p in range(2)]
        idx_used, bit0_ready, cand_ready, picked, kept = (
            Tally(nc, ctx, n) for n in ("idx_used", "bit0_ready", "cand_ready", "picked", "kept"))
        with nc.Block() as block:
            @block.sync
            def _(sp):
                sp.dma_start(table[:, :], io["L0_ffn_lut"].partition_broadcast(P)).then_inc(k.loaded.sem, 16)
                for p in range(2):
                    sp.dma_start(idx[:, p, :], io["L0_idx"][:, p, :]).then_inc(idx_in[p].sem, 16)
                with sp.Fori(0, pieces // 2 - 1) as i:
                    for p in range(2):
                        sp.wait_ge(idx_used.sem, 2 * i + p + 1)
                        sp.dma_start(idx[:, p, :], io["L0_idx"][:, bass.ds(2 * i + p + 2, 1), :]
                                     .rearrange("p a n -> p (a n)")).then_inc(idx_in[p].sem, 16)
                for dst, src in loads:
                    sp.dma_start(dst, src).then_inc(k.loaded.sem, 16)
                sp.wait_ge(k.loaded.sem, k.loaded.base + 16 + 16 * len(loads))

            @block.vector
            def _(dve):
                dve.wait_ge(k.loaded.sem, k.loaded.base + 16)
                pairs = table[:, :].rearrange("p (n two) -> p n two", two=2)
                dve.tensor_tensor(step[:, :], pairs[:, :, 1], pairs[:, :, 0], ALU.subtract).then_inc(k.v_chain.sem, 1)
                with dve.Fori(0, pieces // 2) as i:
                    for p in range(2):
                        n = 2 * i + p
                        dve.wait_ge(idx_in[p].sem, 16 * (i + 1))
                        dve.tensor_scalar(bit0[:, p, :], idx[:, p, :], 1, None, ALU.bitwise_and)\
                           .then_inc(bit0_ready.sem, 1)
                        for q in range(3):
                            m = dve.tensor_scalar(bits[:, p, q, :], idx[:, p, :], 2 << q, None, ALU.bitwise_and)
                        m.then_inc(idx_used.sem, 1)
                        dve.wait_ge(idx_used.sem, n + 1)
                        dve.wait_ge(cand_ready.sem, n + 1)
                        dve.memset(hop[:, :], 0.0).then_inc(picked.sem, 1)
                        for q, n_out in enumerate((4, 2, 1)):
                            stride = 2 << q
                            out = cand[:, 0::stride, :]
                            dve.wait_ge(picked.sem, 4 * n + 1 + q)
                            dve.memset(hop[:, :], 0.0)
                            dve.copy_predicated(out, bits[:, p, q, :].unsqueeze(1).to_broadcast([P, n_out, PIECE]),
                                                cand[:, stride // 2::stride, :]).then_inc(picked.sem, 1)

            @block.scalar
            def _(act):
                act.wait_ge(k.v_chain.sem, k.v_chain.base + 1)
                with act.Fori(0, pieces // 2) as i:
                    for p in range(2):
                        n = 2 * i + p
                        act.wait_ge(bit0_ready.sem, n + 1)
                        for q in range(8):
                            m = act.activation(cand[:, q, :], bit0[:, p, :], ACT.Identity,
                                               bias=table[:, 2 * q:2 * q + 1], scale=step[:, q:q + 1])
                        m.then_inc(cand_ready.sem, 1)
                        act.wait_ge(picked.sem, 4 * n + 4)
                        act.activation(wf[:, bass.ds(n * PIECE, PIECE)], cand[:, 0, :], ACT.Copy)\
                           .then_inc(kept.sem, 1)
                        act.wait_ge(kept.sem, n + 1)
        k.loaded.base += 16 + 16 * len(loads)
        k.v_chain.base += 1


class Split:

    def __init__(self, core, ctx, name, items):
        self.core, self.items = core, items
        nc = core.nc
        self.parts = ctx.enter_context(nc.sbuf_tensor("parts" + name, [P, 2, 3, TB], BF16))
        self.rest = ctx.enter_context(nc.sbuf_tensor("rest" + name, [P, 2, TB], F32))
        self.stored = [Tally(nc, ctx, f"parts_stored{name}{n}") for n in range(2)]
        self.a0, self.v0 = core.split_a.base, core.split_v.base
        self.per_buffer = [(items + 1) // 2, items // 2]

    def step(self, b, i):
        return b * (2 * self.items) + 2 * i

    def prime(self, dve):
        for n in range(2):
            dve.memset(self.rest[:, n, 0:1], 0.0).then_inc(self.stored[n].sem, 1)

    def wait_free(self, act, b, i):
        act.wait_ge(self.stored[i % 2].sem, 16 * (b * self.per_buffer[i % 2] + i // 2) + 1)

    def scalar_1(self, act, b, i, src, scale, rows=P):
        self.wait_free(act, b, i)
        act.activation(self.parts[0:rows, i % 2, 0, :], src, ACT.Copy, scale=scale)\
           .then_inc(self.core.split_a.sem, 1)

    def vector_1(self, dve, b, i, src, scale, rows=P):
        dve.wait_ge(self.core.split_a.sem, self.a0 + self.step(b, i) + 1)
        dve.scalar_tensor_tensor(self.rest[0:rows, i % 2, :], src, scale, self.parts[0:rows, i % 2, 0, :],
                                 ALU.mult, ALU.subtract).then_inc(self.core.split_v.sem, 1)

    def scalar_2(self, act, b, i, rows=P):
        act.wait_ge(self.core.split_v.sem, self.v0 + self.step(b, i) + 1)
        act.activation(self.parts[0:rows, i % 2, 1, :], self.rest[0:rows, i % 2, :], ACT.Copy)\
           .then_inc(self.core.split_a.sem, 1)

    def vector_2(self, dve, b, i, rows=P):
        dve.wait_ge(self.core.split_a.sem, self.a0 + self.step(b, i) + 2)
        dve.tensor_tensor(self.parts[0:rows, i % 2, 2, :], self.rest[0:rows, i % 2, :],
                          self.parts[0:rows, i % 2, 1, :], ALU.subtract).then_inc(self.core.split_v.sem, 1)

    def store(self, sp, b, i, dst, rows=P, after=0):
        if after is not None:
            sp.wait_ge(self.core.split_v.sem, self.v0 + self.step(b, i + after) + 2)
        sp.dma_start(dst[:, :, bass.ds(b * TB, TB)].rearrange("a r t -> r a t"),
                     self.parts[0:rows, i % 2, :, :]).then_inc(self.stored[i % 2].sem, 16)

    def wait_done(self, act, b, i):
        act.wait_ge(self.core.split_v.sem, self.v0 + self.step(b, i) + 1)

    def wait_stores(self, sp):
        for n in range(2):
            sp.wait_ge(self.stored[n].sem, 16 * NB * self.per_buffer[n] + 1)

    def close(self):
        self.core.split_a.base += 2 * NB * self.items
        self.core.split_v.base += 2 * NB * self.items


def key_chunks():
    return [(qb, j) for qb in range(NB) for j in range(TPB * (qb + 1))]


def max_pieces():
    return [(i, a, min(a + 1024, (i + 1) * P)) for i in range(TT) for a in range(0, (i + 1) * P, 1024)]


def attention(core, name, heads, dh, q_parts, k_parts, v_all, out, shared=False):
    nc, k = core.nc, core
    passes = 2 if dh == 32 else 1
    order_q, order_k = (0, 0, 1, 1, 0, 2), (0, 1, 0, 1, 2, 0)
    M_ROW = 6 * dh % P
    MAX_ROWS = P if passes == 2 else 6 * dh
    chunks, pieces = key_chunks(), max_pieces()
    NC, NM = len(chunks), len(pieces) + 1
    RING = 8
    LAG = 5
    LOADS = 12
    W = 32
    assert NC % RING == 0 and len(pieces) % 2 == 0

    with ExitStack() as ctx:
        def sb(nm, shape, dt=F32):
            return ctx.enter_context(nc.sbuf_tensor(nm + name, shape, dt))

        def tally(nm, base=0):
            return Tally(nc, ctx, nm + name, base)

        qs, ks = sb("qs", [P, 2, passes, T], BF16), sb("ks", [P, 2, passes, T], BF16)
        vh = sb("vh", [P, 1 if shared else 2, TT, P], BF16)
        v_rest = sb("v_rest", [P, TT, dh])
        expT = sb("expT", [P, RING, TB])
        e_parts = sb("e_parts", [P, RING, 2, TB], F16)
        part_max, neg_max = sb("part_max", [P, TT, 2]), sb("neg_max", [P, TT])
        m_parts, m_rest = sb("m_parts", [TT, 3, P], BF16), sb("m_rest", [TT, P])
        o_first, sums, o_sb = sb("o_first", [P, 2, TB]), sb("sums", [P, 2, TB]), sb("o_sb", [P, 2, TB])
        rec = sb("rec", [P, TB])
        shift, free_note = sb("shift", [P, 1]), sb("free_note", [1, 8])

        qk_in = [tally(f"qk_in{n}") for n in range(2)]
        m_in = [tally(f"m_in{n}") for n in range(2)]
        v_split = tally("v_split")
        max_filled, max_emptied = tally("max_filled"), tally("max_emptied")
        neg_ready, m_split = tally("neg_ready"), tally("m_split")
        scored, exp_done = tally("scored"), tally("exp_done", 2)
        cast_a, cast_v = tally("cast_a"), tally("cast_v")
        rest_done, used = tally("rest_done", RING), tally("used", RING)
        evacuated, o_added, o_joined = tally("evacuated"), tally("o_added"), tally("o_joined", 2)
        rec_done, o_done = tally("rec_done"), tally("o_done", 2)
        o_stored = [tally(f"o_stored{n}", 1) for n in range(2)]
        ready, m_out = tally("ready"), tally("m_out")
        m_rows = core.io["m_rows"]

        def max_bank(n):
            return 4 + 2 * (n % 2)

        steps = {6 + n: n for n in range(len(pieces))}
        steps[32] = len(pieces)
        V_STEP = 35

        def span(t):
            qb, j = chunks[t]
            return slice(max(0, j - TPB * qb) * P, TB)

        def last_chunk(qb):
            return chunks.index((qb, TPB * (qb + 1) - 1))

        ends = {last_chunk(qb): qb for qb in range(NB)}

        def walk(eng, head):
            for p in range(2):
                head(p, p, 0, True)
            with eng.Fori(1, heads // 2 - 1) as it:
                for p in range(2):
                    head(2 * it + p, p, it, True)
            for p in range(2):
                head(heads - 2 + p, p, heads // 2 - 1, p == 0)

        def behind(h, p, t, lag):
            if t >= lag:
                return h, p, t - lag
            if isinstance(h, int) and h == 0:
                return None
            return h - 1, 1 - p, NC + t - lag

        with nc.Block() as block:
            @block.sync
            def _(sp):
                def fetch(h, p):
                    for parts, dst, same, order in ((q_parts, qs, False, order_q), (k_parts, ks, shared, order_k)):
                        for n, which in enumerate(order):
                            at, s = n * dh % P, n * dh // P
                            rows = slice(0, dh) if same else bass.ds(h * dh, dh)
                            sp.dma_start(dst[at:at + dh, p, s, :], parts[which, rows, :]).then_inc(qk_in[p].sem, 16)

                def put_max(h, p):
                    sp.wait_ge(m_split.sem, 4 * h + 4)
                    sp.dma_start(m_rows.rearrange("a (t n) -> t a n", t=TT), m_parts[:, :, :]).then_inc(m_out.sem, 16)
                    sp.wait_ge(m_out.sem, 16 * h + 16)
                    sp.dma_start(qs[M_ROW:M_ROW + 3, p, passes - 1, :], m_rows).then_inc(m_in[p].sem, 16)

                def store(h, p):
                    sp.wait_ge(o_done.sem, h + 3)
                    for qb in range(NB):
                        sp.dma_start(out[bass.ds(h * dh, dh), qb * TB:(qb + 1) * TB], o_sb[W * qb:W * qb + dh, p, :])\
                          .then_inc(o_stored[p].sem, 16)

                sp.wait_ge(ready.sem, 5)
                for h in range(2):
                    fetch(h, h)
                put_max(0, 0)

                def head(h, p, it, more):
                    if not (isinstance(h, int) and h == 0):
                        store(h - 1, 1 - p)
                    if more:
                        put_max(h + 1, 1 - p)
                    if not (isinstance(h, int) and h >= heads - 2):
                        sp.wait_ge(scored.sem, NC * h + NC)
                        fetch(h + 2, p)

                walk(sp, head)
                store(heads - 1, 1)
                for p in range(2):
                    sp.wait_ge(o_stored[p].sem, 16 * NB * (heads // 2) + 1)

            @block.tensor
            def _(pe):
                def max_piece(h, p, it, n, first):
                    if n >= 2:
                        pe.wait_ge(max_emptied.sem, NM * h + (n - 1))
                    elif not first:
                        pe.wait_ge(max_emptied.sem, NM * h)
                    if n == len(pieces):
                        pe.wait_ge(neg_ready.sem, h + 1)
                        pe.transpose(k.ps[0:TT, max_bank(n), 0:P], neg_max[:, :], k.ident[:, :])\
                          .then_inc(max_filled.sem, 1)
                        return
                    if n == 0:
                        pe.wait_ge(qk_in[p].sem, it * (16 * LOADS) + 16 * LOADS)
                    i, a, b = pieces[n]
                    for c in range(a, b, 512):
                        width, bank = min(512, b - c), max_bank(n) + (c - a) // 512
                        diagonal = b == (i + 1) * P and c + 512 >= b
                        if diagonal:
                            pe.matmul(k.ps[:, bank, width - P:width], k.ident_b[:, :], k.mask_b[:, :],
                                      start=True, stop=False, skip_group_check=True)
                        m = pe.matmul(k.ps[:, bank, 0:width], qs[0:MAX_ROWS, p, 0, i * P:(i + 1) * P],
                                      ks[0:MAX_ROWS, p, 0, c:c + width], start=not diagonal, stop=True,
                                      skip_group_check=True)
                    m.then_inc(max_filled.sem, 1)

                def score(h, p, t):
                    qb, j = chunks[t]
                    pe.wait_ge(exp_done.sem, NC * h + t + 1)
                    cols, bank = span(t), t % 2
                    diagonal = j >= TPB * qb
                    if diagonal:
                        pe.matmul(k.ps[:, bank, cols.start:cols.start + P], k.ident_b[:, :], k.maskT_b[:, :],
                                  start=True, stop=False, skip_group_check=True)
                    for s in range(passes):
                        K = P if s < passes - 1 else M_ROW + 3
                        m = pe.matmul(k.ps[:, bank, cols], ks[0:K, p, s, j * P:(j + 1) * P],
                                      qs[0:K, p, s, qb * TB + cols.start:(qb + 1) * TB],
                                      start=s == 0 and not diagonal, stop=s == passes - 1, skip_group_check=True)
                    m.then_inc(scored.sem, 1)

                def weigh(h, p, t):
                    qb, j = chunks[t]
                    if t == 0 and not shared:
                        pe.wait_ge(v_split.sem, 4 * h + 4)
                    if j == 0:
                        pe.wait_ge(o_joined.sem, NB * h + qb + 1)
                    pe.wait_ge(rest_done.sem, NC * h + (t + 1 + RING))
                    for n in range(2):
                        m = pe.matmul(k.ps[:, 2 + qb % 2, span(t)], vh[:, 0 if shared else p, j, :],
                                      e_parts[:, t % RING, n, span(t)], start=j == 0 and n == 0,
                                      stop=j == TPB * (qb + 1) - 1 and n == 1, skip_group_check=True)
                    m.then_inc(used.sem, 1)

                pe.wait_ge(ready.sem, 5)
                pe.wait_ge(v_split.sem, 4)
                pe.wait_ge(exp_done.sem, 2)
                for n in range(NM):
                    max_piece(0, 0, 0, n, True)

                def head(h, p, it, more):
                    pe.wait_ge(m_in[p].sem, 16 * it + 16)
                    for t in range(NC):
                        score(h, p, t)
                        if more and t in steps:
                            max_piece(h + 1, 1 - p, it + p, steps[t], False)
                        last = behind(h, p, t, LAG)
                        if last:
                            weigh(*last)

                walk(pe, head)
                for t in range(NC - LAG, NC):
                    weigh(heads - 1, 1, t)

            @block.scalar
            def _(act):
                def evacuate(h, p, qb):
                    act.wait_ge(used.sem, NC * h + (RING + last_chunk(qb) + 1))
                    if qb == 0:
                        act.wait_ge(o_done.sem, h + 1)
                    rows, bank = slice(W * qb, W * (qb + 1)), 2 + qb % 2
                    act.activation(o_first[rows, p, :], k.ps[0:W, bank, :], ACT.Copy).then_inc(evacuated.sem, 1)
                    act.activation(sums[rows, p, :], k.ps[3 * W:4 * W, bank, :], ACT.Copy)\
                       .then_inc(evacuated.sem, 1)

                def head(h, p, it, more):
                    for t in range(NC):
                        act.wait_ge(rest_done.sem, NC * h + (t + 1))
                        act.wait_ge(scored.sem, NC * h + t + 1)
                        act.activation(expT[:, t % RING, span(t)], k.ps[:, t % 2, span(t)], ACT.Exp,
                                       bias=shift[:, 0:1]).then_inc(exp_done.sem, 1)
                        if t % 2 == 1:
                            act.wait_ge(used.sem, NC * h + t)
                            act.wait_ge(exp_done.sem, NC * h + t + 2)
                            act.activation(e_parts[:, (t - 1) % RING, 0, span(t - 1)],
                                           expT[:, (t - 1) % RING, span(t - 1)], ACT.Copy).then_inc(cast_a.sem, 1)
                        last = behind(h, p, t, LAG + 1)
                        if last and last[2] in ends:
                            evacuate(last[0], last[1], ends[last[2]])

                act.wait_ge(ready.sem, 5)
                walk(act, head)
                evacuate(heads - 1, 1, NB - 1)

            @block.gpsimd
            def _(pool):
                def head(h, p, it, more):
                    for t in range(NC):
                        if t % 2 == 0:
                            pool.wait_ge(cast_a.sem, NC // 2 * h + (t // 2 + 1))
                        else:
                            pool.wait_ge(cast_v.sem, NC // 2 * h + (t // 2 + 1))
                        at = t % RING
                        pool.tensor_tensor(e_parts[:, at, 1, span(t)], expT[:, at, span(t)],
                                           e_parts[:, at, 0, span(t)], ALU.subtract).then_inc(rest_done.sem, 1)

                pool.wait_ge(rest_done.sem, RING)
                walk(pool, head)

            @block.vector
            def _(dve):
                def split_values(h, p):
                    if shared:
                        src = v_all[:, :, :]
                    else:
                        src = v_all[:, :, bass.ds(h * dh, dh)]
                    dst = [vh[:, p, :, W * n:W * n + dh] for n in range(3)]
                    dve.tensor_copy(dst[0], src).then_inc(v_split.sem, 1)
                    dve.wait_ge(v_split.sem, 4 * h + 1)
                    dve.tensor_tensor(v_rest[:, :, :], src, dst[0], ALU.subtract).then_inc(v_split.sem, 1)
                    dve.wait_ge(v_split.sem, 4 * h + 2)
                    dve.tensor_copy(dst[1], v_rest[:, :, :]).then_inc(v_split.sem, 1)
                    dve.wait_ge(v_split.sem, 4 * h + 3)
                    dve.tensor_tensor(dst[2], v_rest[:, :, :], dst[1], ALU.subtract).then_inc(v_split.sem, 1)
                    dve.wait_ge(v_split.sem, 4 * h + 4)

                def take_max(h, n):
                    dve.wait_ge(max_filled.sem, NM * h + n + 1)
                    if n < len(pieces):
                        i, a, b = pieces[n]
                        src = k.ps[:, max_bank(n):max_bank(n) + 2, :].rearrange("p a n -> p (a n)")[:, 0:b - a]
                        dve.tensor_reduce(part_max[:, i, a // 1024:a // 1024 + 1], src, X_AXIS, ALU.max)\
                           .then_inc(max_emptied.sem, 1)
                        if n == len(pieces) - 1:
                            dve.wait_ge(max_emptied.sem, NM * h + n + 1)
                            dve.tensor_reduce(neg_max[:, :], part_max[:, :, :], X_AXIS, ALU.max, negate=True)\
                               .then_inc(neg_ready.sem, 1)
                        return
                    src = k.ps[0:TT, max_bank(n), 0:P]
                    dve.tensor_copy(m_parts[:, 0, :], src).then_inc(m_split.sem, 1)
                    dve.wait_ge(m_split.sem, 4 * h + 1)
                    dve.tensor_tensor(m_rest[:, :], src, m_parts[:, 0, :], ALU.subtract).then_inc(m_split.sem, 1)
                    dve.wait_ge(m_split.sem, 4 * h + 2)
                    dve.tensor_copy(m_parts[:, 1, :], m_rest[:, :]).then_inc(m_split.sem, 1)
                    dve.wait_ge(m_split.sem, 4 * h + 3)
                    dve.tensor_tensor(m_parts[:, 2, :], m_rest[:, :], m_parts[:, 1, :], ALU.subtract)\
                       .then_inc(m_split.sem, 1)
                    dve.wait_ge(m_split.sem, 4 * h + 4)
                    dve.memset(free_note[:, 6:7], 0.0).then_inc(max_emptied.sem, 1)

                def join(h, p, it, qb):
                    rows, bank = slice(W * qb, W * (qb + 1)), 2 + qb % 2
                    dve.wait_ge(evacuated.sem, 2 * NB * h + (2 * qb + 2))
                    dve.tensor_tensor(o_first[rows, p, :], o_first[rows, p, :], k.ps[W:2 * W, bank, :], ALU.add)\
                       .then_inc(o_added.sem, 1)
                    if qb == 0:
                        dve.wait_ge(o_stored[p].sem, 16 * NB * it + 1)
                    dve.wait_ge(o_added.sem, NB * h + (qb + 1))
                    dve.tensor_tensor(o_sb[rows, p, :], o_first[rows, p, :], k.ps[2 * W:3 * W, bank, :], ALU.add)\
                       .then_inc(o_joined.sem, 1)

                def reciprocal(h, p, half):
                    cols = slice(TB // 2 * half, TB // 2 * (half + 1))
                    if half == 0:
                        dve.wait_ge(o_done.sem, h + 2)
                    dve.reciprocal(rec[:, cols], sums[:, p, cols]).then_inc(rec_done.sem, 1)

                def divide(h, p):
                    dve.wait_ge(rec_done.sem, 2 * h + 2)
                    dve.wait_ge(o_joined.sem, NB * h + (NB + 2))
                    dve.tensor_tensor(o_sb[:, p, :], o_sb[:, p, :], rec[:, :], ALU.mult).then_inc(o_done.sem, 1)

                for n, tl in enumerate((exp_done, used, rest_done, o_joined, o_done, *o_stored)):
                    dve.memset(free_note[:, n:n + 1], 0.0).then_inc(tl.sem, tl.base)
                dve.memset(vh[:, :, :, :], 1.0).then_inc(ready.sem, 1)
                dve.memset(part_max[:, :, 1:2], NEG).then_inc(ready.sem, 1)
                dve.memset(ks[M_ROW // 32 * 32:, :, passes - 1, :], 1.0).then_inc(ready.sem, 1)
                dve.memset(shift[:, :], SHIFT).then_inc(ready.sem, 1)
                dve.memset(sums[:, :, :], 1.0).then_inc(ready.sem, 1)
                dve.wait_ge(ready.sem, 5)
                split_values(0, 0)
                for n in range(NM):
                    take_max(0, n)

                def head(h, p, it, more):
                    for t in range(NC):
                        if t % 2 == 1:
                            dve.wait_ge(used.sem, NC * h + t + 1)
                            dve.wait_ge(exp_done.sem, NC * h + t + 3)
                            dve.tensor_copy(e_parts[:, t % RING, 0, span(t)], expT[:, t % RING, span(t)])\
                               .then_inc(cast_v.sem, 1)
                        if more and t in steps:
                            take_max(h + 1, steps[t])
                        if more and t == V_STEP and not shared:
                            if not (isinstance(h, int) and h == 0):
                                dve.wait_ge(used.sem, NC * h + RING)
                            split_values(h + 1, 1 - p)
                        last = behind(h, p, t, LAG + 2)
                        if last and last[2] in ends:
                            join(last[0], last[1], it if last[2] == t - LAG - 2 else it - 1 + p, ends[last[2]])
                        if not (isinstance(h, int) and h == 0):
                            if t in (LAG + 2, LAG + 4):
                                reciprocal(h - 1, 1 - p, t // (LAG + 4))
                            elif t == LAG + 5:
                                divide(h - 1, 1 - p)

                walk(dve, head)
                join(heads - 1, 1, heads // 2 - 1, NB - 1)
                reciprocal(heads - 1, 1, 0)
                reciprocal(heads - 1, 1, 1)
                divide(heads - 1, 1)


def layer1(core):
    nc, k, io = core.nc, core, core.io
    with ExitStack() as ctx:
        def sb(name, shape, dt=F32):
            return ctx.enter_context(nc.sbuf_tensor(name, shape, dt))

        v_all = sb("v1_all", [P, TT, P])
        with ExitStack() as inner:
            layer1_blocks(core, inner, v_all)
        attention(core, "1", 8, 16, io["q1_parts"], io["k1_parts"], v_all, io["o1"])
        w_out, b_out = sb("w_out1", [P, 1, D]), sb("b_out1", [P, C])
        project_out(core, ctx, "1", io["o1"], None, w_out, b_out,
                    [(w_out[:, 0, :], io["L1_out_w"]), (b_out[:, :], io["L1_out_b"])])


def project_out(core, ctx, name, heads_out, added, weights, bias, loads, result=None):
    nc, k = core.nc, core
    chunks = weights.shape[1]
    o_in = ctx.enter_context(nc.sbuf_tensor("o_in" + name, [P, 2, chunks, TB], F32))
    a_in = ctx.enter_context(nc.sbuf_tensor("a_in" + name, [P, 2, C, TB], F32)) if added is not None else None
    arrived = [Tally(nc, ctx, f"o_arrived{name}{n}") for n in range(2)]
    per = 2 if added is not None else 1
    grp = Groups(core, "v" * C)
    chain = Chain(k.v_chain)
    per_chain = C if added is not None else 0
    with nc.Block() as block:
        @block.sync
        def _(sp):
            load(sp, core, loads)

            def fetch(b, p):
                sp.dma_start(o_in[:, p, :, :], heads_out.rearrange("(c p) t -> p c t", p=P)
                             [:, :, bass.ds(b * TB, TB)]).then_inc(arrived[p].sem, 16)
                if added is not None:
                    sp.dma_start(a_in[:, p, :, :], added.rearrange("(c p) t -> p c t", p=P)
                                 [:, :, bass.ds(b * TB, TB)]).then_inc(arrived[p].sem, 16)

            for b in range(NB):
                if b >= 2:
                    grp.wait_block(sp, b - 1)
                fetch(b, b % 2)
            if result is not None:
                for b in range(NB):
                    grp.wait_block(sp, b + 1)
                    sp.dma_start(result.rearrange("(c p) t -> p c t", p=P)[:, :, b * TB:(b + 1) * TB],
                                 k.x[:, :, b * TB:(b + 1) * TB]).then_inc(k.stored.sem, 16)
                sp.wait_ge(k.stored.sem, k.stored.base + 16 * NB)

        @block.tensor
        def _(pe):
            pe.wait_ge(k.loaded.sem, k.loaded.base)
            for b in range(NB):
                grp.wait_block(pe, b)
                pe.wait_ge(arrived[b % 2].sem, 16 * per * (b // 2 + 1))
                for oc in range(C):
                    project(pe, k.ps[:, grp.bank(oc), :], lambda c: weights[:, c, oc * P:(oc + 1) * P],
                            lambda c: o_in[:, b % 2, c, :], chunks).then_inc(k.filled.sem, 1)

        @block.vector
        def _(dve):
            dve.wait_ge(k.loaded.sem, k.loaded.base)
            for b in range(NB):
                chain.start(dve, b * per_chain)
                for oc in range(C):
                    xs = k.x[:, oc, b * TB:(b + 1) * TB]
                    if added is not None:
                        dve.wait_ge(arrived[b % 2].sem, 16 * per * (b // 2 + 1))
                        chain.link(dve.tensor_tensor(xs, xs, a_in[:, b % 2, oc, :], ALU.add))
                    grp.wait_filled(dve, b, oc)
                    dve.scalar_tensor_tensor(xs, k.ps[:, grp.bank(oc), :], bias[:, oc:oc + 1], xs,
                                             ALU.add, ALU.add).then_inc(k.emptied_v.sem, 1)
    grp.close()
    k.v_chain.base += NB * per_chain


def widen(core, ctx, name, dst, src, pieces, loads):
    nc, k = core.nc, core
    with ExitStack() as inner:
        raw = inner.enter_context(nc.sbuf_tensor("raw" + name, [P, 2, 2 * PIECE], I32))
        raw_in = [Tally(nc, ctx, f"raw_in{name}{n}") for n in range(2)]
        widened = Tally(nc, ctx, "widened" + name, 2)
        with nc.Block() as block:
            @block.gpsimd
            def _(pool):
                pool.memset(raw[0:1, 0, 0:1], 0).then_inc(widened.sem, 2)

            @block.sync
            def _(sp):
                for dst_, src_ in loads:
                    sp.dma_start(dst_, src_).then_inc(k.loaded.sem, 16)
                with sp.Fori(0, pieces // 2) as i:
                    for p in range(2):
                        n = 2 * i + p
                        sp.wait_ge(widened.sem, n + 1)
                        sp.dma_start(raw[:, p, :], src[:, bass.ds(n, 1), :].rearrange("p a n -> p (a n)"))\
                          .then_inc(raw_in[p].sem, 16)
                sp.wait_ge(k.loaded.sem, k.loaded.base + 16 * len(loads))

            @block.vector
            def _(dve):
                dve.wait_ge(widened.sem, 2)
                with dve.Fori(0, pieces // 2) as i:
                    for p in range(2):
                        n = 2 * i + p
                        dve.wait_ge(raw_in[p].sem, 16 * (i + 1))
                        dve.tensor_scalar(dst[:, bass.ds(n * 2 * PIECE, 2 * PIECE)], raw[:, p, :], -128.0, None,
                                          ALU.add).then_inc(widened.sem, 1)
        k.loaded.base += 16 * len(loads)


def layer1_blocks(core, ctx, v_all):
    nc, k, io = core.nc, core, core.io

    def sb(name, shape, dt=F32):
        return ctx.enter_context(nc.sbuf_tensor(name, shape, dt))

    wp = sb("wp1", [P, 3, C, P])
    bp = sb("bp1", [P, 3])
    wv, bv = sb("wv1", [P, P]), sb("bv1", [P, P])
    rot = sb("rot1", [P, P])
    wf = sb("wf1", [P, (2 * C + C) * H1])
    w_gate = wf[:, 0:C * H1].rearrange("p (c n) -> p c n", c=C)
    w_up = wf[:, C * H1:2 * C * H1].rearrange("p (c n) -> p c n", c=C)
    w_down = wf[:, 2 * C * H1:].rearrange("p (j n) -> p j n", j=J1)
    s_hid, s_down = sb("s_hid", [P, 2, J1]), sb("s_down", [P, C])
    widen(core, ctx, "1", wf, io["L1_wq"], 12,
          [(wp[:, :, :, :], io["L1_w"]), (bp[:, :], io["L1_b"]), (wv[:, :], io["L1_cv_w"]),
           (bv[:, :], io["L1_cv_b"].partition_broadcast(P)), (rot[:, :], io["L1_rot"]),
           (s_hid[:, :, :], io["L1_s_hid"]), (s_down[:, :], io["L1_s_down"])])

    norm = Norm(core, ctx, 1)
    split = Split(core, ctx, "1", 2)
    plain = sb("plain1", [P, 2, TB])
    turned_, mixed = sb("turned1", [P, 2, TB]), sb("mixed1", [P, 2, TB])
    act_qk = sb("act_qk1", [P, 2, TB])
    ckv = sb("ckv", [P, TB])
    wave = sb("wave1", [P, 2, TB])
    h, sg = sb("h1", [P, J1, TB]), sb("sg1", [P, 2, TB])
    wave_in = Tally(nc, ctx, "wave_in1")
    qk_act = Tally(nc, ctx, "qk_act1")

    grp = Groups(core, "aaa" + "vv" + "v" + "av" * J1 + "v" * C)
    Q, K_, KV, RQ, RK, V, FFN = 0, 1, 2, 3, 4, 5, 6
    DOWN = FFN + 2 * J1
    chain = Chain(k.v_chain)
    per_block = 4

    with nc.Block() as block:
        @block.sync
        def _(sp):
            with sp.Fori(0, NB) as b:
                split.store(sp, b, 0, io["q1_parts"], after=1)
                split.store(sp, b, 1, io["k1_parts"], after=None)
            split.wait_stores(sp)

        @block.tensor
        def _(pe):
            with pe.Fori(0, NB) as b:
                grp.wait_block(pe, b)
                norm.tensor(pe, b)
                for g, w in ((Q, 0), (K_, 2), (KV, 1)):
                    project(pe, k.ps[:, grp.bank(g), :], lambda c: wp[:, w, c, :], lambda c: norm.xn[:, c, :])\
                        .then_inc(k.filled.sem, 1)
                for n, g in enumerate((RQ, RK)):
                    grp.wait_emptied(pe, b, (Q, K_)[n])
                    pe.matmul(k.ps[:, grp.bank(g), :], rot[:, :], plain[:, n, :], start=True, stop=True)\
                      .then_inc(k.filled.sem, 1)
                grp.wait_emptied(pe, b, KV)
                for t in range(TPB):
                    m = pe.matmul(k.ps[:, grp.bank(V), t * P:(t + 1) * P], ckv[:, t * P:(t + 1) * P], wv[:, :],
                                  start=True, stop=True)
                m.then_inc(k.filled.sem, 1)
                for j in range(J1):
                    for u, w in enumerate((w_gate, w_up)):
                        g = FFN + 2 * j + u
                        grp.wait_free(pe, b, g)
                        project(pe, k.ps[:, grp.bank(g), :], lambda c: w[:, c, j * P:(j + 1) * P],
                                lambda c: norm.xn[:, c, :]).then_inc(k.filled.sem, 1)
                grp.wait_emptied(pe, b, DOWN - 1)
                for oc in range(C):
                    grp.wait_free(pe, b, DOWN + oc)
                    project(pe, k.ps[:, grp.bank(DOWN + oc), :], lambda j: w_down[:, j, oc * P:(oc + 1) * P],
                            lambda j: h[:, j, :], J1).then_inc(k.filled.sem, 1)

        @block.scalar
        def _(act):
            with act.Fori(0, NB) as b:
                grp.wait_block(act, b)
                act.dma_start(wave[:, :, :], io["L1_wave"][:, :, bass.ds(b * TB, TB)]).then_inc(wave_in.sem, 16)
                norm.scalar(act, b)
                for n, g in enumerate((Q, K_)):
                    grp.wait_filled(act, b, g)
                    act.activation(plain[:, n, :], k.ps[:, grp.bank(g), :], ACT.Identity,
                                   bias=bp[:, 2 * n:2 * n + 1]).then_inc(k.emptied_a.sem, 1)
                grp.wait_filled(act, b, KV)
                act.activation(ckv[:, :], k.ps[:, grp.bank(KV), :], ACT.Gelu, bias=bp[:, 1:2])\
                   .then_inc(k.emptied_a.sem, 1)
                for n in range(2):
                    act.wait_ge(k.v_chain.sem, chain.tally.base + b * per_block + 2 * n + 2)
                    act.activation(act_qk[:, n, :], mixed[:, n, :], ACT.Gelu).then_inc(qk_act.sem, 1)
                    act.wait_ge(qk_act.sem, 2 * b + n + 1)
                    split.scalar_1(act, b, n, act_qk[:, n, :], (0.25, 1.0)[n])
                    split.scalar_2(act, b, n)
                for j in range(J1):
                    g = FFN + 2 * j
                    if j >= 2:
                        grp.wait_emptied(act, b, g - 3)
                    grp.wait_filled(act, b, g)
                    act.activation(sg[:, j % 2, :], k.ps[:, grp.bank(g), :], ACT.Silu, scale=s_hid[:, 0, j:j + 1])\
                       .then_inc(k.emptied_a.sem, 1)

        @block.vector
        def _(dve):
            split.prime(dve)
            with dve.Fori(0, NB) as b:
                norm.vector(dve, b)
                chain.start(dve, b * per_block)
                dve.wait_ge(wave_in.sem, 16 * (b + 1))
                for n, (g, r) in enumerate(((Q, RQ), (K_, RK))):
                    grp.wait_emptied(dve, b, g)
                    chain.mark(dve.tensor_tensor(mixed[:, n, :], plain[:, n, :], wave[:, 0, :], ALU.mult))
                    grp.wait_filled(dve, b, r)
                    dve.tensor_tensor(turned_[:, n, :], k.ps[:, grp.bank(r), :], wave[:, 1, :], ALU.mult)\
                       .then_inc(k.emptied_v.sem, 1)
                    grp.wait_emptied(dve, b, r)
                    dve.wait_ge(k.v_chain.sem, chain.at + chain.n)
                    chain.link(dve.tensor_tensor(mixed[:, n, :], mixed[:, n, :], turned_[:, n, :], ALU.add))
                for n in range(2):
                    dve.wait_ge(qk_act.sem, 2 * b + n + 1)
                    split.vector_1(dve, b, n, act_qk[:, n, :], (0.25, 1.0)[n])
                    split.vector_2(dve, b, n)
                grp.wait_filled(dve, b, V)
                dve.tensor_tensor(v_all[:, bass.ds(b * TPB, TPB), :],
                                  k.ps[:, grp.bank(V), :].rearrange("p (t n) -> p t n", t=TPB),
                                  bv[:, :].unsqueeze(1).to_broadcast([P, TPB, P]), ALU.add)\
                   .then_inc(k.emptied_v.sem, 1)
                assert chain.n == per_block
                for j in range(J1):
                    g = FFN + 2 * j
                    grp.wait_emptied(dve, b, g)
                    grp.wait_filled(dve, b, g + 1)
                    dve.scalar_tensor_tensor(h[:, j, :], k.ps[:, grp.bank(g + 1), :], s_hid[:, 1, j:j + 1],
                                             sg[:, j % 2, :], ALU.mult, ALU.mult).then_inc(k.emptied_v.sem, 1)
                for oc in range(C):
                    grp.wait_filled(dve, b, DOWN + oc)
                    xs = k.x[:, oc, bass.ds(b * TB, TB)]
                    dve.scalar_tensor_tensor(xs, k.ps[:, grp.bank(DOWN + oc), :], s_down[:, oc:oc + 1], xs,
                                             ALU.mult, ALU.add).then_inc(k.emptied_v.sem, 1)
    grp.close()
    split.close()
    k.v_chain.base += NB * per_block


def layer2(core):
    nc, k, io = core.nc, core, core.io
    with ExitStack() as ctx:
        def sb(name, shape, dt=F32):
            return ctx.enter_context(nc.sbuf_tensor(name, shape, dt))

        rows = sb("rows", [P, TT, D])
        logits = sb("logits", [P, TT, EXPERTS])
        slot_in, slot_out = sb("slot_in", [P, TOPK, TT], I32), sb("slot_out", [P, TOPK, TT], I32)
        share = sb("share", [P, TOPK, TT])
        with ExitStack() as inner:
            layer2_blocks(core, inner, rows, logits)
        with ExitStack() as inner:
            route(core, inner, logits, slot_in, slot_out, share)
        with ExitStack() as inner:
            experts(core, inner, rows, slot_in, slot_out, share)


def layer2_blocks(core, ctx, rows, logits):
    nc, k, io = core.nc, core, core.io

    def sb(name, shape, dt=F32):
        return ctx.enter_context(nc.sbuf_tensor(name, shape, dt))

    HS = JS * P
    wr, br = sb("wr", [P, C, EXPERTS]), sb("br", [P, EXPERTS])
    wv, wo = sb("wv2", [P, C, D]), sb("wo2", [P, C, D])
    s_gate, s_up, s_down = sb("s_gate", [P, C, HS]), sb("s_up", [P, C, HS]), sb("s_down2", [P, JS, D])
    norm = Norm(core, ctx, 2)
    value = sb("value2", [P, C, TB])
    h, sg = sb("h2", [P, JS, TB]), sb("sg2", [P, 2, TB])

    grp = Groups(core, "v" + "a" * TPB + "a" * C + "av" * JS + "v" * C)
    R, ROWS, V = 0, 1, 1 + TPB
    FFN = V + C
    OUT = FFN + 2 * JS
    with nc.Block() as block:
        @block.sync
        def _(sp):
            load(sp, core, [(wr[:, :, :], io["L2_wr"]), (br[:, :], io["L2_br"].partition_broadcast(P)),
                            (wv[:, :, :], io["L2_wv"]), (s_gate[:, :, :], io["L2_sg"]), (s_up[:, :, :], io["L2_su"]),
                            (wo[:, :, :], io["L2_wo"]), (s_down[:, :, :], io["L2_sd"])])

        @block.tensor
        def _(pe):
            pe.wait_ge(k.loaded.sem, k.loaded.base)
            with pe.Fori(0, NB) as b:
                grp.wait_block(pe, b)
                norm.tensor(pe, b)
                for t in range(TPB):
                    m = project(pe, k.ps[:, grp.bank(R), t * EXPERTS:(t + 1) * EXPERTS],
                                lambda c: norm.xn[:, c, t * P:(t + 1) * P], lambda c: wr[:, c, :])
                m.then_inc(k.filled.sem, 1)
                for t in range(TPB):
                    for c in range(C):
                        m = pe.transpose(k.ps[:, grp.bank(ROWS + t), c * P:(c + 1) * P],
                                         norm.xn[:, c, t * P:(t + 1) * P], k.ident[:, :])
                    m.then_inc(k.filled.sem, 1)
                for oc in range(C):
                    grp.wait_free(pe, b, V + oc)
                    project(pe, k.ps[:, grp.bank(V + oc), :], lambda c: wv[:, c, oc * P:(oc + 1) * P],
                            lambda c: norm.xn[:, c, :]).then_inc(k.filled.sem, 1)
                for j in range(JS):
                    for u, w in enumerate((s_gate, s_up)):
                        g = FFN + 2 * j + u
                        grp.wait_free(pe, b, g)
                        project(pe, k.ps[:, grp.bank(g), :], lambda c: w[:, c, j * P:(j + 1) * P],
                                lambda c: norm.xn[:, c, :]).then_inc(k.filled.sem, 1)
                grp.wait_emptied(pe, b, OUT - 1)
                for oc in range(C):
                    grp.wait_free(pe, b, OUT + oc)
                    for j in range(C + JS):
                        w, y = (wo, value) if j < C else (s_down, h)
                        c = j if j < C else j - C
                        m = pe.matmul(k.ps[:, grp.bank(OUT + oc), :], w[:, c, oc * P:(oc + 1) * P], y[:, c, :],
                                      start=j == 0, stop=j == C + JS - 1)
                    m.then_inc(k.filled.sem, 1)

        @block.scalar
        def _(act):
            with act.Fori(0, NB) as b:
                norm.scalar(act, b)
                for t in range(TPB):
                    grp.wait_filled(act, b, ROWS + t)
                    act.activation(rows[:, bass.ds(b * TPB + t, 1), :], k.ps[:, grp.bank(ROWS + t), :].unsqueeze(1), ACT.Copy)\
                       .then_inc(k.emptied_a.sem, 1)
                for oc in range(C):
                    grp.wait_filled(act, b, V + oc)
                    act.activation(value[:, oc, :], k.ps[:, grp.bank(V + oc), :], ACT.Copy)\
                       .then_inc(k.emptied_a.sem, 1)
                for j in range(JS):
                    g = FFN + 2 * j
                    if j >= 2:
                        grp.wait_emptied(act, b, g - 3)
                    grp.wait_filled(act, b, g)
                    act.activation(sg[:, j % 2, :], k.ps[:, grp.bank(g), :], ACT.Silu).then_inc(k.emptied_a.sem, 1)

        @block.vector
        def _(dve):
            dve.wait_ge(k.loaded.sem, k.loaded.base)
            with dve.Fori(0, NB) as b:
                norm.vector(dve, b)
                grp.wait_filled(dve, b, R)
                dve.tensor_tensor(logits[:, bass.ds(b * TPB, TPB), :],
                                  k.ps[:, grp.bank(R), 0:TPB * EXPERTS].rearrange("p (t e) -> p t e", t=TPB),
                                  br[:, :].unsqueeze(1).to_broadcast([P, TPB, EXPERTS]), ALU.add)\
                   .then_inc(k.emptied_v.sem, 1)
                for j in range(JS):
                    g = FFN + 2 * j
                    grp.wait_emptied(dve, b, g)
                    grp.wait_filled(dve, b, g + 1)
                    dve.tensor_tensor(h[:, j, :], k.ps[:, grp.bank(g + 1), :], sg[:, j % 2, :], ALU.mult)\
                       .then_inc(k.emptied_v.sem, 1)
                for oc in range(C):
                    grp.wait_filled(dve, b, OUT + oc)
                    xs = k.x[:, oc, bass.ds(b * TB, TB)]
                    dve.tensor_tensor(xs, xs, k.ps[:, grp.bank(OUT + oc), :], ALU.add).then_inc(k.emptied_v.sem, 1)
    grp.close()


def route(core, ctx, logits, slot_in, slot_out, share):
    nc, k, io = core.nc, core, core.io

    def sb(name, shape, dt=F32):
        return ctx.enter_context(nc.sbuf_tensor(name, shape, dt))

    E, PAD = EXPERTS, 8
    TAKEN, NONE = -7.0, -5.0
    row = sb("row", [P, 4, TT])
    expd = sb("expd", [P, TT, E])
    score = sb("score", [P, TT, E + PAD])
    left = sb("left", [P, TT, E + PAD])
    best, taken = sb("best", [P, TT, 8]), sb("taken", [P, TT, 8])
    picked = sb("picked_e", [P, TT, E])
    before = sb("before", [P, TT, E])
    place = sb("place", [P, TT, E])
    which, one, got = sb("which", [P, 1, E]), sb("one", [P, TT, E]), sb("got", [P, 4, TT])
    which_i = sb("which_i", [P, E], I32)
    earlier, ones = sb("earlier", [P, P]), sb("ones_p", [P, P])
    best_e = sb("best_e", [P, TT, 8], U32)
    best_f = sb("best_f", [P, TT, 8])
    made, expd_done, placed = Tally(nc, ctx, "route_made"), Tally(nc, ctx, "route_exp"), Tally(nc, ctx, "route_pe")
    shifted = Tally(nc, ctx, "route_shifted")
    chosen = Tally(nc, ctx, "route_chosen")
    chain = Chain(k.v_chain)

    with nc.Block() as block:
        @block.gpsimd
        def _(pool):
            pool.memset(earlier[:, :], 1.0).then_inc(made.sem, 1)
            pool.memset(ones[:, :], 1.0).then_inc(made.sem, 1)
            pool.iota(which_i[:, :], pattern=[[1, E]], base=0, channel_multiplier=0).then_inc(made.sem, 1)
            pool.wait_ge(made.sem, 3)
            pool.affine_select(out=earlier[:, :], in_=earlier[:, :], compare_op=ALU.is_gt, fill=0.0,
                               base=0, pattern=[[1, P]], channel_multiplier=-1).then_inc(made.sem, 1)

        @block.scalar
        def _(act):
            act.wait_ge(shifted.sem, 1)
            act.activation(expd[:, :, :], logits[:, :, :], ACT.Exp).then_inc(expd_done.sem, 1)

        @block.tensor
        def _(pe):
            pe.wait_ge(made.sem, 4)
            pe.wait_ge(chosen.sem, 1)
            for n in range(2):
                half = slice(n * TT // 2, (n + 1) * TT // 2)
                out = k.ps[:, n, :].rearrange("p (t e) -> p t e", e=E)
                pe.matmul(out, earlier[:, :], picked[:, half, :], start=True, stop=False)
                pe.matmul(out, ones[:, :], before[:, half, :], start=False, stop=True).then_inc(placed.sem, 1)

        @block.vector
        def _(dve):
            chain.start(dve)

            def wide(v, n=E):
                return v.unsqueeze(2).to_broadcast([P, TT, n])

            chain.mark(dve.memset(score[:, :, E:], NONE))
            chain.mark(dve.memset(taken[:, :, :], NONE))
            chain.link(dve.tensor_reduce(row[:, 0, :], logits[:, :, :], X_AXIS, ALU.max))
            dve.tensor_tensor(logits[:, :, :], logits[:, :, :], wide(row[:, 0, :]), ALU.subtract)\
               .then_inc(shifted.sem, 1)
            dve.wait_ge(expd_done.sem, 1)
            chain.link(dve.tensor_reduce(row[:, 1, :], expd[:, :, :], X_AXIS, ALU.add))
            chain.link(dve.reciprocal(row[:, 2, :], row[:, 1, :]))
            chain.link(dve.tensor_tensor(score[:, :, 0:E], expd[:, :, :], wide(row[:, 2, :]), ALU.mult))
            for t in range(TT):
                chain.mark(dve.max(best[:, t, :], score[:, t, 0:E]))
            dve.wait_ge(k.v_chain.sem, chain.at + chain.n)
            chain.link(dve.tensor_copy(taken[:, :, 0:TOPK], best[:, :, 0:TOPK]))
            for t in range(TT):
                chain.mark(dve.match_replace(left[:, t, :], taken[:, t, :], score[:, t, :], TAKEN))
                chain.mark(dve.max_index(best_e[:, t, :], best[:, t, :], score[:, t, 0:E]))
            dve.wait_ge(k.v_chain.sem, chain.at + chain.n)
            chain.link(dve.tensor_scalar(picked[:, :, :], left[:, :, 0:E], NONE - 1.0, None, ALU.is_lt))
            chain.link(dve.memset(before[:, 0, :], 0.0))
            for t in range(1, TT):
                chain.link(dve.tensor_tensor(before[:, t, :], before[:, t - 1, :], picked[:, t - 1, :], ALU.add))
            chain.link(dve.memset(got[:, :, :], 0.0))
            dve.tensor_copy(best_f[:, :, :], best_e[:, :, :]).then_inc(chosen.sem, 1)
            chain.link(dve.tensor_reduce(row[:, 3, :], best[:, :, 0:TOPK], X_AXIS, ALU.add))
            chain.link(dve.reciprocal(row[:, 3, :], row[:, 3, :]))
            dve.wait_ge(made.sem, 3)
            chain.link(dve.tensor_copy(which[:, 0, :], which_i[:, :]))
            dve.wait_ge(placed.sem, 2)
            for n in range(2):
                chain.mark(dve.tensor_copy(place[:, n * TT // 2:(n + 1) * TT // 2, :],
                                           k.ps[:, n, :].rearrange("p (t e) -> p t e", e=E)))
            dve.wait_ge(k.v_chain.sem, chain.at + chain.n)
            dve.wait_ge(chosen.sem, 1)
            for c in range(TOPK):
                e = best_f[:, :, c]
                chain.link(dve.tensor_tensor(one[:, :, :], wide(e), which[:, :, :].to_broadcast([P, TT, E]),
                                             ALU.is_equal))
                chain.link(dve.tensor_tensor(one[:, :, :], one[:, :, :], place[:, :, :], ALU.mult))
                chain.link(dve.tensor_reduce(got[:, 0, :], one[:, :, :], X_AXIS, ALU.add))
                chain.mark(dve.tensor_scalar(got[:, 1, :], got[:, 0, :], float(CAP), None, ALU.is_lt))
                chain.mark(dve.tensor_scalar(got[:, 2, :], got[:, 0, :], float(CAP - 1), None, ALU.min))
                chain.link(dve.tensor_scalar(got[:, 3, :], e, float(CAP), None, ALU.mult))
                chain.link(dve.tensor_tensor(got[:, 2, :], got[:, 2, :], got[:, 3, :], ALU.add))
                chain.mark(dve.tensor_copy(slot_out[:, c, :], got[:, 2, :]))
                chain.link(dve.tensor_scalar(got[:, 3, :], got[:, 1, :], -float(2 * SLOTS), float(2 * SLOTS),
                                             ALU.mult, ALU.add))
                chain.link(dve.tensor_tensor(got[:, 3, :], got[:, 3, :], got[:, 2, :], ALU.add))
                chain.mark(dve.tensor_copy(slot_in[:, c, :], got[:, 3, :]))
                chain.link(dve.tensor_tensor(share[:, c, :], best[:, :, c], row[:, 3, :], ALU.mult))
                chain.link(dve.tensor_tensor(share[:, c, :], share[:, c, :], got[:, 1, :], ALU.mult))
    k.v_chain.base += chain.n


def experts(core, ctx, rows, slot_in, slot_out, share):
    nc, k, io = core.nc, core, core.io

    def sb(name, shape, dt=F32):
        return ctx.enter_context(nc.sbuf_tensor(name, shape, dt))

    sent = Tally(nc, ctx, "sent")
    w = sb("w_exp", [P, 2, 3 * D])
    xe, xeT = sb("xe", [P, 2, D]), sb("xeT", [P, 2, C, P])
    ge, he, ye = sb("ge", [P, 2, P]), sb("he", [P, 2, P]), sb("ye", [P, 2, D])
    w_in = [Tally(nc, ctx, f"w_in{n}") for n in range(2)]
    y_out = [Tally(nc, ctx, f"y_out{n}", 1) for n in range(2)]
    xT_filled, xT_copied = Tally(nc, ctx, "xT_filled"), Tally(nc, ctx, "xT_copied")
    gu_filled, g_done, h_done = Tally(nc, ctx, "gu_filled"), Tally(nc, ctx, "g_done"), Tally(nc, ctx, "h_done")
    y_filled, y_copied = Tally(nc, ctx, "y_filled", 2), Tally(nc, ctx, "y_copied", 2)
    note = sb("note2", [1, 8])

    with nc.Block() as block:
        @block.gpsimd
        def _(pool):
            for n, tl in enumerate((*y_out, y_filled, y_copied)):
                pool.memset(note[:, n:n + 1], 0.0).then_inc(tl.sem, tl.base)
            for t in range(TT):
                for c in range(TOPK):
                    pool.indirect_dma_start(
                        out=io["slots_x"], out_offset=bass.IndirectOffsetOnAxis(ap=slot_in[:, c, t:t + 1], axis=0),
                        in_=rows[:, t, :], in_offset=None, bounds_check=SLOTS - 1, oob_is_err=False)\
                        .then_inc(sent.sem, 16)

        @block.sync
        def _(sp):
            sp.wait_ge(y_filled.sem, 2)
            with sp.Fori(0, EXPERTS // 2) as it:
                for p in range(2):
                    e = 2 * it + p
                    sp.wait_ge(y_filled.sem, e + 1)
                    sp.dma_start(w[:, p, :], io["L2_we"][bass.ds(e, 1), :, :].rearrange("a p n -> (a p) n"))\
                      .then_inc(w_in[p].sem, 16)
                    sp.wait_ge(sent.sem, 16 * TT * TOPK)
                    sp.dma_start(xe[:, p, :], io["slots_x"][bass.ds(e * CAP, CAP), :]).then_inc(w_in[p].sem, 16)

        @block.tensor
        def _(pe):
            with pe.Fori(0, EXPERTS // 2) as it:
                for p in range(2):
                    e = 2 * it + p
                    pe.wait_ge(w_in[p].sem, 32 * (it + 1))
                    pe.wait_ge(y_copied.sem, e + 1)
                    for c in range(C):
                        m = pe.transpose(k.ps[:, p, c * P:(c + 1) * P], xe[:, p, c * P:(c + 1) * P], k.ident[:, :])
                    m.then_inc(xT_filled.sem, 1)
                    pe.wait_ge(xT_copied.sem, e + 1)
                    for u in range(2):
                        m = project(pe, k.ps[:, 2 + 2 * u + p, 0:P],
                                    lambda c: w[:, p, u * D + c * P:u * D + (c + 1) * P], lambda c: xeT[:, p, c, :])
                        m.then_inc(gu_filled.sem, 1)
                    pe.wait_ge(h_done.sem, e + 1)
                    pe.matmul(k.ps[:, 6 + p, :], he[:, p, :], w[:, p, 2 * D:3 * D], start=True, stop=True)\
                      .then_inc(y_filled.sem, 1)

        @block.scalar
        def _(act):
            with act.Fori(0, EXPERTS // 2) as it:
                for p in range(2):
                    e = 2 * it + p
                    act.wait_ge(gu_filled.sem, 2 * e + 1)
                    act.activation(ge[:, p, :], k.ps[:, 2 + p, 0:P], ACT.Silu).then_inc(g_done.sem, 1)
                    act.wait_ge(y_filled.sem, e + 3)
                    act.wait_ge(y_out[p].sem, 16 * it + 1)
                    act.activation(ye[:, p, :], k.ps[:, 6 + p, :], ACT.Copy).then_inc(y_copied.sem, 1)
                    act.wait_ge(y_copied.sem, e + 3)
                    act.dma_start(io["slots_y"][bass.ds(e * CAP, CAP), :], ye[:, p, :]).then_inc(y_out[p].sem, 16)
            for p in range(2):
                act.wait_ge(y_out[p].sem, 16 * (EXPERTS // 2) + 1)

        @block.vector
        def _(dve):
            with dve.Fori(0, EXPERTS // 2) as it:
                for p in range(2):
                    e = 2 * it + p
                    dve.wait_ge(xT_filled.sem, e + 1)
                    dve.tensor_copy(xeT[:, p, :, :], k.ps[:, p, :].rearrange("p (c n) -> p c n", c=C))\
                       .then_inc(xT_copied.sem, 1)
                    dve.wait_ge(gu_filled.sem, 2 * e + 2)
                    dve.wait_ge(g_done.sem, e + 1)
                    dve.tensor_tensor(he[:, p, :], k.ps[:, 4 + p, 0:P], ge[:, p, :], ALU.mult).then_inc(h_done.sem, 1)

    res, acc = sb("res", [P, 2, TOPK, D]), sb("acc2", [P, 2, D])
    fetched = [Tally(nc, ctx, f"fetched{n}") for n in range(2)]
    summed, acc_turned, added = Tally(nc, ctx, "summed"), Tally(nc, ctx, "acc_turned"), Tally(nc, ctx, "added")
    with nc.Block() as block:
        def add_back(dve, t):
            dve.wait_ge(acc_turned.sem, t + 1)
            xs = k.x[:, :, t * P:(t + 1) * P]
            dve.tensor_tensor(xs, xs, k.ps[:, t % 2, :].rearrange("p (c n) -> p c n", c=C), ALU.add)\
               .then_inc(added.sem, 1)

        @block.gpsimd
        def _(pool):
            for t in range(TT):
                if t >= 2:
                    pool.wait_ge(summed.sem, 4 * (t - 1))
                for c in range(TOPK):
                    pool.indirect_dma_start(
                        out=res[:, t % 2, c, :], out_offset=None, in_=io["slots_y"],
                        in_offset=bass.IndirectOffsetOnAxis(ap=slot_out[:, c, t:t + 1], axis=0),
                        bounds_check=SLOTS - 1, oob_is_err=False).then_inc(fetched[t % 2].sem, 16)

        @block.vector
        def _(dve):
            for t in range(TT):
                dve.wait_ge(fetched[t % 2].sem, 16 * TOPK * (t // 2 + 1))
                if t >= 2:
                    dve.wait_ge(acc_turned.sem, t - 1)
                a = acc[:, t % 2, :]
                dve.tensor_scalar(a, res[:, t % 2, 0, :], share[:, 0, t:t + 1], None, ALU.mult).then_inc(summed.sem, 1)
                for c in range(1, TOPK):
                    dve.wait_ge(summed.sem, 4 * t + c)
                    dve.scalar_tensor_tensor(a, res[:, t % 2, c, :], share[:, c, t:t + 1], a, ALU.mult, ALU.add)\
                       .then_inc(summed.sem, 1)
                if t >= 1:
                    add_back(dve, t - 1)
            add_back(dve, TT - 1)

        @block.tensor
        def _(pe):
            for t in range(TT):
                pe.wait_ge(summed.sem, 4 * (t + 1))
                if t >= 2:
                    pe.wait_ge(added.sem, t - 1)
                for c in range(C):
                    m = pe.transpose(k.ps[:, t % 2, c * P:(c + 1) * P], acc[:, t % 2, c * P:(c + 1) * P],
                                     k.ident[:, :])
                m.then_inc(acc_turned.sem, 1)


def clear_slots(core):
    nc, k = core.nc, core
    with ExitStack() as ctx:
        zero = ctx.enter_context(nc.sbuf_tensor("zero", [P, D], F32))
        cleared, zeroed = Tally(nc, ctx, "cleared"), Tally(nc, ctx, "zeroed")
        with nc.Block() as block:
            @block.vector
            def _(dve):
                dve.memset(zero[:, :], 0.0).then_inc(zeroed.sem, 1)

            @block.sync
            def _(sp):
                sp.wait_ge(zeroed.sem, 1)
                for n in range(4):
                    sp.dma_start(k.io["slots_x"][n * SLOTS // 4:(n + 1) * SLOTS // 4, :]
                                 .rearrange("(p s) n -> p s n", p=P),
                                 zero[:, :].unsqueeze(1).to_broadcast([P, SLOTS // 4 // P, D]))\
                      .then_inc(cleared.sem, 16)
                sp.wait_ge(cleared.sem, 64)


def layer3(core):
    nc, k, io = core.nc, core, core.io
    with ExitStack() as ctx:
        def sb(name, shape, dt=F32):
            return ctx.enter_context(nc.sbuf_tensor(name, shape, dt))

        v_all = sb("v3_all", [P, TT, D])
        v_one = sb("v3_one", [P, TT, 32])
        with ExitStack() as inner:
            layer3_blocks(core, inner, v_all, v_one)
        attention(core, "3", 16, 32, io["q3_parts"], io["k3_parts"], v_all, io["o3"])
        attention(core, "4", 16, 32, io["q4_parts"], io["k4_parts"], v_one, io["o4"], shared=True)
        w_out, b_out = sb("w_out3", [P, C, D]), sb("b_out3", [P, C])
        project_out(core, ctx, "3", io["o3"], io["o4"], w_out, b_out,
                    [(w_out[:, :, :], io["L3_wo"]), (b_out[:, :], io["L3_bo"])], io["out"])


def layer3_blocks(core, ctx, v_all, v_one):
    nc, k, io = core.nc, core, core.io

    def sb(name, shape, dt=F32):
        return ctx.enter_context(nc.sbuf_tensor(name, shape, dt))

    HEADS, DH = 16, 32
    SCALE = float(1.0 / np.sqrt(np.float32(DH)))
    TAKEN, NONE = -7.0, -5.0
    wa, ba = sb("wa3", [P, 2, C, D]), sb("ba3", [P, 2, C])
    wv, bv = sb("wv3", [P, C, D]), sb("bv3", [P, D])
    wf, wg = sb("wf3", [P, 3, C, D]), sb("wg3", [P, C, HEADS])
    rot = sb("rot3", [P, P])
    norm = Norm(core, ctx, 3)
    split = Split(core, ctx, "3", 13)
    plain = sb("plain3", [P, 4, TB])
    turned_, mixed = sb("turned3", [P, TB]), sb("mixed3", [P, 2, TB])
    fq = sb("fq", [P, 2, TB])
    wave = sb("wave3", [P, 2, TB])
    gate, gexp = sb("gate3", [P, TPB, HEADS]), sb("gexp3", [P, TPB, HEADS])
    gsum, ginv = sb("gsum3", [P, TPB]), sb("ginv3", [P, TPB])
    prob, left = sb("gprob3", [P, TPB, HEADS + 8]), sb("gleft3", [P, TPB, HEADS + 8])
    best, taken = sb("gbest3", [P, TPB, 8]), sb("gtaken3", [P, TPB, 8])
    pick = sb("pick3", [P, 2, TPB, HEADS])
    prod = sb("prod3", [P, D])
    hop = sb("hop3", [P, 2])
    k_one, kT = sb("k_one3", [P, TPB, DH]), sb("kT3", [DH, TB])
    wave_in, mixed_ready, g_exp = Tally(nc, ctx, "wave_in3"), Tally(nc, ctx, "mixed_ready3"), Tally(nc, ctx, "g_exp3")
    k_ready = Tally(nc, ctx, "k_ready3")

    order = ["p0", "p1", "p2", "p3", "r0", "r1", "p4", "p5", "r2", "r3", "p6", "p7", "r4", "r5", "gate", "r6", "r7"]
    order += [f"{n}{t}" for t in range(TPB) for n in "kv"]
    order += [f"f{n}" for n in range(C)] + ["kT"] + [f"V{t}" for t in range(TPB)]
    at = {n: g for g, n in enumerate(order)}
    grp = Groups(core, "".join("a" if n[0] in "pf" or n == "kT" else "v" for n in order))
    chain = Chain(k.v_chain)
    per_block = 31

    with nc.Block() as block:
        def choose(dve, b):
            g = at["gate"]
            grp.wait_filled(dve, b, g)
            logits = k.ps[:, grp.bank(g), 0:TPB * HEADS].rearrange("p (t h) -> p t h", t=TPB)
            chain.link(dve.tensor_reduce(gsum[:, :], logits, X_AXIS, ALU.max))
            dve.tensor_tensor(gate[:, :, :], logits, gsum[:, :].unsqueeze(2).to_broadcast([P, TPB, HEADS]),
                              ALU.subtract).then_inc(k.emptied_v.sem, 1)
            dve.wait_ge(g_exp.sem, b + 1)
            chain.link(dve.tensor_reduce(gsum[:, :], gexp[:, :, :], X_AXIS, ALU.add))
            chain.link(dve.reciprocal(ginv[:, :], gsum[:, :]))
            chain.link(dve.tensor_tensor(prob[:, :, 0:HEADS], gexp[:, :, :],
                                         ginv[:, :].unsqueeze(2).to_broadcast([P, TPB, HEADS]), ALU.mult))
            dve.memset(hop[:, 0:1], 0.0)
            for t in range(TPB):
                chain.mark(dve.max(best[:, t, :], prob[:, t, 0:HEADS]))
            dve.wait_ge(k.v_chain.sem, chain.at + chain.n)
            chain.link(dve.tensor_copy(taken[:, :, 0:1], best[:, :, 0:1]))
            dve.memset(hop[:, 1:2], 0.0)
            for t in range(TPB):
                chain.mark(dve.match_replace(left[:, t, :], taken[:, t, :], prob[:, t, :], TAKEN))
            dve.wait_ge(k.v_chain.sem, chain.at + chain.n)
            chain.link(dve.tensor_scalar(pick[:, 0, :, :], left[:, :, 0:HEADS], NONE - 1.0, None, ALU.is_lt))
            chain.link(dve.tensor_tensor(pick[:, 1, :, :], pick[:, 0, :, :],
                                         best[:, :, 0:1].to_broadcast([P, TPB, HEADS]), ALU.mult))

        @block.sync
        def _(sp):
            load(sp, core, [(wa[:, :, :, :], io["L3_wqk"]), (ba[:, :, :], io["L3_bqk"]), (rot[:, :], io["L3_rot"]),
                            (wg[:, :, :], io["L3_wg"]), (wf[:, :, :, :], io["L3_wf"]), (wv[:, :, :], io["L3_wv"]),
                            (bv[:, :], io["L3_bv"].partition_broadcast(P))])
            with sp.Fori(0, NB) as b:
                for n in range(8):
                    dst = io["q3_parts"] if n % 2 == 0 else io["k3_parts"]
                    split.store(sp, b, n, dst[:, n // 2 * P:(n // 2 + 1) * P, :], after={0: 1, 1: None}.get(n, 0))
                for n in range(C):
                    split.store(sp, b, 8 + n, io["q4_parts"][:, n * P:(n + 1) * P, :])
                split.store(sp, b, 12, io["k4_parts"], DH)
            split.wait_stores(sp)

        @block.tensor
        def _(pe):
            pe.wait_ge(k.loaded.sem, k.loaded.base)
            with pe.Fori(0, NB) as b:
                grp.wait_block(pe, b)
                norm.tensor(pe, b)
                for g, name in enumerate(order):
                    grp.wait_free(pe, b, g)
                    out, n = k.ps[:, grp.bank(g), :], int(name[1]) if name[1].isdigit() else 0
                    tile = slice(n * P, (n + 1) * P)
                    if name[0] == "p":
                        oc = n // 2
                        m = project(pe, out, lambda c: wa[:, n % 2, c, oc * P:(oc + 1) * P],
                                    lambda c: norm.xn[:, c, :])
                    elif name[0] == "r":
                        grp.wait_emptied(pe, b, at[f"p{n}"])
                        m = pe.matmul(out, rot[:, :], plain[:, n % 4, :], start=True, stop=True)
                    elif name == "gate":
                        for t in range(TPB):
                            m = project(pe, k.ps[:, grp.bank(g), t * HEADS:(t + 1) * HEADS],
                                        lambda c: norm.xn[:, c, t * P:(t + 1) * P], lambda c: wg[:, c, :])
                    elif name == "kT":
                        pe.wait_ge(k_ready.sem, b + 1)
                        for t in range(TPB):
                            m = pe.transpose(k.ps[0:DH, grp.bank(g), t * P:(t + 1) * P], k_one[:, t, :], k.ident[:, :])
                    elif name[0] in "kv":
                        u = 1 + "kv".index(name[0])
                        m = project(pe, out, lambda c: norm.xn[:, c, tile], lambda c: wf[:, u, c, :])
                    elif name[0] == "f":
                        m = project(pe, out, lambda c: wf[:, 0, c, tile], lambda c: norm.xn[:, c, :])
                    else:
                        m = project(pe, out, lambda c: norm.xn[:, c, tile], lambda c: wv[:, c, :])
                    m.then_inc(k.filled.sem, 1)

        @block.scalar
        def _(act):
            with act.Fori(0, NB) as b:
                grp.wait_block(act, b)
                act.dma_start(wave[:, :, :], io["L3_wave"][:, :, bass.ds(b * TB, TB)]).then_inc(wave_in.sem, 16)
                norm.scalar(act, b)

                def take(n):
                    g = at[f"p{n}"]
                    if n >= 4:
                        grp.wait_emptied(act, b, at[f"r{n - 4}"])
                    grp.wait_filled(act, b, g)
                    act.activation(plain[:, n % 4, :], k.ps[:, grp.bank(g), :], ACT.Identity,
                                   bias=ba[:, n % 2, n // 2:n // 2 + 1]).then_inc(k.emptied_a.sem, 1)

                def parts(n):
                    act.wait_ge(mixed_ready.sem, 8 * b + n + 1)
                    split.scalar_1(act, b, n, mixed[:, n % 2, :], SCALE if n % 2 == 0 else 1.0)
                    split.scalar_2(act, b, n)

                for n in range(4):
                    take(n)
                for n in range(8):
                    parts(n)
                    if n % 2 == 1 and n < 4:
                        take(n + 3)
                        take(n + 4)
                    if n == 5:
                        grp.wait_emptied(act, b, at["gate"])
                        act.activation(gexp[:, :, :], gate[:, :, :], ACT.Exp).then_inc(g_exp.sem, 1)
                for n in range(C):
                    g = at[f"f{n}"]
                    grp.wait_filled(act, b, g)
                    act.activation(fq[:, n % 2, :], k.ps[:, grp.bank(g), :], ACT.Copy).then_inc(k.emptied_a.sem, 1)
                    grp.wait_emptied(act, b, g)
                    split.scalar_1(act, b, 8 + n, fq[:, n % 2, :], SCALE)
                    split.scalar_2(act, b, 8 + n)
                grp.wait_filled(act, b, at["kT"])
                act.activation(kT[:, :], k.ps[0:DH, grp.bank(at["kT"]), :], ACT.Copy).then_inc(k.emptied_a.sem, 1)
                grp.wait_emptied(act, b, at["kT"])
                split.scalar_1(act, b, 12, kT[:, :], 1.0, DH)
                split.scalar_2(act, b, 12, DH)

        @block.vector
        def _(dve):
            split.prime(dve)
            chain.start(dve)
            chain.link(dve.memset(prob[:, :, HEADS:], NONE))
            chain.link(dve.memset(taken[:, :, :], NONE))
            dve.wait_ge(k.loaded.sem, k.loaded.base)
            with dve.Fori(0, NB) as b:
                norm.vector(dve, b)
                chain.start(dve, 2 + b * per_block)
                dve.wait_ge(wave_in.sem, 16 * (b + 1))
                for n in range(8):
                    grp.wait_emptied(dve, b, at[f"p{n}"])
                    chain.mark(dve.tensor_tensor(mixed[:, n % 2, :], plain[:, n % 4, :], wave[:, 0, :], ALU.mult))
                    g = at[f"r{n}"]
                    grp.wait_filled(dve, b, g)
                    dve.tensor_tensor(turned_[:, :], k.ps[:, grp.bank(g), :], wave[:, 1, :], ALU.mult)\
                       .then_inc(k.emptied_v.sem, 1)
                    grp.wait_emptied(dve, b, g)
                    dve.wait_ge(k.v_chain.sem, chain.at + chain.n)
                    dve.tensor_tensor(mixed[:, n % 2, :], mixed[:, n % 2, :], turned_[:, :], ALU.add)\
                       .then_inc(mixed_ready.sem, 1)
                    split.vector_1(dve, b, n, mixed[:, n % 2, :], SCALE if n % 2 == 0 else 1.0)
                    split.vector_2(dve, b, n)
                    if n == 5:
                        choose(dve, b)
                for t in range(TPB):
                    for u, name in enumerate("kv"):
                        g = at[f"{name}{t}"]
                        grp.wait_filled(dve, b, g)
                        dve.tensor_tensor(prod[:, :].rearrange("p (h d) -> p h d", d=DH),
                                          k.ps[:, grp.bank(g), :].rearrange("p (h d) -> p h d", d=DH),
                                          pick[:, u, t, :].unsqueeze(2).to_broadcast([P, HEADS, DH]), ALU.mult)\
                           .then_inc(k.emptied_v.sem, 1)
                        grp.wait_emptied(dve, b, g)
                        dst = k_one[:, t:t + 1, :] if u == 0 else v_one[:, bass.ds(b * TPB + t, 1), :]
                        chain.link(dve.tensor_reduce(dst.rearrange("p a d -> p (a d)"),
                                                     prod[:, :].rearrange("p (h d) -> p d h", d=DH), X_AXIS, ALU.add))
                dve.memset(gsum[:, 0:1], 0.0).then_inc(k_ready.sem, 1)
                for n in range(C):
                    split.vector_1(dve, b, 8 + n, fq[:, n % 2, :], SCALE)
                    split.vector_2(dve, b, 8 + n)
                split.vector_1(dve, b, 12, kT[:, :], 1.0, DH)
                split.vector_2(dve, b, 12, DH)
                for t in range(TPB):
                    g = at[f"V{t}"]
                    grp.wait_filled(dve, b, g)
                    dve.tensor_tensor(v_all[:, bass.ds(b * TPB + t, 1), :].rearrange("p a d -> p (a d)"),
                                      k.ps[:, grp.bank(g), :], bv[:, :], ALU.add).then_inc(k.emptied_v.sem, 1)
                assert chain.n == per_block, chain.n
    grp.close()
    split.close()
    k.v_chain.base += 2 + NB * per_block


def program(nc, io, upto=4, start=0):
    def scratch(name, shape, dt=BF16):
        io[name] = nc.dram_tensor(name, shape, dt, kind="Internal").ap()

    scratch("q1_parts", (3, P, T))
    scratch("m_rows", (3, T))
    scratch("k1_parts", (3, P, T))
    scratch("slots_x", (SLOTS, D), F32)
    scratch("slots_y", (SLOTS, D), F32)
    for n in "34":
        scratch(f"q{n}_parts", (3, D, T))
        scratch(f"k{n}_parts", (3, D if n == "3" else 32, T))
        scratch("o" + n, (D, T), F32)
    scratch("o1", (P, T), F32)
    with ExitStack() as ctx:
        core = Core(nc, ctx, io)
        core.start = start
        setup(core)
        clear_slots(core)
        for n, layer in enumerate((layer0, layer1, layer2, layer3)):
            if start <= n < upto:
                layer(core)
        if upto < 4:
            dump(core)


def dump(core):
    nc, k = core.nc, core
    with nc.Block() as block:
        @block.sync
        def _(sp):
            sp.dma_start(k.io["out"].rearrange("(c p) t -> p c t", p=P), k.x[:, :, :]).then_inc(k.stored.sem, 16)
            sp.wait_ge(k.stored.sem, k.stored.base + 16)


def columns(v):
    return np.ascontiguousarray(v.reshape(-1, P).T)


def chunked(w):
    o, i = w.shape
    return np.ascontiguousarray(w.T.reshape(i // P, P, o).transpose(1, 0, 2))


def layout(inputs):
    a = {n: np.asarray(v) for n, v in inputs.items()}
    out = {"xT": np.ascontiguousarray(a["L0_attn_x"][0].T), "L0_ffn_lut": a["L0_ffn_lut"]}
    out["L0_w"] = np.stack([chunked(a["L0_attn_W" + n]) for n in "vkgq"], 1)
    out["L0_b"] = np.stack([columns(a["L0_attn_b" + n]) for n in "vkgq"], 1)
    idx = np.zeros((P, 24 * PIECE), np.int32)
    for n, name in enumerate(("gate", "up")):
        w = idx[:, n * C * H1:(n + 1) * C * H1].reshape(P, C, H1)
        w[:, :, :H0] = chunked(a[f"L0_ffn_{name}_idx"])
    w = idx[:, 2 * C * H1:2 * C * H1 + J0 * D].reshape(P, J0, D)
    down = np.zeros((J0 * P, D), np.int32)
    down[:H0] = a["L0_ffn_down_idx"].T
    w[:, :, :] = down.reshape(J0, P, D).transpose(1, 0, 2)
    out["L0_idx"] = idx.reshape(P, 24, PIECE)
    out["L1_w"] = np.stack([chunked(a[f"L1_attn_{n}_w"]) for n in ("CQR", "CKV", "CKR")], 1)
    out["L1_b"] = np.stack([a[f"L1_attn_{n}_b"] for n in ("CQR", "CKV", "CKR")], 1)
    out["L1_cv_w"], out["L1_cv_b"] = np.ascontiguousarray(a["L1_attn_CV_w"].T), a["L1_attn_CV_b"]
    out["L1_out_w"], out["L1_out_b"] = np.ascontiguousarray(a["L1_attn_OUT_w"].T), columns(a["L1_attn_OUT_b"])
    out["L1_wq"] = np.concatenate([chunked(a["L1_ffn_wq_" + n]).reshape(P, 4, H1) for n in ("gate", "up", "down")], 1)
    out["L1_s_hid"] = np.stack([columns(a["L1_ffn_s_gate"]), columns(a["L1_ffn_s_up"])], 1)
    out["L1_s_down"] = columns(a["L1_ffn_s_down"])
    out["L2_wr"], out["L2_br"] = chunked(a["L2_ffn_Wr"].T), a["L2_ffn_router_bias"]
    out["L2_wv"], out["L2_wo"] = chunked(a["L2_attn_weight_qkv"][2 * D:]), chunked(a["L2_attn_weight_out"])
    for n, name in (("L2_sg", "L2_ffn_Sg"), ("L2_su", "L2_ffn_Su")):
        out[n] = chunked(a[name].transpose(0, 2, 1).reshape(JS * P, D))
    out["L2_sd"] = chunked(a["L2_ffn_Sd"].reshape(JS * P, D).T)
    we = [a["L2_ffn_" + n].reshape(EXPERTS, C, P, HX).transpose(0, 2, 1, 3).reshape(EXPERTS, P, D)
          for n in ("Wg", "Wu")]
    out["L2_we"] = np.concatenate(we + [a["L2_ffn_Wd"]], 2)
    out["L3_wqk"] = np.stack([chunked(a["L3_attn_W" + n]) for n in "qk"], 1)
    out["L3_bqk"] = np.stack([columns(a["L3_attn_b" + n]) for n in "qk"], 1)
    out["L3_wv"], out["L3_bv"] = chunked(a["L3_attn_Wv"]), a["L3_attn_bv"]
    out["L3_wo"], out["L3_bo"] = chunked(a["L3_attn_Wo"]), columns(a["L3_attn_bo"])
    out["L3_wg"] = chunked(a["L3_ffn_W_gate"])
    out["L3_wf"] = np.stack([chunked(a["L3_ffn_W_qkv"][n * D:(n + 1) * D]) for n in range(3)], 1)
    freq = (1.0 / 10000.0 ** (np.arange(16, dtype=np.float32) / 16)).astype(np.float32)
    angle = np.tile(np.repeat(np.outer(np.arange(T, dtype=np.float32), freq), 2, 1), (1, 4)).T
    out["L3_wave"] = np.ascontiguousarray(np.stack([np.cos(angle), np.sin(angle)], 1).astype(np.float32))
    rot = np.zeros((P, P), np.float32)
    for f in range(0, P, 2):
        rot[f + 1, f], rot[f, f + 1] = -1.0, 1.0
    out["L3_rot"] = rot
    freq = (1.0 / 10000.0 ** (np.arange(0, P, 2, dtype=np.float32) / P)).astype(np.float32)
    angle = np.tile(np.outer(np.arange(T, dtype=np.float32), freq), (1, 2)).T
    out["L1_wave"] = np.ascontiguousarray(np.stack([np.cos(angle), np.sin(angle)], 1).astype(np.float32))
    rot = np.zeros((P, P), np.float32)
    for f in range(P // 2):
        rot[f + P // 2, f], rot[f, f + P // 2] = -1.0, 1.0
    out["L1_rot"] = rot
    return out


def kernel(**inputs):
    import concourse.bacc as bacc
    from concourse.bass_utils import run_bass_kernel_spmd

    nc = bacc.Bacc("TRN2", target_bir_lowering=False, num_devices=1)
    arrays = {f"in_{n}": v for n, v in layout(inputs).items()}
    io = {n[3:]: nc.dram_tensor(n, v.shape, mybir.dt.from_np(v.dtype), kind="ExternalInput").ap()
          for n, v in arrays.items()}
    io["out"] = nc.dram_tensor("out", (D, T), F32, kind="ExternalOutput").ap()
    program(nc, io)
    result = run_bass_kernel_spmd(nc, [arrays], core_ids=[0]).results[0]["out"]
    return np.ascontiguousarray(result.T)[None]
```

```python
import numpy as np
import concourse.bass as bass
from concourse import mybir
from contextlib import ExitStack

F32, BF16, F16 = mybir.dt.float32, mybir.dt.bfloat16, mybir.dt.float16
I32, U32 = mybir.dt.int32, mybir.dt.uint32
ALU = mybir.AluOpType
ACT = mybir.ActivationFunctionType
X_AXIS = mybir.AxisListType.X

P = 128
T = 2048
D = 512
C = D // P
TB = 512
NB = T // TB
TT = T // P
TPB = TB // P
H0 = 1376
H1 = 1408
J0 = -(-H0 // P)
J1 = H1 // P
LUT = 16
LOOKUP = 264
LOOKUPS = 3 * C * H1 // LOOKUP
EXPERTS, TOPK, CAP = 64, 4, 128
HX = 128
JS = 8
SLOTS = EXPERTS * CAP
EPS = 1e-5
NEG = -3.0e38
BANKS = 8
SHIFT = float(10 * np.log(2))


class Tally:

    def __init__(self, nc, ctx, name, base=0):
        self.sem = ctx.enter_context(nc.semaphore(name))
        self.base = base


class Chain:

    def __init__(self, tally):
        self.tally, self.engine, self.n = tally, None, 0

    def start(self, engine, passed=0):
        self.engine, self.at, self.n = engine, self.tally.base + passed, 0

    def link(self, ins):
        ins.then_inc(self.tally.sem, 1)
        self.n += 1
        self.engine.wait_ge(self.tally.sem, self.at + self.n)

    def mark(self, ins):
        ins.then_inc(self.tally.sem, 1)
        self.n += 1


class Groups:

    def __init__(self, core, kinds, ring=BANKS):
        self.kinds, self.core, self.ring = kinds, core, ring
        self.total = {e: kinds.count(e) for e in "av"}
        self.filled0 = core.filled.base
        self.base = {"a": core.emptied_a.base, "v": core.emptied_v.base}

    def bank(self, g):
        return (g + 2) % BANKS if self.ring == BANKS else 2 + g % self.ring

    def wait_free(self, pe, b, g):
        if g >= self.ring:
            self.wait_emptied(pe, b, g - self.ring)

    def wait_emptied(self, eng, b, g):
        e = self.kinds[g]
        tally = self.core.emptied_a if e == "a" else self.core.emptied_v
        eng.wait_ge(tally.sem, self.base[e] + b * self.total[e] + self.kinds[:g + 1].count(e))

    def wait_filled(self, eng, b, g):
        eng.wait_ge(self.core.filled.sem, self.filled0 + b * len(self.kinds) + g + 1)

    def wait_block(self, eng, b):
        eng.wait_ge(self.core.emptied_v.sem, self.base["v"] + b * self.total["v"])

    def close(self):
        self.core.filled.base += NB * len(self.kinds)
        self.core.emptied_a.base += NB * self.total["a"]
        self.core.emptied_v.base += NB * self.total["v"]


class Core:

    def __init__(self, nc, ctx, io):
        self.nc, self.io = nc, io

        def sb(name, shape, dt=F32):
            return ctx.enter_context(nc.sbuf_tensor(name, shape, dt))

        self.x = sb("x", [P, C, T])
        self.ident = sb("ident", [P, P])
        self.ident_b = sb("ident_b", [P, P], BF16)
        self.mask_b, self.maskT_b = sb("mask_b", [P, P], BF16), sb("maskT_b", [P, P], BF16)
        self.mean_w = sb("mean_w", [P, P])
        self.ones = sb("ones", [P, TB])
        self.eps = sb("eps", [P, 1])
        self.ps = ctx.enter_context(nc.psum_tensor("ps", [P, BANKS, 512], F32))

        def tally(name, base=0):
            return Tally(nc, ctx, name, base)

        self.loaded, self.loaded_first = tally("loaded"), tally("loaded_first")
        self.stored = tally("stored", 1)
        self.const = tally("const")
        self.filled = tally("filled")
        self.emptied_a = tally("emptied_a", 1)
        self.emptied_v = tally("emptied_v", 1)
        self.v_chain, self.a_chain = tally("v_chain"), tally("a_chain")
        self.ln_mean, self.ln_centred, self.ln_squared = tally("ln_mean"), tally("ln_centred"), tally("ln_squared")
        self.ln_var, self.ln_std, self.ln_rstd, self.xn_ready = (
            tally("ln_var"), tally("ln_std"), tally("ln_rstd"), tally("xn_ready"))
        self.split_a, self.split_v = tally("split_a"), tally("split_v")


class Norm:

    def __init__(self, core, ctx, layer, buffers=1):
        self.core, self.layer = core, layer
        nc = core.nc

        def sb(name, shape):
            return ctx.enter_context(nc.sbuf_tensor(f"{name}{layer}", shape, F32))

        self.xc = sb("xc", [P, C, TB])
        self.std = sb("std", [P, TB])
        self.rstd = sb("rstd", [P, TB])
        self.both = [sb(f"xn_{n}_", [P, C, TB]) for n in range(buffers)]
        self.xn = self.both[0]

    def xn_of(self, p):
        return self.both[p % len(self.both)]

    def count(self, b):
        return NB * (self.layer - self.core.start) + b + 1

    def tensor(self, pe, b):
        self.tensor_mean(pe, b)
        self.tensor_var(pe, b)
        self.wait_ready(pe, b)

    def wait_ready(self, pe, b):
        pe.wait_ge(self.core.xn_ready.sem, self.count(b))

    def tensor_mean(self, pe, b):
        k = self.core
        for c in range(C):
            m = pe.matmul(k.ps[:, 0, :], k.mean_w[:, :], k.x[:, c, bass.ds(b * TB, TB)],
                          start=c == 0, stop=c == C - 1)
        m.then_inc(k.ln_mean.sem, 1)

    def tensor_var(self, pe, b, p=0):
        k = self.core
        pe.wait_ge(k.ln_squared.sem, self.count(b))
        for c in range(C):
            m = pe.matmul(k.ps[:, 1, :], k.mean_w[:, :], self.xn_of(p)[:, c, :], start=c == 0, stop=c == C - 1)
        m.then_inc(k.ln_var.sem, 1)

    def scalar(self, act, b, meanwhile=None, p=0):
        k = self.core
        act.wait_ge(k.ln_centred.sem, self.count(b))
        act.activation(self.xn_of(p)[:, :, :], self.xc[:, :, :], ACT.Square).then_inc(k.ln_squared.sem, 1)
        if meanwhile:
            meanwhile()
        act.wait_ge(k.ln_var.sem, self.count(b))
        act.activation(self.std[:, :], k.ps[:, 1, :], ACT.Sqrt, bias=k.eps[:, 0:1]).then_inc(k.ln_std.sem, 1)

    def vector(self, dve, b, meanwhile=None, p=0):
        k = self.core
        dve.wait_ge(k.ln_mean.sem, self.count(b))
        dve.tensor_tensor(self.xc[:, :, :], k.x[:, :, bass.ds(b * TB, TB)],
                          k.ps[:, 0, :].unsqueeze(1).to_broadcast([P, C, TB]), ALU.subtract)\
           .then_inc(k.ln_centred.sem, 1)
        if meanwhile:
            meanwhile()
        dve.wait_ge(k.ln_std.sem, self.count(b))
        dve.reciprocal(self.rstd[:, :], self.std[:, :]).then_inc(k.ln_rstd.sem, 1)
        dve.wait_ge(k.ln_rstd.sem, self.count(b))
        dve.wait_ge(k.ln_centred.sem, self.count(b))
        dve.tensor_tensor(self.xn_of(p)[:, :, :], self.xc[:, :, :],
                          self.rstd[:, :].unsqueeze(1).to_broadcast([P, C, TB]), ALU.mult)\
           .then_inc(k.xn_ready.sem, 1)


def each_block(eng, body, first_apart=False):
    if first_apart:
        body(0, True)
    with eng.Fori(int(first_apart), NB - 1) as b:
        body(b, True)
    body(NB - 1, False)


def each_pair(eng, body):
    with eng.Fori(0, NB // 2 - 1) as it:
        for p in range(2):
            body(2 * it + p, p, True)
    for p in range(2):
        body(NB - 2 + p, p, p == 0)


def project(pe, out, weights, moving, chunks=C):
    for c in range(chunks):
        m = pe.matmul(out, weights(c), moving(c), start=c == 0, stop=c == chunks - 1)
    return m


def tokens(core, b):
    return core.io["xT"].rearrange("(c p) t -> p c t", p=P)[:, :, b * TB:(b + 1) * TB]


def load(eng, core, pairs, first=False):
    tally = core.loaded_first if first else core.loaded
    for dst, src in pairs:
        eng.dma_start(dst, src).then_inc(tally.sem, 16)
    tally.base += 16 * len(pairs)


def setup(core):
    nc, k = core.nc, core
    with nc.Block() as block:
        @block.sync
        def _(sp):
            load(sp, k, [(k.x[:, :, 0:TB], tokens(k, 0))], first=True)

        @block.vector
        def _(dve):
            dve.memset(k.mean_w[:, :], 1.0 / D).then_inc(k.emptied_v.sem, 1)
            dve.memset(k.ones[:, :], 1.0).then_inc(k.emptied_a.sem, 1)
            dve.memset(k.eps[:, :], EPS).then_inc(k.stored.sem, 1)
            dve.wait_ge(k.const.sem, 6)
            dve.tensor_copy(k.ident_b[:, :], k.ident[:, :]).then_inc(k.const.sem, 1)

        @block.gpsimd
        def _(pool):
            pool.memset(k.ident[:, :], 0.0).then_inc(k.const.sem, 1)
            pool.memset(k.mask_b[:, :], 0.0).then_inc(k.const.sem, 1)
            pool.memset(k.maskT_b[:, :], 0.0).then_inc(k.const.sem, 1)
            pool.wait_ge(k.const.sem, 3)
            pool.affine_select(out=k.ident[:, :], in_=k.ident[:, :], compare_op=ALU.not_equal, fill=1.0,
                               base=0, pattern=[[-1, P]], channel_multiplier=1).then_inc(k.const.sem, 1)
            pool.affine_select(out=k.mask_b[:, :], in_=k.mask_b[:, :], compare_op=ALU.is_ge, fill=NEG,
                               base=0, pattern=[[-1, P]], channel_multiplier=1).then_inc(k.const.sem, 1)
            pool.affine_select(out=k.maskT_b[:, :], in_=k.maskT_b[:, :], compare_op=ALU.is_ge, fill=NEG,
                               base=0, pattern=[[1, P]], channel_multiplier=-1).then_inc(k.const.sem, 1)


def layer0(core):
    with ExitStack() as ctx:
        wf = ctx.enter_context(core.nc.sbuf_tensor("wf", [P, LOOKUPS * LOOKUP], F32))
        with ExitStack() as inner:
            layer0_attention(core, inner, wf)
        with ExitStack() as inner:
            layer0_ffn(core, inner, wf)


def layer0_attention(core, ctx, wf):
    nc, k, io = core.nc, core, core.io
    BLOCK = LOOKUPS // NB
    FIRST = BLOCK - 3 * C - 1
    START = [FIRST, FIRST + 4, FIRST + 7, FIRST + 10, BLOCK]
    AHEAD = 4
    assert LOOKUPS % NB == 0 and BLOCK % AHEAD == 0

    def sb(name, shape, dt=F32):
        return ctx.enter_context(nc.sbuf_tensor(name, shape, dt))

    def tally(name, base=0):
        return Tally(nc, ctx, name, base)

    wa = sb("wa", [P, 4, C, D])
    ba = sb("ba", [P, 4, C])
    norm = Norm(core, ctx, 0)
    carry = sb("carry", [P, C])
    v_sb, g_sb = sb("v_sb", [P, 2, TB]), sb("g_sb", [P, 2, TB])
    kv, kvs, qg = sb("kv", [P, TB]), sb("kvs", [P, TB]), sb("qg", [P, TB])
    table, step = sb("table", [P, LUT]), sb("step", [P, LUT // 2])
    idx = sb("idx", [P, AHEAD, LOOKUP], I32)
    bit0, bits = sb("bit0", [P, 2, LOOKUP], I32), sb("bits", [P, 2, 3, LOOKUP], I32)
    cand = sb("cand", [P, 2, 8, LOOKUP])
    hop, note = sb("hop", [P, 1]), sb("note0", [P, 3])
    idx_in = [tally(f"idx_in{n}") for n in range(AHEAD)]
    idx_used, bit0_ready, cand_ready = tally("idx_used"), tally("bit0_ready"), tally("cand_ready")
    x_in, table_in = tally("x_in"), tally("table_in")
    picked, kept, xn_out = tally("picked", 1), tally("kept", 2), tally("xn_out", 1)

    grp = Groups(core, "avav" * C, ring=6)
    per_block = 4 * C
    chain = Chain(k.v_chain)

    with nc.Block() as block:
        @block.sync
        def _(sp):
            def fetch(n, slot):
                src = io["L0_idx"][:, bass.ds(n, 1), :].rearrange("p a n -> p (a n)")
                sp.dma_start(idx[:, slot, :], src).then_inc(idx_in[slot].sem, 16)

            sp.dma_start(table[:, :], io["L0_ffn_lut"].partition_broadcast(P)).then_inc(table_in.sem, 16)
            for n in range(AHEAD):
                fetch(n, n)
            load(sp, core, [(wa[:, :, :, :], io["L0_w"]), (ba[:, :, :], io["L0_b"])])
            for b in range(1, NB):
                sp.dma_start(k.x[:, :, b * TB:(b + 1) * TB], tokens(core, b)).then_inc(x_in.sem, 16)
            with sp.Fori(0, NB) as b:
                sp.wait_ge(k.xn_ready.sem, b + 1)
                sp.dma_start(io["xn_saved"].rearrange("(c p) t -> p c t", p=P)[:, :, bass.ds(b * TB, TB)],
                             norm.xn[:, :, :]).then_inc(xn_out.sem, 16)
                for i in range(BLOCK):
                    sp.wait_ge(idx_used.sem, BLOCK * b + i + 1)
                    fetch(BLOCK * b + (i + AHEAD), i % AHEAD)
            for n in range(AHEAD):
                sp.wait_ge(idx_in[n].sem, 16 * (LOOKUPS // AHEAD + 1))
            sp.wait_ge(xn_out.sem, 16 * NB + 1)

        @block.tensor
        def _(pe):
            def body(b, more):
                norm.tensor_var(pe, b)
                grp.wait_block(pe, b)
                norm.wait_ready(pe, b)
                pe.wait_ge(k.loaded.sem, k.loaded.base)
                for g in range(4 * C):
                    grp.wait_free(pe, b, g)
                    oc, which = g // 4, g % 4
                    project(pe, k.ps[:, grp.bank(g), :], lambda c: wa[:, which, c, oc * P:(oc + 1) * P],
                            lambda c: norm.xn[:, c, :]).then_inc(k.filled.sem, 1)
                if more:
                    pe.wait_ge(x_in.sem, 16 * (NB - 1))
                    norm.tensor_mean(pe, b + 1)

            pe.wait_ge(k.loaded_first.sem, k.loaded_first.base)
            norm.tensor_mean(pe, 0)
            each_block(pe, body)

        @block.scalar
        def _(act):
            def candidates(b, first, end):
                for i in range(first, end):
                    n, p = BLOCK * b + i, i % 2
                    act.wait_ge(bit0_ready.sem, n + 1)
                    act.wait_ge(kept.sem, n + 1)
                    for q in range(8):
                        m = act.activation(cand[:, p, q, :], bit0[:, p, :], ACT.Identity,
                                           bias=table[:, 2 * q:2 * q + 1], scale=step[:, q:q + 1])
                    m.then_inc(cand_ready.sem, 1)

            act.wait_ge(k.v_chain.sem, k.v_chain.base + 2)
            with act.Fori(0, NB) as b:
                act.wait_ge(xn_out.sem, 16 * b + 1)
                norm.scalar(act, b, lambda: candidates(b, 0, FIRST))
                for oc in range(C):
                    candidates(b, START[oc], START[oc + 1])
                    if oc >= 2:
                        grp.wait_emptied(act, b, 4 * (oc - 2) + 3)
                    else:
                        grp.wait_block(act, b)
                    grp.wait_filled(act, b, 4 * oc)
                    act.activation(v_sb[:, oc % 2, :], k.ps[:, grp.bank(4 * oc), :], ACT.Identity,
                                   bias=ba[:, 0, oc:oc + 1]).then_inc(k.emptied_a.sem, 1)
                    grp.wait_filled(act, b, 4 * oc + 2)
                    act.activation(g_sb[:, oc % 2, :], k.ps[:, grp.bank(4 * oc + 2), :], ACT.Sigmoid,
                                   bias=ba[:, 2, oc:oc + 1]).then_inc(k.emptied_a.sem, 1)

        @block.gpsimd
        def _(pool):
            with pool.Fori(0, NB) as b:
                for i in range(BLOCK):
                    n = BLOCK * b + i
                    pool.wait_ge(picked.sem, 4 * n + 5)
                    pool.tensor_copy(wf[:, bass.ds(n * LOOKUP, LOOKUP)], cand[:, i % 2, 0, :]).then_inc(kept.sem, 1)
                    pool.wait_ge(kept.sem, n + 3)

        @block.vector
        def _(dve):
            def mask(n, i):
                p, slot = i % 2, i % AHEAD
                dve.tensor_scalar(bit0[:, p, :], idx[:, slot, :], 1, None, ALU.bitwise_and).then_inc(bit0_ready.sem, 1)
                for q in range(3):
                    m = dve.tensor_scalar(bits[:, p, q, :], idx[:, slot, :], 2 << q, None, ALU.bitwise_and)
                m.then_inc(idx_used.sem, 1)

            def pick(b, first, end):
                for i in range(first, end):
                    n, p = BLOCK * b + i, i % 2
                    dve.wait_ge(picked.sem, 4 * n + 1)
                    if i + 1 < BLOCK:
                        dve.wait_ge(idx_in[(i + 1) % AHEAD].sem, b * (16 * BLOCK // AHEAD) + 16 * ((i + 1) // AHEAD + 1))
                    else:
                        dve.wait_ge(idx_in[0].sem, b * (16 * BLOCK // AHEAD) + 16 * (BLOCK // AHEAD + 1))
                    mask(n + 1, i + 1)
                    dve.wait_ge(cand_ready.sem, n + 1)
                    dve.wait_ge(idx_used.sem, n + 1)
                    dve.memset(hop[:, :], 0.0).then_inc(picked.sem, 1)
                    for q, n_out in enumerate((4, 2, 1)):
                        stride = 2 << q
                        dve.wait_ge(picked.sem, 4 * n + 2 + q)
                        dve.memset(hop[:, :], 0.0)
                        dve.copy_predicated(cand[:, p, 0::stride, :],
                                            bits[:, p, q, :].unsqueeze(1).to_broadcast([P, n_out, LOOKUP]),
                                            cand[:, p, stride // 2::stride, :]).then_inc(picked.sem, 1)

            chain.start(dve)
            chain.link(dve.memset(carry[:, :], 0.0))
            for n, tl in enumerate((picked, kept, xn_out)):
                dve.memset(note[:, n:n + 1], 0.0).then_inc(tl.sem, tl.base)
            dve.wait_ge(table_in.sem, 16)
            pairs = table[:, :].rearrange("p (n two) -> p n two", two=2)
            chain.link(dve.tensor_tensor(step[:, :], pairs[:, :, 1], pairs[:, :, 0], ALU.subtract))
            dve.wait_ge(idx_in[0].sem, 16)
            mask(0, 0)
            with dve.Fori(0, NB) as b:
                norm.vector(dve, b, lambda: pick(b, 0, FIRST))
                chain.start(dve, 2 + b * per_block)
                for oc in range(C):
                    pick(b, START[oc], START[oc + 1])
                    grp.wait_filled(dve, b, 4 * oc + 1)
                    grp.wait_emptied(dve, b, 4 * oc)
                    dve.scalar_tensor_tensor(kv[:, :], k.ps[:, grp.bank(4 * oc + 1), :], ba[:, 1, oc:oc + 1],
                                             v_sb[:, oc % 2, :], ALU.add, ALU.mult).then_inc(k.emptied_v.sem, 1)
                    grp.wait_emptied(dve, b, 4 * oc + 1)
                    chain.link(dve.tensor_tensor_scan(kvs[:, :], k.ones[:, :], kv[:, :], carry[:, oc:oc + 1],
                                                      ALU.mult, ALU.add))
                    chain.mark(dve.tensor_copy(carry[:, oc:oc + 1], kvs[:, TB - 1:TB]))
                    grp.wait_filled(dve, b, 4 * oc + 3)
                    grp.wait_emptied(dve, b, 4 * oc + 2)
                    dve.scalar_tensor_tensor(qg[:, :], k.ps[:, grp.bank(4 * oc + 3), :], ba[:, 3, oc:oc + 1],
                                             g_sb[:, oc % 2, :], ALU.add, ALU.mult).then_inc(k.emptied_v.sem, 1)
                    grp.wait_emptied(dve, b, 4 * oc + 3)
                    chain.link(dve.tensor_tensor(qg[:, :], qg[:, :], kvs[:, :], ALU.mult))
                    xs = k.x[:, oc, bass.ds(b * TB, TB)]
                    chain.link(dve.tensor_tensor(xs, xs, qg[:, :], ALU.add))
                assert chain.n == per_block
            dve.wait_ge(picked.sem, 4 * LOOKUPS + 1)
    grp.close()
    k.v_chain.base += 2 + NB * per_block


def clear_slots(sp, core, zero, cleared):
    for n in range(4):
        sp.dma_start(core.io["slots_x"][n * SLOTS // 4:(n + 1) * SLOTS // 4, :].rearrange("(p s) n -> p s n", p=P),
                     zero[:, :].unsqueeze(1).to_broadcast([P, SLOTS // 4 // P, D])).then_inc(cleared.sem, 16)


def layer0_ffn(core, ctx, wf):
    nc, k, io = core.nc, core, core.io

    def sb(name, shape, dt=F32):
        return ctx.enter_context(nc.sbuf_tensor(name, shape, dt))

    w_gate = wf[:, 0:C * H1].rearrange("p (c n) -> p c n", c=C)
    w_up = wf[:, C * H1:2 * C * H1].rearrange("p (c n) -> p c n", c=C)
    w_down = wf[:, 2 * C * H1:2 * C * H1 + J0 * D].rearrange("p (j n) -> p j n", j=J0)
    xn = sb("xn_in0", [P, 2, C, TB])
    h, sg = sb("h", [P, J0, TB]), sb("sg", [P, 2, TB])
    zero = sb("zero", [P, D])
    cleared, zeroed = Tally(nc, ctx, "cleared"), Tally(nc, ctx, "zeroed")
    arrived = [Tally(nc, ctx, f"xn_arrived{p}") for p in range(2)]
    grp = Groups(core, "av" * J0 + "v" * C)
    down = 2 * J0

    with nc.Block() as block:
        @block.sync
        def _(sp):
            for b in range(NB):
                if b >= 2:
                    grp.wait_block(sp, b - 1)
                sp.dma_start(xn[:, b % 2, :, :], io["xn_saved"].rearrange("(c p) t -> p c t", p=P)
                             [:, :, b * TB:(b + 1) * TB]).then_inc(arrived[b % 2].sem, 16)
                if b == 1:
                    sp.wait_ge(zeroed.sem, 1)
                    clear_slots(sp, core, zero, cleared)
            sp.wait_ge(cleared.sem, 64)

        @block.tensor
        def _(pe):
            with pe.Fori(0, NB // 2) as it:
                for p in range(2):
                    b = 2 * it + p
                    grp.wait_block(pe, b)
                    pe.wait_ge(arrived[p].sem, 16 * it + 16)
                    for j in range(J0):
                        rows = min(P, H0 - j * P)
                        for u, w in enumerate((w_gate, w_up)):
                            g = 2 * j + u
                            grp.wait_free(pe, b, g)
                            project(pe, k.ps[0:rows, grp.bank(g), :], lambda c: w[:, c, j * P:j * P + rows],
                                    lambda c: xn[:, p, c, :]).then_inc(k.filled.sem, 1)
                    for oc in range(C):
                        grp.wait_free(pe, b, down + oc)
                        for j in range(J0):
                            if oc == 0:
                                grp.wait_emptied(pe, b, 2 * j + 1)
                            rows = min(P, H0 - j * P)
                            m = pe.matmul(k.ps[:, grp.bank(down + oc), :], w_down[0:rows, j, oc * P:(oc + 1) * P],
                                          h[0:rows, j, :], start=j == 0, stop=j == J0 - 1)
                        m.then_inc(k.filled.sem, 1)

        @block.scalar
        def _(act):
            with act.Fori(0, NB) as b:
                for j in range(J0):
                    rows = min(P, H0 - j * P)
                    g = 2 * j
                    if j >= 2:
                        grp.wait_emptied(act, b, g - 3)
                    else:
                        grp.wait_block(act, b)
                    grp.wait_filled(act, b, g)
                    act.activation(sg[0:rows, j % 2, :], k.ps[0:rows, grp.bank(g), :], ACT.Silu)\
                       .then_inc(k.emptied_a.sem, 1)

        @block.vector
        def _(dve):
            dve.memset(zero[:, :], 0.0).then_inc(zeroed.sem, 1)
            with dve.Fori(0, NB) as b:
                for j in range(J0):
                    rows = min(P, H0 - j * P)
                    g = 2 * j
                    grp.wait_emptied(dve, b, g)
                    grp.wait_filled(dve, b, g + 1)
                    dve.tensor_tensor(h[0:rows, j, :], k.ps[0:rows, grp.bank(g + 1), :], sg[0:rows, j % 2, :],
                                      ALU.mult).then_inc(k.emptied_v.sem, 1)
                for oc in range(C):
                    grp.wait_filled(dve, b, down + oc)
                    xs = k.x[:, oc, bass.ds(b * TB, TB)]
                    dve.tensor_tensor(xs, xs, k.ps[:, grp.bank(down + oc), :], ALU.add)\
                       .then_inc(k.emptied_v.sem, 1)
    grp.close()


class Split:

    def __init__(self, core, ctx, name, items):
        self.core, self.items = core, items
        nc = core.nc
        self.parts = ctx.enter_context(nc.sbuf_tensor("parts" + name, [P, 2, 3, TB], BF16))
        self.rest = ctx.enter_context(nc.sbuf_tensor("rest" + name, [P, 2, TB], F32))
        self.stored = [Tally(nc, ctx, f"parts_stored{name}{n}") for n in range(2)]
        self.a0, self.v0 = core.split_a.base, core.split_v.base
        self.per_buffer = [(items + 1) // 2, items // 2]

    def step(self, b, i):
        return b * (2 * self.items) + 2 * i

    def prime(self, dve):
        for n in range(2):
            dve.memset(self.rest[:, n, 0:1], 0.0).then_inc(self.stored[n].sem, 1)

    def wait_free(self, act, b, i):
        act.wait_ge(self.stored[i % 2].sem, 16 * (b * self.per_buffer[i % 2] + i // 2) + 1)

    def scalar_1(self, act, b, i, src, scale, rows=P):
        self.wait_free(act, b, i)
        act.activation(self.parts[0:rows, i % 2, 0, :], src, ACT.Copy, scale=scale)\
           .then_inc(self.core.split_a.sem, 1)

    def vector_1(self, dve, b, i, src, scale, rows=P):
        dve.wait_ge(self.core.split_a.sem, self.a0 + self.step(b, i) + 1)
        dve.scalar_tensor_tensor(self.rest[0:rows, i % 2, :], src, scale, self.parts[0:rows, i % 2, 0, :],
                                 ALU.mult, ALU.subtract).then_inc(self.core.split_v.sem, 1)

    def scalar_2(self, act, b, i, rows=P):
        act.wait_ge(self.core.split_v.sem, self.v0 + self.step(b, i) + 1)
        act.activation(self.parts[0:rows, i % 2, 1, :], self.rest[0:rows, i % 2, :], ACT.Copy)\
           .then_inc(self.core.split_a.sem, 1)

    def vector_2(self, dve, b, i, rows=P):
        dve.wait_ge(self.core.split_a.sem, self.a0 + self.step(b, i) + 2)
        dve.tensor_tensor(self.parts[0:rows, i % 2, 2, :], self.rest[0:rows, i % 2, :],
                          self.parts[0:rows, i % 2, 1, :], ALU.subtract).then_inc(self.core.split_v.sem, 1)

    def store(self, sp, b, i, dst, rows=P, after=0):
        if after is not None:
            sp.wait_ge(self.core.split_v.sem, self.v0 + self.step(b, i + after) + 2)
        sp.dma_start(dst[:, :, bass.ds(b * TB, TB)].rearrange("a r t -> r a t"),
                     self.parts[0:rows, i % 2, :, :]).then_inc(self.stored[i % 2].sem, 16)

    def wait_done(self, act, b, i):
        act.wait_ge(self.core.split_v.sem, self.v0 + self.step(b, i) + 1)

    def wait_stores(self, sp):
        for n in range(2):
            sp.wait_ge(self.stored[n].sem, 16 * NB * self.per_buffer[n] + 1)

    def close(self):
        self.core.split_a.base += 2 * NB * self.items
        self.core.split_v.base += 2 * NB * self.items


def key_chunks():
    return [(qb, j) for qb in range(NB) for j in range(TPB * (qb + 1))]


def max_pieces():
    return [(i, a, min(a + 1024, (i + 1) * P)) for i in range(TT) for a in range(0, (i + 1) * P, 1024)]


def attention(core, name, heads, dh, q_parts, k_parts, v_all, out, shared=False, ahead=(), first=6):
    nc, k = core.nc, core
    passes = 2 if dh == 32 else 1
    order_q, order_k = (0, 0, 1, 1, 0, 2), (0, 1, 0, 1, 2, 0)
    M_ROW = 6 * dh % P
    MAX_ROWS = P if passes == 2 else 6 * dh
    chunks, pieces = key_chunks(), max_pieces()
    NC, NM = len(chunks), len(pieces) + 1
    RING = 8
    LAG = 5
    LOADS = [(1 if shared else 2) * sum(n * dh // P == s for n in range(6)) for s in range(passes)]
    W = 32
    assert NC % RING == 0 and len(pieces) % 2 == 0

    with ExitStack() as ctx:
        def sb(nm, shape, dt=F32):
            return ctx.enter_context(nc.sbuf_tensor(nm + name, shape, dt))

        def tally(nm, base=0):
            return Tally(nc, ctx, nm + name, base)

        qs, ks = sb("qs", [P, 2, passes, T], BF16), sb("ks", [P, 1 if shared else 2, passes, T], BF16)
        vh = sb("vh", [P, 1 if shared else 2, TT, P], BF16)
        v_rest = sb("v_rest", [P, TT, dh])
        expT = sb("expT", [P, RING, TB])
        e_parts = sb("e_parts", [P, RING, 2, TB], F16)
        part_max, neg_max = sb("part_max", [P, TT, 2]), sb("neg_max", [P, TT])
        m_parts, m_rest = sb("m_parts", [TT, 3, P], BF16), sb("m_rest", [TT, P])
        o_first, sums, o_sb = sb("o_first", [P, 2, TB]), sb("sums", [P, 2, TB]), sb("o_sb", [P, 2, TB])
        rec = sb("rec", [P, TB])
        shift, free_note = sb("shift", [P, 1]), sb("free_note", [1, 8])

        qk_in = [[tally(f"qk_in{n}_{s}") for s in range(passes)] for n in range(2)]
        keys_in = tally("keys_in")
        m_in = [tally(f"m_in{n}") for n in range(2)]
        v_split = tally("v_split")
        max_filled, max_emptied = tally("max_filled"), tally("max_emptied")
        neg_ready, m_split = tally("neg_ready"), tally("m_split")
        scored, exp_done = tally("scored"), tally("exp_done", 2)
        cast_a, cast_v = tally("cast_a"), tally("cast_v")
        rest_done, used = tally("rest_done", RING), tally("used", RING)
        evacuated, o_added, o_joined = tally("evacuated"), tally("o_added"), tally("o_joined", 2)
        rec_done, o_done = tally("rec_done"), tally("o_done", 2)
        o_stored = [tally(f"o_stored{n}", 1) for n in range(2)]
        ready, m_out = tally("ready"), tally("m_out")
        m_rows = core.io["m_rows"]

        def max_bank(n):
            return 4 + 2 * (n % 2)

        steps = dict(zip((t for t in range(first, NC) if t != 10), range(len(pieces))))
        steps[first + 26] = len(pieces)
        V_STEP = 35

        def span(t):
            qb, j = chunks[t]
            return slice(max(0, j - TPB * qb) * P, TB)

        def last_chunk(qb):
            return chunks.index((qb, TPB * (qb + 1) - 1))

        ends = {last_chunk(qb): qb for qb in range(NB)}

        def walk(eng, head):
            for p in range(2):
                head(p, p, 0, True)
            with eng.Fori(1, heads // 2 - 1) as it:
                for p in range(2):
                    head(2 * it + p, p, it, True)
            for p in range(2):
                head(heads - 2 + p, p, heads // 2 - 1, p == 0)

        def behind(h, p, t, lag):
            if t >= lag:
                return h, p, t - lag
            if isinstance(h, int) and h == 0:
                return None
            return h - 1, 1 - p, NC + t - lag

        with nc.Block() as block:
            @block.sync
            def _(sp):
                def operands(parts, dst, order, s, sem, rows):
                    for n, which in enumerate(order):
                        if n * dh // P == s:
                            sp.dma_start(dst[n * dh % P:n * dh % P + dh, s, :], parts[which, rows, :]).then_inc(sem, 16)

                def fetch(h, p):
                    rows = bass.ds(h * dh, dh)
                    for s in range(passes):
                        operands(q_parts, qs[:, p, :, :], order_q, s, qk_in[p][s].sem, rows)
                        if not shared:
                            operands(k_parts, ks[:, p, :, :], order_k, s, qk_in[p][s].sem, rows)

                def put_max(h, p):
                    sp.wait_ge(m_split.sem, 4 * h + 4)
                    sp.dma_start(m_rows.rearrange("a (t n) -> t a n", t=TT), m_parts[:, :, :]).then_inc(m_out.sem, 16)
                    sp.wait_ge(m_out.sem, 16 * h + 16)
                    sp.dma_start(qs[M_ROW:M_ROW + 3, p, passes - 1, :], m_rows).then_inc(m_in[p].sem, 16)

                def store(h, p):
                    sp.wait_ge(o_done.sem, h + 3)
                    for qb in range(NB):
                        sp.dma_start(out[bass.ds(h * dh, dh), qb * TB:(qb + 1) * TB], o_sb[W * qb:W * qb + dh, p, :])\
                          .then_inc(o_stored[p].sem, 16)

                sp.wait_ge(ready.sem, 5)
                for s in range(passes if shared else 0):
                    operands(k_parts, ks[:, 0, :, :], order_k, s, keys_in.sem, slice(0, dh))
                for h in range(2):
                    fetch(h, h)
                put_max(0, 0)
                load(sp, core, ahead)

                def head(h, p, it, more):
                    if not (isinstance(h, int) and h == 0):
                        store(h - 1, 1 - p)
                    if more:
                        put_max(h + 1, 1 - p)
                    if not (isinstance(h, int) and h >= heads - 2):
                        sp.wait_ge(scored.sem, NC * h + NC)
                        fetch(h + 2, p)

                walk(sp, head)
                store(heads - 1, 1)
                for p in range(2):
                    sp.wait_ge(o_stored[p].sem, 16 * NB * (heads // 2) + 1)
                sp.wait_ge(k.loaded.sem, k.loaded.base)

            @block.tensor
            def _(pe):
                def max_piece(h, p, it, n, first):
                    if n >= 2:
                        pe.wait_ge(max_emptied.sem, NM * h + (n - 1))
                    elif not first:
                        pe.wait_ge(max_emptied.sem, NM * h)
                    if n == len(pieces):
                        pe.wait_ge(neg_ready.sem, h + 1)
                        pe.transpose(k.ps[0:TT, max_bank(n), 0:P], neg_max[:, :], k.ident[:, :])\
                          .then_inc(max_filled.sem, 1)
                        return
                    if n == 0:
                        pe.wait_ge(qk_in[p][0].sem, it * (16 * LOADS[0]) + 16 * LOADS[0])
                    i, a, b = pieces[n]
                    for c in range(a, b, 512):
                        width, bank = min(512, b - c), max_bank(n) + (c - a) // 512
                        diagonal = b == (i + 1) * P and c + 512 >= b
                        if diagonal:
                            pe.matmul(k.ps[:, bank, width - P:width], k.ident_b[:, :], k.mask_b[:, :],
                                      start=True, stop=False, skip_group_check=True)
                        m = pe.matmul(k.ps[:, bank, 0:width], qs[0:MAX_ROWS, p, 0, i * P:(i + 1) * P],
                                      ks[0:MAX_ROWS, 0 if shared else p, 0, c:c + width], start=not diagonal, stop=True,
                                      skip_group_check=True)
                    m.then_inc(max_filled.sem, 1)

                def score(h, p, t):
                    qb, j = chunks[t]
                    pe.wait_ge(exp_done.sem, NC * h + t + 1)
                    cols, bank = span(t), t % 2
                    diagonal = j >= TPB * qb
                    if diagonal:
                        pe.matmul(k.ps[:, bank, cols.start:cols.start + P], k.ident_b[:, :], k.maskT_b[:, :],
                                  start=True, stop=False, skip_group_check=True)
                    for s in range(passes):
                        K = P if s < passes - 1 else M_ROW + 3
                        m = pe.matmul(k.ps[:, bank, cols], ks[0:K, 0 if shared else p, s, j * P:(j + 1) * P],
                                      qs[0:K, p, s, qb * TB + cols.start:(qb + 1) * TB],
                                      start=s == 0 and not diagonal, stop=s == passes - 1, skip_group_check=True)
                    m.then_inc(scored.sem, 1)

                def weigh(h, p, t):
                    qb, j = chunks[t]
                    if t == 0 and not shared:
                        pe.wait_ge(v_split.sem, 4 * h + 4)
                    if j == 0:
                        pe.wait_ge(o_joined.sem, NB * h + qb + 1)
                    pe.wait_ge(rest_done.sem, NC * h + (t + 1 + RING))
                    for n in range(2):
                        m = pe.matmul(k.ps[:, 2 + qb % 2, span(t)], vh[:, 0 if shared else p, j, :],
                                      e_parts[:, t % RING, n, span(t)], start=j == 0 and n == 0,
                                      stop=j == TPB * (qb + 1) - 1 and n == 1, skip_group_check=True)
                    m.then_inc(used.sem, 1)

                pe.wait_ge(ready.sem, 5)
                pe.wait_ge(v_split.sem, 4)
                if shared:
                    pe.wait_ge(keys_in.sem, 16 * 6)
                pe.wait_ge(exp_done.sem, 2)
                for n in range(NM):
                    max_piece(0, 0, 0, n, True)

                def head(h, p, it, more):
                    pe.wait_ge(m_in[p].sem, 16 * it + 16)
                    pe.wait_ge(qk_in[p][-1].sem, it * (16 * LOADS[-1]) + 16 * LOADS[-1])
                    for t in range(NC):
                        score(h, p, t)
                        last = behind(h, p, t, LAG)
                        if last:
                            weigh(*last)
                        if more and t in steps:
                            max_piece(h + 1, 1 - p, it + p, steps[t], False)

                walk(pe, head)
                for t in range(NC - LAG, NC):
                    weigh(heads - 1, 1, t)

            @block.scalar
            def _(act):
                def evacuate(h, p, qb):
                    act.wait_ge(used.sem, NC * h + (RING + last_chunk(qb) + 1))
                    if qb == 0:
                        act.wait_ge(o_done.sem, h + 1)
                    rows, bank = slice(W * qb, W * (qb + 1)), 2 + qb % 2
                    act.activation(o_first[rows, p, :], k.ps[0:W, bank, :], ACT.Copy).then_inc(evacuated.sem, 1)
                    act.activation(sums[rows, p, :], k.ps[3 * W:4 * W, bank, :], ACT.Copy)\
                       .then_inc(evacuated.sem, 1)

                def head(h, p, it, more):
                    for t in range(NC):
                        act.wait_ge(rest_done.sem, NC * h + (t + 1))
                        act.wait_ge(scored.sem, NC * h + t + 1)
                        act.activation(expT[:, t % RING, span(t)], k.ps[:, t % 2, span(t)], ACT.Exp,
                                       bias=shift[:, 0:1]).then_inc(exp_done.sem, 1)
                        if t % 2 == 1:
                            act.wait_ge(used.sem, NC * h + t)
                            act.wait_ge(exp_done.sem, NC * h + t + 2)
                            act.activation(e_parts[:, (t - 1) % RING, 0, span(t - 1)],
                                           expT[:, (t - 1) % RING, span(t - 1)], ACT.Copy).then_inc(cast_a.sem, 1)
                        last = behind(h, p, t, LAG + 1)
                        if last and last[2] in ends:
                            evacuate(last[0], last[1], ends[last[2]])

                act.wait_ge(ready.sem, 5)
                walk(act, head)
                evacuate(heads - 1, 1, NB - 1)

            @block.gpsimd
            def _(pool):
                def head(h, p, it, more):
                    for t in range(NC):
                        if t % 2 == 0:
                            pool.wait_ge(cast_a.sem, NC // 2 * h + (t // 2 + 1))
                        else:
                            pool.wait_ge(cast_v.sem, NC // 2 * h + (t // 2 + 1))
                        at = t % RING
                        pool.tensor_tensor(e_parts[:, at, 1, span(t)], expT[:, at, span(t)],
                                           e_parts[:, at, 0, span(t)], ALU.subtract).then_inc(rest_done.sem, 1)

                pool.wait_ge(rest_done.sem, RING)
                walk(pool, head)

            @block.vector
            def _(dve):
                def split_values(h, p):
                    if shared:
                        src = v_all[:, :, :]
                    else:
                        src = v_all[:, :, bass.ds(h * dh, dh)]
                    dst = [vh[:, p, :, W * n:W * n + dh] for n in range(3)]
                    dve.tensor_copy(dst[0], src).then_inc(v_split.sem, 1)
                    dve.wait_ge(v_split.sem, 4 * h + 1)
                    dve.tensor_tensor(v_rest[:, :, :], src, dst[0], ALU.subtract).then_inc(v_split.sem, 1)
                    dve.wait_ge(v_split.sem, 4 * h + 2)
                    dve.tensor_copy(dst[1], v_rest[:, :, :]).then_inc(v_split.sem, 1)
                    dve.wait_ge(v_split.sem, 4 * h + 3)
                    dve.tensor_tensor(dst[2], v_rest[:, :, :], dst[1], ALU.subtract).then_inc(v_split.sem, 1)
                    dve.wait_ge(v_split.sem, 4 * h + 4)

                def take_max(h, n):
                    dve.wait_ge(max_filled.sem, NM * h + n + 1)
                    if n < len(pieces):
                        i, a, b = pieces[n]
                        src = k.ps[:, max_bank(n):max_bank(n) + 2, :].rearrange("p a n -> p (a n)")[:, 0:b - a]
                        dve.tensor_reduce(part_max[:, i, a // 1024:a // 1024 + 1], src, X_AXIS, ALU.max)\
                           .then_inc(max_emptied.sem, 1)
                        if n == len(pieces) - 1:
                            dve.wait_ge(max_emptied.sem, NM * h + n + 1)
                            dve.tensor_reduce(neg_max[:, :], part_max[:, :, :], X_AXIS, ALU.max, negate=True)\
                               .then_inc(neg_ready.sem, 1)
                        return
                    src = k.ps[0:TT, max_bank(n), 0:P]
                    dve.tensor_copy(m_parts[:, 0, :], src).then_inc(m_split.sem, 1)
                    dve.wait_ge(m_split.sem, 4 * h + 1)
                    dve.tensor_tensor(m_rest[:, :], src, m_parts[:, 0, :], ALU.subtract).then_inc(m_split.sem, 1)
                    dve.wait_ge(m_split.sem, 4 * h + 2)
                    dve.tensor_copy(m_parts[:, 1, :], m_rest[:, :]).then_inc(m_split.sem, 1)
                    dve.wait_ge(m_split.sem, 4 * h + 3)
                    dve.tensor_tensor(m_parts[:, 2, :], m_rest[:, :], m_parts[:, 1, :], ALU.subtract)\
                       .then_inc(m_split.sem, 1)
                    dve.wait_ge(m_split.sem, 4 * h + 4)
                    dve.memset(free_note[:, 6:7], 0.0).then_inc(max_emptied.sem, 1)

                def join(h, p, it, qb):
                    rows, bank = slice(W * qb, W * (qb + 1)), 2 + qb % 2
                    dve.wait_ge(evacuated.sem, 2 * NB * h + (2 * qb + 2))
                    dve.tensor_tensor(o_first[rows, p, :], o_first[rows, p, :], k.ps[W:2 * W, bank, :], ALU.add)\
                       .then_inc(o_added.sem, 1)
                    if qb == 0:
                        dve.wait_ge(o_stored[p].sem, 16 * NB * it + 1)
                    dve.wait_ge(o_added.sem, NB * h + (qb + 1))
                    dve.tensor_tensor(o_sb[rows, p, :], o_first[rows, p, :], k.ps[2 * W:3 * W, bank, :], ALU.add)\
                       .then_inc(o_joined.sem, 1)

                def reciprocal(h, p, half):
                    cols = slice(TB // 2 * half, TB // 2 * (half + 1))
                    if half == 0:
                        dve.wait_ge(o_done.sem, h + 2)
                    dve.reciprocal(rec[:, cols], sums[:, p, cols]).then_inc(rec_done.sem, 1)

                def divide(h, p):
                    dve.wait_ge(rec_done.sem, 2 * h + 2)
                    dve.wait_ge(o_joined.sem, NB * h + (NB + 2))
                    dve.tensor_tensor(o_sb[:, p, :], o_sb[:, p, :], rec[:, :], ALU.mult).then_inc(o_done.sem, 1)

                for n, tl in enumerate((exp_done, used, rest_done, o_joined, o_done, *o_stored)):
                    dve.memset(free_note[:, n:n + 1], 0.0).then_inc(tl.sem, tl.base)
                dve.memset(vh[:, :, :, :], 1.0).then_inc(ready.sem, 1)
                dve.memset(part_max[:, :, 1:2], NEG).then_inc(ready.sem, 1)
                dve.memset(ks[M_ROW // 32 * 32:, :, passes - 1, :], 1.0).then_inc(ready.sem, 1)
                dve.memset(shift[:, :], SHIFT).then_inc(ready.sem, 1)
                dve.memset(sums[:, :, :], 1.0).then_inc(ready.sem, 1)
                dve.wait_ge(ready.sem, 5)
                split_values(0, 0)
                for n in range(NM):
                    take_max(0, n)

                def head(h, p, it, more):
                    for t in range(NC):
                        if t % 2 == 1:
                            dve.wait_ge(used.sem, NC * h + t + 1)
                            dve.wait_ge(exp_done.sem, NC * h + t + 3)
                            dve.tensor_copy(e_parts[:, t % RING, 0, span(t)], expT[:, t % RING, span(t)])\
                               .then_inc(cast_v.sem, 1)
                        if more and t in steps:
                            take_max(h + 1, steps[t])
                        if more and t == V_STEP and not shared:
                            if not (isinstance(h, int) and h == 0):
                                dve.wait_ge(used.sem, NC * h + RING)
                            split_values(h + 1, 1 - p)
                        last = behind(h, p, t, LAG + 2)
                        if last and last[2] in ends:
                            join(last[0], last[1], it if last[2] == t - LAG - 2 else it - 1 + p, ends[last[2]])
                        if not (isinstance(h, int) and h == 0):
                            if t in (LAG + 10, LAG + 16):
                                reciprocal(h - 1, 1 - p, t // (LAG + 16))
                            elif t == LAG + 17:
                                divide(h - 1, 1 - p)

                walk(dve, head)
                join(heads - 1, 1, heads // 2 - 1, NB - 1)
                reciprocal(heads - 1, 1, 0)
                reciprocal(heads - 1, 1, 1)
                divide(heads - 1, 1)


def layer1(core):
    nc, k, io = core.nc, core, core.io
    with ExitStack() as ctx:
        def sb(name, shape, dt=F32):
            return ctx.enter_context(nc.sbuf_tensor(name, shape, dt))

        v_all = sb("v1_all", [P, TT, P])
        with ExitStack() as inner:
            layer1_blocks(core, inner, v_all)
        w_out, b_out = sb("w_out1", [P, 1, D]), sb("b_out1", [P, C])
        attention(core, "1", 8, 16, io["q1_parts"], io["k1_parts"], v_all, io["o1"],
                  ahead=[(w_out[:, 0, :], io["L1_out_w"]), (b_out[:, :], io["L1_out_b"])])
        project_out(core, ctx, "1", io["o1"], None, w_out, b_out)


def project_out(core, ctx, name, heads_out, added, weights, bias, result=None):
    nc, k = core.nc, core
    chunks = weights.shape[1]
    o_in = ctx.enter_context(nc.sbuf_tensor("o_in" + name, [P, 2, chunks, TB], F32))
    a_in = ctx.enter_context(nc.sbuf_tensor("a_in" + name, [P, 2, C, TB], F32)) if added is not None else None
    arrived = [Tally(nc, ctx, f"o_arrived{name}{n}") for n in range(2)]
    per = 2 if added is not None else 1
    grp = Groups(core, "v" * C)
    chain = Chain(k.v_chain)
    per_chain = C if added is not None else 0
    with nc.Block() as block:
        @block.sync
        def _(sp):
            def fetch(b, p):
                sp.dma_start(o_in[:, p, :, :], heads_out.rearrange("(c p) t -> p c t", p=P)
                             [:, :, bass.ds(b * TB, TB)]).then_inc(arrived[p].sem, 16)
                if added is not None:
                    sp.dma_start(a_in[:, p, :, :], added.rearrange("(c p) t -> p c t", p=P)
                                 [:, :, bass.ds(b * TB, TB)]).then_inc(arrived[p].sem, 16)

            for b in range(NB):
                if b >= 2:
                    grp.wait_block(sp, b - 1)
                fetch(b, b % 2)
            if result is not None:
                for b in range(NB):
                    grp.wait_block(sp, b + 1)
                    sp.dma_start(result.rearrange("(c p) t -> p c t", p=P)[:, :, b * TB:(b + 1) * TB],
                                 k.x[:, :, b * TB:(b + 1) * TB]).then_inc(k.stored.sem, 16)
                sp.wait_ge(k.stored.sem, k.stored.base + 16 * NB)

        @block.tensor
        def _(pe):
            for b in range(NB):
                grp.wait_block(pe, b)
                pe.wait_ge(arrived[b % 2].sem, 16 * per * (b // 2 + 1))
                for oc in range(C):
                    project(pe, k.ps[:, grp.bank(oc), :], lambda c: weights[:, c, oc * P:(oc + 1) * P],
                            lambda c: o_in[:, b % 2, c, :], chunks).then_inc(k.filled.sem, 1)

        @block.vector
        def _(dve):
            for b in range(NB):
                chain.start(dve, b * per_chain)
                for oc in range(C):
                    xs = k.x[:, oc, b * TB:(b + 1) * TB]
                    if added is not None:
                        dve.wait_ge(arrived[b % 2].sem, 16 * per * (b // 2 + 1))
                        chain.link(dve.tensor_tensor(xs, xs, a_in[:, b % 2, oc, :], ALU.add))
                    grp.wait_filled(dve, b, oc)
                    dve.scalar_tensor_tensor(xs, k.ps[:, grp.bank(oc), :], bias[:, oc:oc + 1], xs,
                                             ALU.add, ALU.add).then_inc(k.emptied_v.sem, 1)
    grp.close()
    k.v_chain.base += NB * per_chain


def layer1_blocks(core, ctx, v_all):
    nc, k, io = core.nc, core, core.io

    def sb(name, shape, dt=F32):
        return ctx.enter_context(nc.sbuf_tensor(name, shape, dt))

    wp = sb("wp1", [P, 3, C, P])
    bp = sb("bp1", [P, 3])
    wv, bv = sb("wv1", [P, P]), sb("bv1", [P, P])
    rot = sb("rot1", [P, P])
    wf = sb("wf1", [P, (2 * C + C) * H1])
    w_gate = wf[:, 0:C * H1].rearrange("p (c n) -> p c n", c=C)
    w_up = wf[:, C * H1:2 * C * H1].rearrange("p (c n) -> p c n", c=C)
    w_down = wf[:, 2 * C * H1:].rearrange("p (j n) -> p j n", j=J1)
    s_hid, s_down = sb("s_hid", [P, 2, J1]), sb("s_down", [P, C])
    raw_in = [Tally(nc, ctx, f"raw_in{n}") for n in range(3)]
    widened = Tally(nc, ctx, "widened")

    norm = Norm(core, ctx, 1)
    split = Split(core, ctx, "1", 2)
    plain = sb("plain1", [P, 2, TB])
    turned_, mixed = sb("turned1", [P, 2, TB]), sb("mixed1", [P, 2, TB])
    act_qk = sb("act_qk1", [P, 2, TB])
    ckv = sb("ckv", [P, TB])
    wave = sb("wave1", [P, 2, TB])
    h, sg = sb("h1", [P, J1, TB]), sb("sg1", [P, 2, TB])
    wave_in = Tally(nc, ctx, "wave_in1")
    qk_act = Tally(nc, ctx, "qk_act1")

    grp = Groups(core, "aaa" + "vv" + "v" + "av" * J1 + "v" * C, ring=6)
    Q, K_, KV, RQ, RK, V, FFN = 0, 1, 2, 3, 4, 5, 6
    DOWN = FFN + 2 * J1
    chain = Chain(k.v_chain)
    per_block = 4

    with nc.Block() as block:
        def third(n):
            return wf[:, n * C * H1:(n + 1) * C * H1]

        @block.sync
        def _(sp):
            load(sp, core, [(wp[:, :, :, :], io["L1_w"]), (bp[:, :], io["L1_b"]), (wv[:, :], io["L1_cv_w"]),
                            (bv[:, :], io["L1_cv_b"].partition_broadcast(P)), (rot[:, :], io["L1_rot"]),
                            (s_hid[:, :, :], io["L1_s_hid"]), (s_down[:, :], io["L1_s_down"])])
            for n in range(3):
                sp.dma_start(third(n).bitcast(I32), io["L1_wq"][:, 4 * n:4 * (n + 1), :].rearrange("p a n -> p (a n)"))\
                  .then_inc(raw_in[n].sem, 16)
            with sp.Fori(0, NB) as b:
                split.store(sp, b, 0, io["q1_parts"], after=1)
                split.store(sp, b, 1, io["k1_parts"], after=None)
            split.wait_stores(sp)

        @block.tensor
        def _(pe):
            def body(b, more):
                grp.wait_block(pe, b)
                norm.wait_ready(pe, b)
                for g, w in ((Q, 0), (K_, 2), (KV, 1)):
                    project(pe, k.ps[:, grp.bank(g), :], lambda c: wp[:, w, c, :], lambda c: norm.xn[:, c, :])\
                        .then_inc(k.filled.sem, 1)
                for n, g in enumerate((RQ, RK)):
                    grp.wait_emptied(pe, b, (Q, K_)[n])
                    pe.matmul(k.ps[:, grp.bank(g), :], rot[:, :], plain[:, n, :], start=True, stop=True)\
                      .then_inc(k.filled.sem, 1)
                grp.wait_emptied(pe, b, KV)
                for t in range(TPB):
                    m = pe.matmul(k.ps[:, grp.bank(V), t * P:(t + 1) * P], ckv[:, t * P:(t + 1) * P], wv[:, :],
                                  start=True, stop=True)
                m.then_inc(k.filled.sem, 1)
                pe.wait_ge(widened.sem, 2)
                for j in range(J1):
                    for u, w in enumerate((w_gate, w_up)):
                        g = FFN + 2 * j + u
                        grp.wait_free(pe, b, g)
                        project(pe, k.ps[:, grp.bank(g), :], lambda c: w[:, c, j * P:(j + 1) * P],
                                lambda c: norm.xn[:, c, :]).then_inc(k.filled.sem, 1)
                if more:
                    norm.tensor_mean(pe, b + 1)
                pe.wait_ge(widened.sem, 3)
                grp.wait_emptied(pe, b, DOWN - 1)
                for oc in range(C):
                    if more and oc == 1:
                        norm.tensor_var(pe, b + 1)
                    grp.wait_free(pe, b, DOWN + oc)
                    project(pe, k.ps[:, grp.bank(DOWN + oc), :], lambda j: w_down[:, j, oc * P:(oc + 1) * P],
                            lambda j: h[:, j, :], J1).then_inc(k.filled.sem, 1)

            norm.tensor_mean(pe, 0)
            norm.tensor_var(pe, 0)
            pe.wait_ge(k.loaded.sem, k.loaded.base)
            each_block(pe, body)

        @block.scalar
        def _(act):
            def body(b, more):
                grp.wait_block(act, b)
                act.dma_start(wave[:, :, :], io["L1_wave"][:, :, bass.ds(b * TB, TB)]).then_inc(wave_in.sem, 16)
                for n, g in enumerate((Q, K_)):
                    grp.wait_filled(act, b, g)
                    act.activation(plain[:, n, :], k.ps[:, grp.bank(g), :], ACT.Identity,
                                   bias=bp[:, 2 * n:2 * n + 1]).then_inc(k.emptied_a.sem, 1)
                grp.wait_filled(act, b, KV)
                act.activation(ckv[:, :], k.ps[:, grp.bank(KV), :], ACT.Gelu, bias=bp[:, 1:2])\
                   .then_inc(k.emptied_a.sem, 1)
                for n in range(2):
                    act.wait_ge(k.v_chain.sem, chain.tally.base + b * per_block + 2 * n + 2)
                    act.activation(act_qk[:, n, :], mixed[:, n, :], ACT.Gelu).then_inc(qk_act.sem, 1)
                    act.wait_ge(qk_act.sem, 2 * b + n + 1)
                    split.scalar_1(act, b, n, act_qk[:, n, :], (0.25, 1.0)[n])
                    split.scalar_2(act, b, n)
                for j in range(J1):
                    g = FFN + 2 * j
                    if j >= 2:
                        grp.wait_emptied(act, b, g - 3)
                    grp.wait_filled(act, b, g)
                    act.activation(sg[:, j % 2, :], k.ps[:, grp.bank(g), :], ACT.Silu, scale=s_hid[:, 0, j:j + 1])\
                       .then_inc(k.emptied_a.sem, 1)
                if more:
                    norm.scalar(act, b + 1)

            norm.scalar(act, 0)
            each_block(act, body)

        @block.vector
        def _(dve):
            split.prime(dve)
            def body(b, more):
                chain.start(dve, b * per_block)
                dve.wait_ge(wave_in.sem, 16 * (b + 1))
                for n, (g, r) in enumerate(((Q, RQ), (K_, RK))):
                    grp.wait_emptied(dve, b, g)
                    chain.mark(dve.tensor_tensor(mixed[:, n, :], plain[:, n, :], wave[:, 0, :], ALU.mult))
                    grp.wait_filled(dve, b, r)
                    dve.tensor_tensor(turned_[:, n, :], k.ps[:, grp.bank(r), :], wave[:, 1, :], ALU.mult)\
                       .then_inc(k.emptied_v.sem, 1)
                    grp.wait_emptied(dve, b, r)
                    dve.wait_ge(k.v_chain.sem, chain.at + chain.n)
                    chain.link(dve.tensor_tensor(mixed[:, n, :], mixed[:, n, :], turned_[:, n, :], ALU.add))
                for n in range(2):
                    dve.wait_ge(qk_act.sem, 2 * b + n + 1)
                    split.vector_1(dve, b, n, act_qk[:, n, :], (0.25, 1.0)[n])
                    split.vector_2(dve, b, n)
                grp.wait_filled(dve, b, V)
                dve.tensor_tensor(v_all[:, bass.ds(b * TPB, TPB), :],
                                  k.ps[:, grp.bank(V), :].rearrange("p (t n) -> p t n", t=TPB),
                                  bv[:, :].unsqueeze(1).to_broadcast([P, TPB, P]), ALU.add)\
                   .then_inc(k.emptied_v.sem, 1)
                assert chain.n == per_block
                if isinstance(b, int) and b == 0:
                    for n in range(3):
                        dve.wait_ge(raw_in[n].sem, 16)
                        dve.tensor_scalar(third(n), third(n).bitcast(I32), -128.0, None, ALU.add)\
                           .then_inc(widened.sem, 1)
                for j in range(J1):
                    g = FFN + 2 * j
                    grp.wait_emptied(dve, b, g)
                    grp.wait_filled(dve, b, g + 1)
                    dve.scalar_tensor_tensor(h[:, j, :], k.ps[:, grp.bank(g + 1), :], s_hid[:, 1, j:j + 1],
                                             sg[:, j % 2, :], ALU.mult, ALU.mult).then_inc(k.emptied_v.sem, 1)
                if more:
                    norm.vector(dve, b + 1)
                for oc in range(C):
                    grp.wait_filled(dve, b, DOWN + oc)
                    xs = k.x[:, oc, bass.ds(b * TB, TB)]
                    dve.scalar_tensor_tensor(xs, k.ps[:, grp.bank(DOWN + oc), :], s_down[:, oc:oc + 1], xs,
                                             ALU.mult, ALU.add).then_inc(k.emptied_v.sem, 1)

            norm.vector(dve, 0)
            each_block(dve, body, first_apart=True)

    grp.close()
    split.close()
    k.v_chain.base += NB * per_block


def layer2(core):
    nc, k, io = core.nc, core, core.io
    with ExitStack() as ctx:
        def sb(name, shape, dt=F32):
            return ctx.enter_context(nc.sbuf_tensor(name, shape, dt))

        rows = sb("rows", [P, TT, D])
        slot_in, slot_out = sb("slot_in", [P, TOPK, TT], I32), sb("slot_out", [P, TOPK, TT], I32)
        share = sb("share", [P, TOPK, TT])
        sent = Tally(nc, ctx, "sent")
        with ExitStack() as inner:
            layer2_blocks(core, inner, Route(core, inner, slot_in, slot_out, share), rows, sent)
        with ExitStack() as inner:
            experts(core, inner, slot_out, share, sent)


class Route:

    TAKEN, NONE = -7.0, -5.0

    def __init__(self, core, ctx, slot_in, slot_out, share):
        self.core = core
        self.slot_in, self.slot_out, self.share = slot_in, slot_out, share
        nc, E, PAD = core.nc, EXPERTS, 8

        def sb(name, shape, dt=F32):
            return ctx.enter_context(nc.sbuf_tensor(name, shape, dt))

        self.logits = sb("logits", [P, TPB, E])
        self.row = sb("row", [P, 4, TPB])
        self.expd = sb("expd", [P, TPB, E])
        self.score = sb("score", [P, TPB, E + PAD])
        self.left = sb("left", [P, TPB, E + PAD])
        self.best, self.taken = sb("best", [P, TPB, 8]), sb("taken", [P, TPB, 8])
        self.picked = sb("picked_e", [P, TPB, E])
        self.before = sb("before", [P, TPB + 1, E])
        self.place = sb("place", [P, TPB, E])
        self.which, self.one, self.got = sb("which", [P, 1, E]), sb("one", [P, TPB, E]), sb("got", [P, 4, TPB])
        self.which_i = sb("which_i", [P, E], I32)
        self.earlier, self.ones = sb("earlier", [P, P]), sb("ones_p", [P, P])
        self.best_e = sb("best_e", [P, TPB, 8], U32)
        self.best_f = sb("best_f", [P, TPB, 8])
        self.hop = sb("hop2", [P, 5])
        self.made, self.shifted, self.expd_done, self.chosen, self.placed, self.copied, self.routed = (
            Tally(nc, ctx, "route_" + n) for n in ("made", "shifted", "exp", "chosen", "placed", "copied", "routed"))
        self.chain = Chain(core.v_chain)
        self.PRE, self.PER_CHOOSE, self.PER_SLOTS = 4, 9 + 4 * TPB, 1 + 13 * TOPK

    def close(self):
        self.core.v_chain.base += self.PRE + NB * (self.PER_CHOOSE + self.PER_SLOTS)

    def masks(self, pool):
        pool.memset(self.earlier[:, :], 1.0).then_inc(self.made.sem, 1)
        pool.memset(self.ones[:, :], 1.0).then_inc(self.made.sem, 1)
        pool.iota(self.which_i[:, :], pattern=[[1, EXPERTS]], base=0, channel_multiplier=0).then_inc(self.made.sem, 1)
        pool.wait_ge(self.made.sem, 3)
        pool.affine_select(out=self.earlier[:, :], in_=self.earlier[:, :], compare_op=ALU.is_gt, fill=0.0,
                           base=0, pattern=[[1, P]], channel_multiplier=-1).then_inc(self.made.sem, 1)

    def scalar(self, act, b):
        act.wait_ge(self.shifted.sem, b + 1)
        act.activation(self.expd[:, :, :], self.logits[:, :, :], ACT.Exp).then_inc(self.expd_done.sem, 1)

    def tensor(self, pe, b):
        pe.wait_ge(self.chosen.sem, b + 1)
        out = self.core.ps[:, 0, 0:TPB * EXPERTS].rearrange("p (t e) -> p t e", e=EXPERTS)
        pe.matmul(out, self.earlier[:, :], self.picked[:, :, :], start=True, stop=False)
        pe.matmul(out, self.ones[:, :], self.before[:, 0:TPB, :], start=False, stop=True).then_inc(self.placed.sem, 1)

    def wide(self, v, n=EXPERTS):
        return v.unsqueeze(2).to_broadcast([P, TPB, n])

    def prepare(self, dve):
        chain = self.chain
        chain.start(dve)
        chain.mark(dve.memset(self.score[:, :, EXPERTS:], self.NONE))
        chain.mark(dve.memset(self.taken[:, :, :], self.NONE))
        chain.mark(dve.memset(self.before[:, TPB, :], 0.0))
        dve.wait_ge(self.made.sem, 3)
        chain.link(dve.tensor_copy(self.which[:, 0, :], self.which_i[:, :]))
        assert chain.n == self.PRE

    def choose(self, dve, b):
        chain, E, wide, row, best, before = self.chain, EXPERTS, self.wide, self.row, self.best, self.before
        chain.start(dve, self.PRE + b * (self.PER_CHOOSE + self.PER_SLOTS))
        chain.link(dve.tensor_reduce(row[:, 0, :], self.logits[:, :, :], X_AXIS, ALU.max))
        chain.mark(dve.tensor_copy(before[:, 0, :], before[:, TPB, :]))
        dve.tensor_tensor(self.logits[:, :, :], self.logits[:, :, :], wide(row[:, 0, :]), ALU.subtract)\
           .then_inc(self.shifted.sem, 1)
        dve.wait_ge(self.expd_done.sem, b + 1)
        chain.link(dve.tensor_reduce(row[:, 1, :], self.expd[:, :, :], X_AXIS, ALU.add))
        chain.link(dve.reciprocal(row[:, 2, :], row[:, 1, :]))
        chain.link(dve.tensor_tensor(self.score[:, :, 0:E], self.expd[:, :, :], wide(row[:, 2, :]), ALU.mult))
        dve.memset(self.hop[:, 0:1], 0.0)
        for t in range(TPB):
            chain.mark(dve.max(best[:, t, :], self.score[:, t, 0:E]))
        dve.wait_ge(chain.tally.sem, chain.at + chain.n)
        chain.link(dve.tensor_copy(self.taken[:, :, 0:TOPK], best[:, :, 0:TOPK]))
        dve.memset(self.hop[:, 1:2], 0.0)
        for t in range(TPB):
            chain.mark(dve.match_replace(self.left[:, t, :], self.taken[:, t, :], self.score[:, t, :], self.TAKEN))
            chain.mark(dve.max_index(self.best_e[:, t, :], best[:, t, :], self.score[:, t, 0:E]))
        dve.wait_ge(chain.tally.sem, chain.at + chain.n)
        chain.link(dve.tensor_scalar(self.picked[:, :, :], self.left[:, :, 0:E], self.NONE - 1.0, None, ALU.is_lt))
        for t in range(1, TPB + 1):
            chain.link(dve.tensor_tensor(before[:, t, :], before[:, t - 1, :], self.picked[:, t - 1, :], ALU.add))
        dve.tensor_copy(self.best_f[:, :, :], self.best_e[:, :, :]).then_inc(self.chosen.sem, 1)
        chain.link(dve.tensor_reduce(row[:, 3, :], best[:, :, 0:TOPK], X_AXIS, ALU.add))
        chain.link(dve.reciprocal(row[:, 3, :], row[:, 3, :]))
        assert chain.n == self.PER_CHOOSE, chain.n

    def slots(self, dve, b):
        chain, wide, got, one, best = self.chain, self.wide, self.got, self.one, self.best
        tiles = bass.ds(b * TPB, TPB)
        slot_in, slot_out, share = self.slot_in, self.slot_out, self.share
        chain.start(dve, self.PRE + b * (self.PER_CHOOSE + self.PER_SLOTS) + self.PER_CHOOSE)
        dve.wait_ge(self.placed.sem, b + 1)
        chain.link(dve.tensor_copy(self.place[:, :, :], self.core.ps[:, 0, 0:TPB * EXPERTS]
                                   .rearrange("p (t e) -> p t e", e=EXPERTS)))
        dve.memset(self.hop[:, 2:3], 0.0).then_inc(self.copied.sem, 1)
        dve.wait_ge(self.chosen.sem, b + 1)
        for c in range(TOPK):
            e = self.best_f[:, :, c]
            chain.link(dve.tensor_tensor(one[:, :, :], wide(e), self.which[:, :, :].to_broadcast([P, TPB, EXPERTS]),
                                         ALU.is_equal))
            chain.link(dve.tensor_tensor(one[:, :, :], one[:, :, :], self.place[:, :, :], ALU.mult))
            chain.link(dve.tensor_reduce(got[:, 0, :], one[:, :, :], X_AXIS, ALU.add))
            chain.mark(dve.tensor_scalar(got[:, 1, :], got[:, 0, :], float(CAP), None, ALU.is_lt))
            chain.mark(dve.tensor_scalar(got[:, 2, :], got[:, 0, :], float(CAP - 1), None, ALU.min))
            chain.link(dve.tensor_scalar(got[:, 3, :], e, float(CAP), None, ALU.mult))
            chain.link(dve.tensor_tensor(got[:, 2, :], got[:, 2, :], got[:, 3, :], ALU.add))
            chain.mark(dve.tensor_copy(slot_out[:, c:c + 1, tiles], got[:, 2:3, :]))
            chain.link(dve.tensor_scalar(got[:, 3, :], got[:, 1, :], -float(2 * SLOTS), float(2 * SLOTS),
                                         ALU.mult, ALU.add))
            chain.link(dve.tensor_tensor(got[:, 3, :], got[:, 3, :], got[:, 2, :], ALU.add))
            chain.mark(dve.tensor_copy(slot_in[:, c:c + 1, tiles], got[:, 3:4, :]))
            chain.link(dve.tensor_tensor(share[:, c:c + 1, tiles], best[:, :, c].unsqueeze(1), self.row[:, 3:4, :],
                                         ALU.mult))
            chain.link(dve.tensor_tensor(share[:, c:c + 1, tiles], share[:, c:c + 1, tiles], got[:, 1:2, :],
                                         ALU.mult))
        dve.memset(self.hop[:, 3:4], 0.0).then_inc(self.routed.sem, 1)
        assert chain.n == self.PER_SLOTS, chain.n


def layer2_blocks(core, ctx, route, rows, sent):
    nc, k, io = core.nc, core, core.io

    def sb(name, shape, dt=F32):
        return ctx.enter_context(nc.sbuf_tensor(name, shape, dt))

    HS = JS * P
    wr, br = sb("wr", [P, C, EXPERTS]), sb("br", [P, EXPERTS])
    wv, wo = sb("wv2", [P, C, D]), sb("wo2", [P, C, D])
    s_gate, s_up, s_down = sb("s_gate", [P, C, HS]), sb("s_up", [P, C, HS]), sb("s_down2", [P, JS, D])
    norm = Norm(core, ctx, 2)
    value = sb("value2", [P, C, TB])
    h, sg = sb("h2", [P, JS, TB]), sb("sg2", [P, 2, TB])

    grp = Groups(core, "v" + "a" * TPB + "a" * C + "av" * JS + "v" * C, ring=6)
    R, ROWS, V = 0, 1, 1 + TPB
    PLACED_AFTER = 1
    FFN = V + C
    OUT = FFN + 2 * JS
    with nc.Block() as block:
        @block.sync
        def _(sp):
            load(sp, core, [(wr[:, :, :], io["L2_wr"]), (br[:, :], io["L2_br"].partition_broadcast(P)),
                            (wv[:, :, :], io["L2_wv"])], first=True)
            load(sp, core, [(s_gate[:, :, :], io["L2_sg"]), (s_up[:, :, :], io["L2_su"]),
                            (wo[:, :, :], io["L2_wo"]), (s_down[:, :, :], io["L2_sd"])])

        @block.tensor
        def _(pe):
            pe.wait_ge(route.made.sem, 4)

            def body(b, more):
                grp.wait_block(pe, b)
                norm.wait_ready(pe, b)
                for t in range(TPB):
                    m = project(pe, k.ps[:, grp.bank(R), t * EXPERTS:(t + 1) * EXPERTS],
                                lambda c: norm.xn[:, c, t * P:(t + 1) * P], lambda c: wr[:, c, :])
                m.then_inc(k.filled.sem, 1)
                for t in range(TPB):
                    for c in range(C):
                        m = pe.transpose(k.ps[:, grp.bank(ROWS + t), c * P:(c + 1) * P],
                                         norm.xn[:, c, t * P:(t + 1) * P], k.ident[:, :])
                    m.then_inc(k.filled.sem, 1)
                for oc in range(C):
                    grp.wait_free(pe, b, V + oc)
                    project(pe, k.ps[:, grp.bank(V + oc), :], lambda c: wv[:, c, oc * P:(oc + 1) * P],
                            lambda c: norm.xn[:, c, :]).then_inc(k.filled.sem, 1)
                pe.wait_ge(k.loaded.sem, k.loaded.base)
                for j in range(JS):
                    for u, w in enumerate((s_gate, s_up)):
                        g = FFN + 2 * j + u
                        grp.wait_free(pe, b, g)
                        project(pe, k.ps[:, grp.bank(g), :], lambda c: w[:, c, j * P:(j + 1) * P],
                                lambda c: norm.xn[:, c, :]).then_inc(k.filled.sem, 1)
                    if j == PLACED_AFTER:
                        route.tensor(pe, b)
                if more:
                    pe.wait_ge(route.copied.sem, b + 1)
                    norm.tensor_mean(pe, b + 1)
                grp.wait_emptied(pe, b, OUT - 1)
                for oc in range(C):
                    if more and oc == 1:
                        norm.tensor_var(pe, b + 1)
                    grp.wait_free(pe, b, OUT + oc)
                    for j in range(C + JS):
                        w, y = (wo, value) if j < C else (s_down, h)
                        c = j if j < C else j - C
                        m = pe.matmul(k.ps[:, grp.bank(OUT + oc), :], w[:, c, oc * P:(oc + 1) * P], y[:, c, :],
                                      start=j == 0, stop=j == C + JS - 1)
                    m.then_inc(k.filled.sem, 1)

            norm.tensor_mean(pe, 0)
            norm.tensor_var(pe, 0)
            pe.wait_ge(k.loaded_first.sem, k.loaded_first.base)
            each_block(pe, body)

        @block.scalar
        def _(act):
            def body(b, more):
                for t in range(TPB):
                    grp.wait_filled(act, b, ROWS + t)
                    act.activation(rows[:, bass.ds(b * TPB + t, 1), :], k.ps[:, grp.bank(ROWS + t), :].unsqueeze(1), ACT.Copy)\
                       .then_inc(k.emptied_a.sem, 1)
                for oc in range(C):
                    grp.wait_filled(act, b, V + oc)
                    act.activation(value[:, oc, :], k.ps[:, grp.bank(V + oc), :], ACT.Copy)\
                       .then_inc(k.emptied_a.sem, 1)
                    if oc == 1:
                        route.scalar(act, b)
                for j in range(JS):
                    g = FFN + 2 * j
                    if j >= 2:
                        grp.wait_emptied(act, b, g - 3)
                    grp.wait_filled(act, b, g)
                    act.activation(sg[:, j % 2, :], k.ps[:, grp.bank(g), :], ACT.Silu).then_inc(k.emptied_a.sem, 1)
                if more:
                    norm.scalar(act, b + 1)

            norm.scalar(act, 0)
            each_block(act, body)

        @block.vector
        def _(dve):
            dve.wait_ge(k.loaded_first.sem, k.loaded_first.base)
            route.prepare(dve)

            def body(b, more):
                grp.wait_filled(dve, b, R)
                dve.tensor_tensor(route.logits[:, :, :],
                                  k.ps[:, grp.bank(R), 0:TPB * EXPERTS].rearrange("p (t e) -> p t e", t=TPB),
                                  br[:, :].unsqueeze(1).to_broadcast([P, TPB, EXPERTS]), ALU.add)\
                   .then_inc(k.emptied_v.sem, 1)
                grp.wait_emptied(dve, b, R)
                route.choose(dve, b)
                for j in range(JS):
                    g = FFN + 2 * j
                    grp.wait_emptied(dve, b, g)
                    grp.wait_filled(dve, b, g + 1)
                    dve.tensor_tensor(h[:, j, :], k.ps[:, grp.bank(g + 1), :], sg[:, j % 2, :], ALU.mult)\
                       .then_inc(k.emptied_v.sem, 1)
                    if j == PLACED_AFTER:
                        route.slots(dve, b)
                if more:
                    norm.vector(dve, b + 1)
                for oc in range(C):
                    grp.wait_filled(dve, b, OUT + oc)
                    xs = k.x[:, oc, bass.ds(b * TB, TB)]
                    dve.tensor_tensor(xs, xs, k.ps[:, grp.bank(OUT + oc), :], ALU.add).then_inc(k.emptied_v.sem, 1)

            norm.vector(dve, 0)
            each_block(dve, body)

        @block.gpsimd
        def _(pool):
            route.masks(pool)
            for t in range(TT):
                if t % TPB == 0:
                    pool.wait_ge(route.routed.sem, t // TPB + 1)
                    grp.wait_emptied(pool, t // TPB, ROWS + TPB - 1)
                for c in range(TOPK):
                    pool.indirect_dma_start(
                        out=io["slots_x"], out_offset=bass.IndirectOffsetOnAxis(ap=route.slot_in[:, c, t:t + 1], axis=0),
                        in_=rows[:, t, :], in_offset=None, bounds_check=SLOTS - 1, oob_is_err=False)\
                        .then_inc(sent.sem, 16)
            pool.wait_ge(sent.sem, 16 * TT * TOPK)
    grp.close()
    route.close()


def experts(core, ctx, slot_out, share, sent):
    nc, k, io = core.nc, core, core.io

    def sb(name, shape, dt=F32):
        return ctx.enter_context(nc.sbuf_tensor(name, shape, dt))

    AHEAD = 4
    w = sb("w_exp", [P, AHEAD, 3 * D])
    xe, xeT = sb("xe", [P, AHEAD, D]), sb("xeT", [P, 2, C, P])
    ge, he, ye = sb("ge", [P, 2, P]), sb("he", [P, 2, P]), sb("ye", [P, 2, D])
    w_in = [Tally(nc, ctx, f"w_in{n}") for n in range(AHEAD)]
    y_out = [Tally(nc, ctx, f"y_out{n}", 1) for n in range(2)]
    xT_filled, xT_copied = Tally(nc, ctx, "xT_filled"), Tally(nc, ctx, "xT_copied")
    gu_filled, g_done, h_done = Tally(nc, ctx, "gu_filled"), Tally(nc, ctx, "g_done"), Tally(nc, ctx, "h_done")
    y_filled, y_copied = Tally(nc, ctx, "y_filled", AHEAD), Tally(nc, ctx, "y_copied", 2)
    note = sb("note2", [1, 8])

    def walk(eng, expert):
        with eng.Fori(0, EXPERTS // AHEAD - 1) as it:
            for u in range(AHEAD):
                expert(AHEAD * it + u, u, it, True)
        for u in range(AHEAD):
            expert(EXPERTS - AHEAD + u, u, EXPERTS // AHEAD - 1, u < AHEAD - 1)

    with nc.Block() as block:
        @block.gpsimd
        def _(pool):
            for n, tl in enumerate((*y_out, y_filled, y_copied)):
                pool.memset(note[:, n:n + 1], 0.0).then_inc(tl.sem, tl.base)

        @block.sync
        def _(sp):
            sp.wait_ge(y_filled.sem, AHEAD)
            sp.wait_ge(sent.sem, 16 * TT * TOPK)

            def expert(e, u, it, more):
                sp.wait_ge(y_filled.sem, e + 1)
                sp.dma_start(w[:, u, :], io["L2_we"][bass.ds(e, 1), :, :].rearrange("a p n -> (a p) n"))\
                  .then_inc(w_in[u].sem, 16)
                sp.dma_start(xe[:, u, :], io["slots_x"][bass.ds(e * CAP, CAP), :]).then_inc(w_in[u].sem, 16)

            walk(sp, expert)

        @block.tensor
        def _(pe):
            def turn(e, u, it):
                pe.wait_ge(w_in[u].sem, 32 * it + 32)
                for c in range(C):
                    m = pe.transpose(k.ps[:, u % 2, c * P:(c + 1) * P], xe[:, u, c * P:(c + 1) * P], k.ident[:, :])
                m.then_inc(xT_filled.sem, 1)

            def expert(e, u, it, more):
                p = u % 2
                pe.wait_ge(xT_copied.sem, e + 1)
                for n in range(2):
                    m = project(pe, k.ps[:, 2 + 2 * n + p, 0:P],
                                lambda c: w[:, u, n * D + c * P:n * D + (c + 1) * P], lambda c: xeT[:, p, c, :])
                    m.then_inc(gu_filled.sem, 1)
                if more:
                    turn(e + 1, (u + 1) % AHEAD, it + (u + 1) // AHEAD)
                pe.wait_ge(y_copied.sem, e + 1)
                pe.wait_ge(h_done.sem, e + 1)
                pe.matmul(k.ps[:, 6 + p, :], he[:, p, :], w[:, u, 2 * D:3 * D], start=True, stop=True)\
                  .then_inc(y_filled.sem, 1)

            turn(0, 0, 0)
            walk(pe, expert)

        @block.scalar
        def _(act):
            def expert(e, u, it, more):
                p = u % 2
                act.wait_ge(gu_filled.sem, 2 * e + 1)
                act.activation(ge[:, p, :], k.ps[:, 2 + p, 0:P], ACT.Silu).then_inc(g_done.sem, 1)
                act.wait_ge(y_filled.sem, e + (1 + AHEAD))
                act.wait_ge(y_out[p].sem, it * (16 * AHEAD // 2) + (16 * (u // 2) + 1))
                act.activation(ye[:, p, :], k.ps[:, 6 + p, :], ACT.Copy).then_inc(y_copied.sem, 1)
                act.wait_ge(y_copied.sem, e + 3)
                act.dma_start(io["slots_y"][bass.ds(e * CAP, CAP), :], ye[:, p, :]).then_inc(y_out[p].sem, 16)

            walk(act, expert)
            for p in range(2):
                act.wait_ge(y_out[p].sem, 16 * (EXPERTS // 2) + 1)

        @block.vector
        def _(dve):
            def turned(e, u):
                dve.wait_ge(xT_filled.sem, e + 1)
                dve.tensor_copy(xeT[:, u % 2, :, :], k.ps[:, u % 2, :].rearrange("p (c n) -> p c n", c=C))\
                   .then_inc(xT_copied.sem, 1)

            def expert(e, u, it, more):
                p = u % 2
                dve.wait_ge(gu_filled.sem, 2 * e + 2)
                dve.wait_ge(g_done.sem, e + 1)
                dve.tensor_tensor(he[:, p, :], k.ps[:, 4 + p, 0:P], ge[:, p, :], ALU.mult).then_inc(h_done.sem, 1)
                if more:
                    turned(e + 1, u + 1)

            turned(0, 0)
            walk(dve, expert)

    res, acc = sb("res", [P, 2, TOPK, D]), sb("acc2", [P, 2, D])
    fetched = [Tally(nc, ctx, f"fetched{n}") for n in range(2)]
    summed, acc_turned, added = Tally(nc, ctx, "summed"), Tally(nc, ctx, "acc_turned"), Tally(nc, ctx, "added")
    with nc.Block() as block:
        def add_back(dve, t):
            dve.wait_ge(acc_turned.sem, t + 1)
            xs = k.x[:, :, t * P:(t + 1) * P]
            dve.tensor_tensor(xs, xs, k.ps[:, t % 2, :].rearrange("p (c n) -> p c n", c=C), ALU.add)\
               .then_inc(added.sem, 1)

        @block.gpsimd
        def _(pool):
            for t in range(TT):
                if t >= 2:
                    pool.wait_ge(summed.sem, 4 * (t - 1))
                for c in range(TOPK):
                    pool.indirect_dma_start(
                        out=res[:, t % 2, c, :], out_offset=None, in_=io["slots_y"],
                        in_offset=bass.IndirectOffsetOnAxis(ap=slot_out[:, c, t:t + 1], axis=0),
                        bounds_check=SLOTS - 1, oob_is_err=False).then_inc(fetched[t % 2].sem, 16)

        @block.vector
        def _(dve):
            for t in range(TT):
                dve.wait_ge(fetched[t % 2].sem, 16 * TOPK * (t // 2 + 1))
                if t >= 2:
                    dve.wait_ge(acc_turned.sem, t - 1)
                a = acc[:, t % 2, :]
                dve.tensor_scalar(a, res[:, t % 2, 0, :], share[:, 0, t:t + 1], None, ALU.mult).then_inc(summed.sem, 1)
                for c in range(1, TOPK):
                    dve.wait_ge(summed.sem, 4 * t + c)
                    dve.scalar_tensor_tensor(a, res[:, t % 2, c, :], share[:, c, t:t + 1], a, ALU.mult, ALU.add)\
                       .then_inc(summed.sem, 1)
                if t >= 1:
                    add_back(dve, t - 1)
            add_back(dve, TT - 1)

        @block.tensor
        def _(pe):
            for t in range(TT):
                pe.wait_ge(summed.sem, 4 * (t + 1))
                if t >= 2:
                    pe.wait_ge(added.sem, t - 1)
                for c in range(C):
                    m = pe.transpose(k.ps[:, t % 2, c * P:(c + 1) * P], acc[:, t % 2, c * P:(c + 1) * P],
                                     k.ident[:, :])
                m.then_inc(acc_turned.sem, 1)


def layer3(core):
    nc, k, io = core.nc, core, core.io
    with ExitStack() as ctx:
        def sb(name, shape, dt=F32):
            return ctx.enter_context(nc.sbuf_tensor(name, shape, dt))

        v_all = sb("v3_all", [P, TT, D])
        v_one = sb("v3_one", [P, TT, 32])
        with ExitStack() as inner:
            layer3_blocks(core, inner, v_all, v_one)
        attention(core, "3", 16, 32, io["q3_parts"], io["k3_parts"], v_all, io["o3"], first=5)
        w_out, b_out = sb("w_out3", [P, C, D]), sb("b_out3", [P, C])
        attention(core, "4", 16, 32, io["q4_parts"], io["k4_parts"], v_one, io["o4"], shared=True, first=5,
                  ahead=[(w_out[:, :, :], io["L3_wo"]), (b_out[:, :], io["L3_bo"])])
        project_out(core, ctx, "3", io["o3"], io["o4"], w_out, b_out, io["out"])


def layer3_blocks(core, ctx, v_all, v_one):
    nc, k, io = core.nc, core, core.io

    def sb(name, shape, dt=F32):
        return ctx.enter_context(nc.sbuf_tensor(name, shape, dt))

    HEADS, DH = 16, 32
    SCALE = float(1.0 / np.sqrt(np.float32(DH)))
    TAKEN, NONE = -7.0, -5.0
    wa, ba = sb("wa3", [P, 2, C, D]), sb("ba3", [P, 2, C])
    wv, bv = sb("wv3", [P, C, D]), sb("bv3", [P, D])
    wf, wg = sb("wf3", [P, 3, C, D]), sb("wg3", [P, C, HEADS])
    rot = sb("rot3", [P, P])
    norm = Norm(core, ctx, 3, buffers=2)
    split = Split(core, ctx, "3", 13)
    plain = sb("plain3", [P, 4, TB])
    turned_, mixed = sb("turned3", [P, TB]), sb("mixed3", [P, 2, TB])
    fq = sb("fq", [P, 2, TB])
    wave = sb("wave3", [P, 2, TB])
    gate, gexp = sb("gate3", [P, TPB, HEADS]), sb("gexp3", [P, TPB, HEADS])
    gsum, ginv = sb("gsum3", [P, TPB]), sb("ginv3", [P, TPB])
    prob, left = sb("gprob3", [P, TPB, HEADS + 8]), sb("gleft3", [P, TPB, HEADS + 8])
    best, taken = sb("gbest3", [P, TPB, 8]), sb("gtaken3", [P, TPB, 8])
    pick = sb("pick3", [P, 2, TPB, HEADS])
    prod = sb("prod3", [P, D])
    hop = sb("hop3", [P, 2])
    k_one, kT = sb("k_one3", [P, TPB, DH]), sb("kT3", [DH, TB])
    wave_in, mixed_ready, g_exp = Tally(nc, ctx, "wave_in3"), Tally(nc, ctx, "mixed_ready3"), Tally(nc, ctx, "g_exp3")
    k_ready = Tally(nc, ctx, "k_ready3")

    order = ["p0", "p1", "p2", "p3", "r0", "r1", "p4", "p5", "r2", "r3", "p6", "p7", "r4", "r5", "gate", "r6", "r7"]
    order += [f"{n}{t}" for t in range(TPB) for n in "kv"]
    order += [f"f{n}" for n in range(C)] + ["kT"] + [f"V{t}" for t in range(TPB)]
    at = {n: g for g, n in enumerate(order)}
    grp = Groups(core, "".join("a" if n[0] in "pf" or n == "kT" else "v" for n in order), ring=6)
    chain = Chain(k.v_chain)
    per_block = 31

    with nc.Block() as block:
        def choose(dve, b):
            g = at["gate"]
            grp.wait_filled(dve, b, g)
            logits = k.ps[:, grp.bank(g), 0:TPB * HEADS].rearrange("p (t h) -> p t h", t=TPB)
            chain.link(dve.tensor_reduce(gsum[:, :], logits, X_AXIS, ALU.max))
            dve.tensor_tensor(gate[:, :, :], logits, gsum[:, :].unsqueeze(2).to_broadcast([P, TPB, HEADS]),
                              ALU.subtract).then_inc(k.emptied_v.sem, 1)
            dve.wait_ge(g_exp.sem, b + 1)
            chain.link(dve.tensor_reduce(gsum[:, :], gexp[:, :, :], X_AXIS, ALU.add))
            chain.link(dve.reciprocal(ginv[:, :], gsum[:, :]))
            chain.link(dve.tensor_tensor(prob[:, :, 0:HEADS], gexp[:, :, :],
                                         ginv[:, :].unsqueeze(2).to_broadcast([P, TPB, HEADS]), ALU.mult))
            dve.memset(hop[:, 0:1], 0.0)
            for t in range(TPB):
                chain.mark(dve.max(best[:, t, :], prob[:, t, 0:HEADS]))
            dve.wait_ge(k.v_chain.sem, chain.at + chain.n)
            chain.link(dve.tensor_copy(taken[:, :, 0:1], best[:, :, 0:1]))
            dve.memset(hop[:, 1:2], 0.0)
            for t in range(TPB):
                chain.mark(dve.match_replace(left[:, t, :], taken[:, t, :], prob[:, t, :], TAKEN))
            dve.wait_ge(k.v_chain.sem, chain.at + chain.n)
            chain.link(dve.tensor_scalar(pick[:, 0, :, :], left[:, :, 0:HEADS], NONE - 1.0, None, ALU.is_lt))
            chain.link(dve.tensor_tensor(pick[:, 1, :, :], pick[:, 0, :, :],
                                         best[:, :, 0:1].to_broadcast([P, TPB, HEADS]), ALU.mult))

        @block.sync
        def _(sp):
            load(sp, core, [(wa[:, :, :, :], io["L3_wqk"]), (ba[:, :, :], io["L3_bqk"]), (rot[:, :], io["L3_rot"]),
                            (wg[:, :, :], io["L3_wg"])], first=True)
            load(sp, core, [(wf[:, :, :, :], io["L3_wf"]), (wv[:, :, :], io["L3_wv"]),
                            (bv[:, :], io["L3_bv"].partition_broadcast(P))])
            with sp.Fori(0, NB) as b:
                for n in range(8):
                    dst = io["q3_parts"] if n % 2 == 0 else io["k3_parts"]
                    split.store(sp, b, n, dst[:, n // 2 * P:(n // 2 + 1) * P, :], after={0: 1, 1: None}.get(n, 0))
                for n in range(C):
                    split.store(sp, b, 8 + n, io["q4_parts"][:, n * P:(n + 1) * P, :])
                split.store(sp, b, 12, io["k4_parts"], DH)
            split.wait_stores(sp)

        @block.tensor
        def _(pe):
            def body(b, p, more):
                xn = norm.xn_of(p)
                grp.wait_block(pe, b)
                norm.wait_ready(pe, b)
                for g, name in enumerate(order):
                    if more and name == "V0":
                        norm.tensor_mean(pe, b + 1)
                    if more and name == "V3":
                        norm.tensor_var(pe, b + 1, 1 - p)
                    if name == "k0":
                        pe.wait_ge(k.loaded.sem, k.loaded.base)
                    grp.wait_free(pe, b, g)
                    out, n = k.ps[:, grp.bank(g), :], int(name[1]) if name[1].isdigit() else 0
                    tile = slice(n * P, (n + 1) * P)
                    if name[0] == "p":
                        oc = n // 2
                        m = project(pe, out, lambda c: wa[:, n % 2, c, oc * P:(oc + 1) * P],
                                    lambda c: xn[:, c, :])
                    elif name[0] == "r":
                        grp.wait_emptied(pe, b, at[f"p{n}"])
                        m = pe.matmul(out, rot[:, :], plain[:, n % 4, :], start=True, stop=True)
                    elif name == "gate":
                        for t in range(TPB):
                            m = project(pe, k.ps[:, grp.bank(g), t * HEADS:(t + 1) * HEADS],
                                        lambda c: xn[:, c, t * P:(t + 1) * P], lambda c: wg[:, c, :])
                    elif name == "kT":
                        pe.wait_ge(k_ready.sem, b + 1)
                        for t in range(TPB):
                            m = pe.transpose(k.ps[0:DH, grp.bank(g), t * P:(t + 1) * P], k_one[:, t, :], k.ident[:, :])
                    elif name[0] in "kv":
                        u = 1 + "kv".index(name[0])
                        m = project(pe, out, lambda c: xn[:, c, tile], lambda c: wf[:, u, c, :])
                    elif name[0] == "f":
                        m = project(pe, out, lambda c: wf[:, 0, c, tile], lambda c: xn[:, c, :])
                    else:
                        m = project(pe, out, lambda c: xn[:, c, tile], lambda c: wv[:, c, :])
                    m.then_inc(k.filled.sem, 1)

            norm.tensor_mean(pe, 0)
            norm.tensor_var(pe, 0)
            pe.wait_ge(k.loaded_first.sem, k.loaded_first.base)
            each_pair(pe, body)

        @block.scalar
        def _(act):
            def body(b, p, more):
                grp.wait_block(act, b)
                act.dma_start(wave[:, :, :], io["L3_wave"][:, :, bass.ds(b * TB, TB)]).then_inc(wave_in.sem, 16)

                def take(n):
                    g = at[f"p{n}"]
                    if n >= 4:
                        grp.wait_emptied(act, b, at[f"r{n - 4}"])
                    grp.wait_filled(act, b, g)
                    act.activation(plain[:, n % 4, :], k.ps[:, grp.bank(g), :], ACT.Identity,
                                   bias=ba[:, n % 2, n // 2:n // 2 + 1]).then_inc(k.emptied_a.sem, 1)

                def parts(n):
                    act.wait_ge(mixed_ready.sem, 8 * b + n + 1)
                    split.scalar_1(act, b, n, mixed[:, n % 2, :], SCALE if n % 2 == 0 else 1.0)
                    split.scalar_2(act, b, n)

                for n in range(4):
                    take(n)
                for n in range(8):
                    parts(n)
                    if n % 2 == 1 and n < 4:
                        take(n + 3)
                        take(n + 4)
                    if n == 5:
                        grp.wait_emptied(act, b, at["gate"])
                        act.activation(gexp[:, :, :], gate[:, :, :], ACT.Exp).then_inc(g_exp.sem, 1)
                for n in range(C):
                    g = at[f"f{n}"]
                    grp.wait_filled(act, b, g)
                    act.activation(fq[:, n % 2, :], k.ps[:, grp.bank(g), :], ACT.Copy).then_inc(k.emptied_a.sem, 1)
                    grp.wait_emptied(act, b, g)
                    split.scalar_1(act, b, 8 + n, fq[:, n % 2, :], SCALE)
                    split.scalar_2(act, b, 8 + n)
                grp.wait_filled(act, b, at["kT"])
                act.activation(kT[:, :], k.ps[0:DH, grp.bank(at["kT"]), :], ACT.Copy).then_inc(k.emptied_a.sem, 1)
                grp.wait_emptied(act, b, at["kT"])
                split.scalar_1(act, b, 12, kT[:, :], 1.0, DH)
                split.scalar_2(act, b, 12, DH)
                if more:
                    norm.scalar(act, b + 1, p=1 - p)

            norm.scalar(act, 0)
            each_pair(act, body)

        @block.vector
        def _(dve):
            split.prime(dve)
            chain.start(dve)
            chain.link(dve.memset(prob[:, :, HEADS:], NONE))
            chain.link(dve.memset(taken[:, :, :], NONE))

            def body(b, p, more):
                chain.start(dve, 2 + b * per_block)
                dve.wait_ge(wave_in.sem, 16 * (b + 1))
                for n in range(8):
                    grp.wait_emptied(dve, b, at[f"p{n}"])
                    chain.mark(dve.tensor_tensor(mixed[:, n % 2, :], plain[:, n % 4, :], wave[:, 0, :], ALU.mult))
                    g = at[f"r{n}"]
                    grp.wait_filled(dve, b, g)
                    dve.tensor_tensor(turned_[:, :], k.ps[:, grp.bank(g), :], wave[:, 1, :], ALU.mult)\
                       .then_inc(k.emptied_v.sem, 1)
                    grp.wait_emptied(dve, b, g)
                    dve.wait_ge(k.v_chain.sem, chain.at + chain.n)
                    dve.tensor_tensor(mixed[:, n % 2, :], mixed[:, n % 2, :], turned_[:, :], ALU.add)\
                       .then_inc(mixed_ready.sem, 1)
                    split.vector_1(dve, b, n, mixed[:, n % 2, :], SCALE if n % 2 == 0 else 1.0)
                    split.vector_2(dve, b, n)
                    if n == 5:
                        choose(dve, b)
                for t in range(TPB):
                    for u, name in enumerate("kv"):
                        g = at[f"{name}{t}"]
                        grp.wait_filled(dve, b, g)
                        dve.tensor_tensor(prod[:, :].rearrange("p (h d) -> p h d", d=DH),
                                          k.ps[:, grp.bank(g), :].rearrange("p (h d) -> p h d", d=DH),
                                          pick[:, u, t, :].unsqueeze(2).to_broadcast([P, HEADS, DH]), ALU.mult)\
                           .then_inc(k.emptied_v.sem, 1)
                        grp.wait_emptied(dve, b, g)
                        dst = k_one[:, t:t + 1, :] if u == 0 else v_one[:, bass.ds(b * TPB + t, 1), :]
                        chain.link(dve.tensor_reduce(dst.rearrange("p a d -> p (a d)"),
                                                     prod[:, :].rearrange("p (h d) -> p d h", d=DH), X_AXIS, ALU.add))
                dve.memset(gsum[:, 0:1], 0.0).then_inc(k_ready.sem, 1)
                for n in range(C):
                    split.vector_1(dve, b, 8 + n, fq[:, n % 2, :], SCALE)
                    split.vector_2(dve, b, 8 + n)
                split.vector_1(dve, b, 12, kT[:, :], 1.0, DH)
                split.vector_2(dve, b, 12, DH)
                if more:
                    norm.vector(dve, b + 1, p=1 - p)
                dve.wait_ge(k.loaded.sem, k.loaded.base)
                for t in range(TPB):
                    g = at[f"V{t}"]
                    grp.wait_filled(dve, b, g)
                    dve.tensor_tensor(v_all[:, bass.ds(b * TPB + t, 1), :].rearrange("p a d -> p (a d)"),
                                      k.ps[:, grp.bank(g), :], bv[:, :], ALU.add).then_inc(k.emptied_v.sem, 1)
                assert chain.n == per_block, chain.n

            norm.vector(dve, 0)
            each_pair(dve, body)
    grp.close()
    split.close()
    k.v_chain.base += 2 + NB * per_block


def program(nc, io, upto=4, start=0):
    def scratch(name, shape, dt=BF16):
        io[name] = nc.dram_tensor(name, shape, dt, kind="Internal").ap()

    scratch("q1_parts", (3, P, T))
    scratch("m_rows", (3, T))
    scratch("xn_saved", (D, T), F32)
    scratch("k1_parts", (3, P, T))
    scratch("slots_x", (SLOTS, D), F32)
    scratch("slots_y", (SLOTS, D), F32)
    for n in "34":
        scratch(f"q{n}_parts", (3, D, T))
        scratch(f"k{n}_parts", (3, D if n == "3" else 32, T))
        scratch("o" + n, (D, T), F32)
    scratch("o1", (P, T), F32)
    with ExitStack() as ctx:
        core = Core(nc, ctx, io)
        core.start = start
        setup(core)
        for n, layer in enumerate((layer0, layer1, layer2, layer3)):
            if start <= n < upto:
                layer(core)
        if upto < 4:
            dump(core)


def dump(core):
    nc, k = core.nc, core
    with nc.Block() as block:
        @block.sync
        def _(sp):
            sp.dma_start(k.io["out"].rearrange("(c p) t -> p c t", p=P), k.x[:, :, :]).then_inc(k.stored.sem, 16)
            sp.wait_ge(k.stored.sem, k.stored.base + 16)


def columns(v):
    return np.ascontiguousarray(v.reshape(-1, P).T)


def chunked(w):
    o, i = w.shape
    return np.ascontiguousarray(w.T.reshape(i // P, P, o).transpose(1, 0, 2))


def layout(inputs):
    a = {n: np.asarray(v) for n, v in inputs.items()}
    out = {"xT": np.ascontiguousarray(a["L0_attn_x"][0].T), "L0_ffn_lut": a["L0_ffn_lut"]}
    out["L0_w"] = np.stack([chunked(a["L0_attn_W" + n]) for n in "vkgq"], 1)
    out["L0_b"] = np.stack([columns(a["L0_attn_b" + n]) for n in "vkgq"], 1)
    idx = np.zeros((P, (LOOKUPS + 4) * LOOKUP), np.int32)
    for n, name in enumerate(("gate", "up")):
        w = idx[:, n * C * H1:(n + 1) * C * H1].reshape(P, C, H1)
        w[:, :, :H0] = chunked(a[f"L0_ffn_{name}_idx"])
    w = idx[:, 2 * C * H1:2 * C * H1 + J0 * D].reshape(P, J0, D)
    down = np.zeros((J0 * P, D), np.int32)
    down[:H0] = a["L0_ffn_down_idx"].T
    w[:, :, :] = down.reshape(J0, P, D).transpose(1, 0, 2)
    out["L0_idx"] = idx.reshape(P, LOOKUPS + 4, LOOKUP)
    out["L1_w"] = np.stack([chunked(a[f"L1_attn_{n}_w"]) for n in ("CQR", "CKV", "CKR")], 1)
    out["L1_b"] = np.stack([a[f"L1_attn_{n}_b"] for n in ("CQR", "CKV", "CKR")], 1)
    out["L1_cv_w"], out["L1_cv_b"] = np.ascontiguousarray(a["L1_attn_CV_w"].T), a["L1_attn_CV_b"]
    out["L1_out_w"], out["L1_out_b"] = np.ascontiguousarray(a["L1_attn_OUT_w"].T), columns(a["L1_attn_OUT_b"])
    out["L1_wq"] = np.concatenate([chunked(a["L1_ffn_wq_" + n]).reshape(P, 4, H1) for n in ("gate", "up", "down")], 1)
    out["L1_s_hid"] = np.stack([columns(a["L1_ffn_s_gate"]), columns(a["L1_ffn_s_up"])], 1)
    out["L1_s_down"] = columns(a["L1_ffn_s_down"])
    out["L2_wr"], out["L2_br"] = chunked(a["L2_ffn_Wr"].T), a["L2_ffn_router_bias"]
    out["L2_wv"], out["L2_wo"] = chunked(a["L2_attn_weight_qkv"][2 * D:]), chunked(a["L2_attn_weight_out"])
    for n, name in (("L2_sg", "L2_ffn_Sg"), ("L2_su", "L2_ffn_Su")):
        out[n] = chunked(a[name].transpose(0, 2, 1).reshape(JS * P, D))
    out["L2_sd"] = chunked(a["L2_ffn_Sd"].reshape(JS * P, D).T)
    we = [a["L2_ffn_" + n].reshape(EXPERTS, C, P, HX).transpose(0, 2, 1, 3).reshape(EXPERTS, P, D)
          for n in ("Wg", "Wu")]
    out["L2_we"] = np.concatenate(we + [a["L2_ffn_Wd"]], 2)
    out["L3_wqk"] = np.stack([chunked(a["L3_attn_W" + n]) for n in "qk"], 1)
    out["L3_bqk"] = np.stack([columns(a["L3_attn_b" + n]) for n in "qk"], 1)
    out["L3_wv"], out["L3_bv"] = chunked(a["L3_attn_Wv"]), a["L3_attn_bv"]
    out["L3_wo"], out["L3_bo"] = chunked(a["L3_attn_Wo"]), columns(a["L3_attn_bo"])
    out["L3_wg"] = chunked(a["L3_ffn_W_gate"])
    out["L3_wf"] = np.stack([chunked(a["L3_ffn_W_qkv"][n * D:(n + 1) * D]) for n in range(3)], 1)
    freq = (1.0 / 10000.0 ** (np.arange(16, dtype=np.float32) / 16)).astype(np.float32)
    angle = np.tile(np.repeat(np.outer(np.arange(T, dtype=np.float32), freq), 2, 1), (1, 4)).T
    out["L3_wave"] = np.ascontiguousarray(np.stack([np.cos(angle), np.sin(angle)], 1).astype(np.float32))
    rot = np.zeros((P, P), np.float32)
    for f in range(0, P, 2):
        rot[f + 1, f], rot[f, f + 1] = -1.0, 1.0
    out["L3_rot"] = rot
    freq = (1.0 / 10000.0 ** (np.arange(0, P, 2, dtype=np.float32) / P)).astype(np.float32)
    angle = np.tile(np.outer(np.arange(T, dtype=np.float32), freq), (1, 2)).T
    out["L1_wave"] = np.ascontiguousarray(np.stack([np.cos(angle), np.sin(angle)], 1).astype(np.float32))
    rot = np.zeros((P, P), np.float32)
    for f in range(P // 2):
        rot[f + P // 2, f], rot[f, f + P // 2] = -1.0, 1.0
    out["L1_rot"] = rot
    return out


def kernel(**inputs):
    import concourse.bacc as bacc
    from concourse.bass_utils import run_bass_kernel_spmd

    nc = bacc.Bacc("TRN2", target_bir_lowering=False, num_devices=1)
    arrays = {f"in_{n}": v for n, v in layout(inputs).items()}
    io = {n[3:]: nc.dram_tensor(n, v.shape, mybir.dt.from_np(v.dtype), kind="ExternalInput").ap()
          for n, v in arrays.items()}
    io["out"] = nc.dram_tensor("out", (D, T), F32, kind="ExternalOutput").ap()
    program(nc, io)
    result = run_bass_kernel_spmd(nc, [arrays], core_ids=[0]).results[0]["out"]
    return np.ascontiguousarray(result.T)[None]
```
